# Optimizing a Trainium2 kernel written in Bass

```python
import numpy as np
import jax
import jax.numpy as jnp

def _softmax(x, axis=-1):
    return jax.nn.softmax(x, axis=axis)

def _gelu(x):
    return jax.nn.gelu(x, approximate=True)

def _silu(x):
    return jax.nn.silu(x)

def _sigmoid(x):
    return jax.nn.sigmoid(x)

def _layernorm(x, axis=-1, eps=1e-05):
    m = jnp.mean(x, axis=axis, keepdims=True)
    v = jnp.var(x, axis=axis, keepdims=True)
    return (x - m) / jnp.sqrt(v + eps)

def _scatter_add(tgt, idx, src, axis=0):
    return tgt.at[idx].add(src)

def _segment_sum(src, seg, n):
    return jax.ops.segment_sum(src, seg, n)
kernel_name = 'mk_decoder_preln_d4_seqx_r8_d11313'

def setup_inputs(seed: int=0):
    np.random.seed(seed)
    _w = jnp.asarray

    def _rec_inputs():
        import jax
        import jax.numpy as jnp
        _rk = jax.random.key(seed)
        x = -0.0002928 + 1 * jax.random.normal(jax.random.fold_in(_rk, 1), (8, 128, 128), jnp.float32)
        _lenS = 128 - jax.random.randint(jax.random.fold_in(_rk, 7), (8,), 0, max(1, 128 // 4) + 1, jnp.int32)
        _lenS2 = 128 - jax.random.randint(jax.random.fold_in(_rk, 8), (8,), 0, max(1, 128 // 4) + 1, jnp.int32)
        _ctx_1024P = jax.random.normal(jax.random.fold_in(_rk, 11), (8, 16, 128), jnp.float32)
        _ctx_1024c = jax.random.dirichlet(jax.random.fold_in(_rk, 511), 0.3 * jnp.ones((16,), jnp.float32), (8, 128))
        _ctx_1024t = jnp.einsum('bsk,bkd->bsd', _ctx_1024c, _ctx_1024P)
        _ctx_1024t = _ctx_1024t * jax.lax.rsqrt(jnp.mean(jnp.square(_ctx_1024t)) + 1e-12) * 0.953939
        ctx_1024 = 4.13588e-05 + 0.999923 * (_ctx_1024t + 0.3 * jax.random.normal(jax.random.fold_in(_rk, 611), (8, 128, 128), jnp.float32))
        _validS = jnp.arange(128)[None, :] < _lenS[:, None]
        _validS2 = jnp.arange(128)[None, :] < _lenS2[:, None]
        _causal = jnp.tril(jnp.ones((128, 128), dtype=bool))
        mask_BxS2_if1 = jnp.where(jnp.ones((8, 128), dtype=bool), 1, 0).astype(jnp.int32)
        return (x, ctx_1024, mask_BxS2_if1)
    x, ctx_1024, mask_BxS2_if1 = _rec_inputs()

    def _L0_attn_setup():
        import jax, jax.numpy as jnp
        import numpy as np
        D_MODEL, D_STATE, D_INNER = (128, 16, 256)
        EPS = 1e-05

        def bit_linear(x, w, b):
            scale = jnp.maximum(jnp.mean(jnp.abs(w)), EPS)
            ws = w / scale
            wq = ws + jax.lax.stop_gradient(jnp.clip(jnp.round(ws), -1.0, 1.0) - ws)
            return jnp.einsum('bsd,od->bso', x, wq) * scale + b

        def causal_dwconv(x, w, b):
            xc = jnp.transpose(x, (0, 2, 1))
            y = jax.lax.conv_general_dilated(xc, w, window_strides=(1,), padding=[(3, 0)], feature_group_count=w.shape[0], dimension_numbers=('NCH', 'OIH', 'NCH'))
            y = y + b[None, :, None]
            return jnp.transpose(y, (0, 2, 1))
        key = jax.random.key(seed)
        ks = jax.random.split(key, 9)
        B, S = (4, 512)
        return {'x': jax.random.normal(ks[0], (B, S, D_MODEL), dtype=jnp.float32), 'w_in': jax.random.normal(ks[1], (2 * D_INNER, D_MODEL), dtype=jnp.float32) * 0.02, 'b_in': jax.random.normal(ks[2], (2 * D_INNER,), dtype=jnp.float32) * 0.02, 'w_conv': jax.random.normal(ks[3], (D_INNER, 1, 4), dtype=jnp.float32) * 0.2, 'b_conv': jax.random.normal(ks[4], (D_INNER,), dtype=jnp.float32) * 0.02, 'w_x': jax.random.normal(ks[5], (D_STATE + D_MODEL + D_INNER, D_INNER), dtype=jnp.float32) * 0.02, 'b_x': jax.random.normal(ks[6], (D_STATE + D_MODEL + D_INNER,), dtype=jnp.float32) * 0.02, 'w_out': jax.random.normal(ks[7], (D_MODEL, D_INNER), dtype=jnp.float32) * 0.02, 'b_out': jax.random.normal(ks[8], (D_MODEL,), dtype=jnp.float32) * 0.02}
    _L0_attn_all = _L0_attn_setup()
    _L0_attn_in = {k: v for k, v in _L0_attn_all.items() if k in ('w_in', 'b_in', 'w_conv', 'b_conv', 'w_x', 'b_x', 'w_out', 'b_out')}
    del _L0_attn_all

    def _L0_xattn_setup():
        import jax, jax.numpy as jnp
        import numpy as np
        DIM = 128
        NUM_HEADS = 16
        DIM_HEAD = 64
        INNER = NUM_HEADS * DIM_HEAD
        SCALE = DIM_HEAD ** (-0.5)

        def _layernorm(x, gamma, beta, eps=1e-05):
            mu = jnp.mean(x, axis=-1, keepdims=True)
            var = jnp.mean(jnp.square(x - mu), axis=-1, keepdims=True)
            return (x - mu) * jax.lax.rsqrt(var + eps) * gamma + beta
        key = jax.random.key(seed)
        ks = jax.random.split(key, 8)
        B, SQ, SK = (2, 256, 512)
        x = jax.random.normal(ks[0], (B, SQ, DIM), dtype=jnp.float32)
        context = jax.random.normal(ks[1], (B, SK, DIM), dtype=jnp.float32)
        ln_gamma = jnp.ones((DIM,), jnp.float32)
        ln_beta = jnp.zeros((DIM,), jnp.float32)
        w_q = jax.random.normal(ks[2], (DIM, INNER), dtype=jnp.float32) / np.sqrt(DIM)
        w_kv = jax.random.normal(ks[3], (DIM, 2 * INNER), dtype=jnp.float32) / np.sqrt(DIM)
        w_out = jax.random.normal(ks[4], (INNER, DIM), dtype=jnp.float32) / np.sqrt(INNER)
        b_out = jnp.zeros((DIM,), jnp.float32)
        gate = jnp.array([0.5], jnp.float32)
        return {'x': x, 'context': context, 'ln_gamma': ln_gamma, 'ln_beta': ln_beta, 'w_q': w_q, 'w_kv': w_kv, 'w_out': w_out, 'b_out': b_out, 'gate': gate}
    _L0_xattn_all = _L0_xattn_setup()
    _L0_xattn_in = {k: v for k, v in _L0_xattn_all.items() if k in ('ln_gamma', 'ln_beta', 'w_q', 'w_kv', 'w_out', 'b_out', 'gate')}
    del _L0_xattn_all

    def _L0_ffn_setup():
        import jax, jax.numpy as jnp
        import numpy as np
        DIM = 128

        def _reference_tuple_inner(x, W_r, W_k, W_v, mu_r, mu_k):
            B, T, C = x.shape
            x_prev = jnp.concatenate([jnp.zeros((B, 1, C), x.dtype), x[:, :-1, :]], axis=1)
            xr = mu_r * x + (1.0 - mu_r) * x_prev
            xk = mu_k * x + (1.0 - mu_k) * x_prev
            r = jax.nn.sigmoid(jnp.einsum('btc,dc->btd', xr, W_r))
            k = jnp.einsum('btc,dc->btd', xk, W_k)
            k_act = jnp.square(jax.nn.relu(k))
            out = r * jnp.einsum('btc,dc->btd', k_act, W_v)
            new_state = x[:, -1, :]
            return (out, new_state)
        key = jax.random.key(seed)
        ks = jax.random.split(key, 6)
        B, T, C = (8, 256, DIM)
        x = jax.random.normal(ks[0], (B, T, C), dtype=jnp.float32)
        s = 1.0 / np.sqrt(C)
        W_r = jax.random.uniform(ks[1], (C, C), jnp.float32, -s, s)
        W_k = jax.random.uniform(ks[2], (C, C), jnp.float32, -s, s)
        W_v = jax.random.uniform(ks[3], (C, C), jnp.float32, -s, s)
        mu_r = jax.random.uniform(ks[4], (C,), jnp.float32)
        mu_k = jax.random.uniform(ks[5], (C,), jnp.float32)
        return {'x': x, 'W_r': W_r, 'W_k': W_k, 'W_v': W_v, 'mu_r': mu_r, 'mu_k': mu_k}
    _L0_ffn_all = _L0_ffn_setup()
    _L0_ffn_in = {k: v for k, v in _L0_ffn_all.items() if k in ('W_r', 'W_k', 'W_v', 'mu_r', 'mu_k')}
    del _L0_ffn_all

    def _L1_attn_setup():
        import math
        import jax, jax.numpy as jnp
        import numpy as np
        B, C, D = (4, 256, 128)
        DQ = DV = 64
        H = 16
        key = jax.random.key(seed)
        kx, kq, kk, kv, kw = jax.random.split(key, 5)
        x = jax.random.normal(kx, (B, C, D), dtype=jnp.float32)
        Q = jax.random.normal(kq, (DQ, D, H), dtype=jnp.float32) / math.sqrt(D)
        K = jax.random.normal(kk, (DQ, D, H), dtype=jnp.float32) / math.sqrt(D)
        V = jax.random.normal(kv, (DV, D, H), dtype=jnp.float32) / math.sqrt(D)
        W = jax.random.normal(kw, (D, DV, H), dtype=jnp.float32) / math.sqrt(DV)
        return {'x': x, 'Q': Q, 'K': K, 'V': V, 'W': W}
    _L1_attn_all = _L1_attn_setup()
    _L1_attn_in = {k: v for k, v in _L1_attn_all.items() if k in ('Q', 'K', 'V', 'W')}
    del _L1_attn_all

    def _L1_xattn_setup():
        import jax, jax.numpy as jnp
        import numpy as np
        B, S, D, NH = (2, 256, 128, 8)
        DH = D // NH
        EPS = 1e-06
        LN_EPS = 1e-05

        def _mlstm_cell(q, k, v, igate_w, igate_b, fgate_w, fgate_b, ln_scale):
            Slen = q.shape[0]
            ifg = jnp.concatenate([q, k, v], axis=-1)
            ig = (ifg @ igate_w.T + igate_b).T
            fg = (ifg @ fgate_w.T + fgate_b).T
            qh = q.reshape(Slen, NH, DH).transpose(1, 0, 2)
            kh = k.reshape(Slen, NH, DH).transpose(1, 0, 2)
            vh = v.reshape(Slen, NH, DH).transpose(1, 0, 2)
            log_f = jax.nn.log_sigmoid(fg)
            cs = jnp.cumsum(log_f, axis=1)
            fg_mat = cs[:, :, None] - cs[:, None, :]
            mask = jnp.tril(jnp.ones((Slen, Slen), dtype=bool))
            log_fg_mat = jnp.where(mask, fg_mat, -jnp.inf)
            log_D = log_fg_mat + ig[:, None, :]
            max_log_D = jnp.max(log_D, axis=-1, keepdims=True)
            D_mat = jnp.exp(log_D - max_log_D)
            qk = jnp.einsum('hsd,htd->hst', qh, kh) / np.sqrt(DH)
            C = qk * D_mat
            normalizer = jnp.maximum(jnp.abs(C.sum(axis=-1, keepdims=True)), jnp.exp(-max_log_D))
            h = jnp.einsum('hst,htd->hsd', C / (normalizer + EPS), vh)
            h = h.transpose(1, 0, 2).reshape(Slen, D)
            mu = h.mean(axis=-1, keepdims=True)
            var = h.var(axis=-1, keepdims=True)
            return (h - mu) / jnp.sqrt(var + LN_EPS) * ln_scale
        key = jax.random.key(seed)
        ks = jax.random.split(key, 8)
        rnd = lambda k, sh, s=1.0: jax.random.normal(k, sh, dtype=jnp.float32) * s
        return {'q': rnd(ks[0], (B, S, D)), 'k': rnd(ks[1], (B, S, D)), 'v': rnd(ks[2], (B, S, D)), 'igate_w': rnd(ks[3], (NH, 3 * D), 0.02), 'igate_b': jnp.linspace(3.0, 6.0, NH, dtype=jnp.float32), 'fgate_w': rnd(ks[4], (NH, 3 * D), 0.02), 'fgate_b': rnd(ks[5], (NH,), 0.3162278), 'ln_scale': jnp.ones((D,), dtype=jnp.float32)}
    _L1_xattn_all = _L1_xattn_setup()
    _L1_xattn_in = {k: v for k, v in _L1_xattn_all.items() if k in ('igate_w', 'igate_b', 'fgate_w', 'fgate_b', 'ln_scale')}
    del _L1_xattn_all

    def _L1_ffn_setup():
        import jax, jax.numpy as jnp
        import numpy as np
        B, S, H, DV = (4, 512, 128, 128)
        E, INNER, P, K = (8, 32, 8, 2)

        def _ln(v, g, b, eps=1e-05):
            m = jnp.mean(v, axis=-1, keepdims=True)
            var = jnp.var(v, axis=-1, keepdims=True)
            return (v - m) * jax.lax.rsqrt(var + eps) * g + b
        key = jax.random.key(seed)
        ks = jax.random.split(key, 8)
        sc = lambda d: 1.0 / np.sqrt(d)
        return {'x': jax.random.normal(ks[0], (B, S, H), jnp.float32), 'Wv': jax.random.normal(ks[1], (DV, H), jnp.float32) * sc(H), 'bv': jnp.zeros((DV,), jnp.float32), 'Wg': jax.random.normal(ks[2], (E, DV), jnp.float32) * sc(DV), 'bg': jnp.zeros((E,), jnp.float32), 'Wp': jax.random.normal(ks[3], (E, P, DV), jnp.float32) * sc(DV), 'alpha': jnp.zeros((), jnp.float32), 'g_r': jnp.ones((E,), jnp.float32), 'b_r': jnp.zeros((E,), jnp.float32), 'g_c': jnp.ones((E,), jnp.float32), 'b_c': jnp.zeros((E,), jnp.float32), 'W1': jax.random.normal(ks[4], (E, INNER, DV), jnp.float32) * sc(DV), 'b1': jnp.zeros((E, INNER), jnp.float32), 'W2': jax.random.normal(ks[5], (E, DV, INNER), jnp.float32) * sc(INNER), 'b2': jnp.zeros((E, DV), jnp.float32)}
    _L1_ffn_all = _L1_ffn_setup()
    _L1_ffn_in = {k: v for k, v in _L1_ffn_all.items() if k in ('Wv', 'bv', 'Wg', 'bg', 'Wp', 'alpha', 'g_r', 'b_r', 'g_c', 'b_c', 'W1', 'b1', 'W2', 'b2')}
    del _L1_ffn_all

    def _L2_attn_setup():
        import jax, jax.numpy as jnp
        import numpy as np
        H, KV, D = (8, 2, 32)
        RD = D // 4
        ROPE_THETA = 10000.0

        def _rope_cos_sin(seq_len, dtype):
            inv_freq = 1.0 / ROPE_THETA ** (jnp.arange(0, RD, 2, dtype=jnp.float32) / RD)
            pos = jnp.arange(seq_len, dtype=jnp.float32)
            freqs = pos[:, None] * inv_freq[None, :]
            emb = jnp.concatenate([freqs, freqs], axis=-1)
            return (jnp.cos(emb).astype(dtype), jnp.sin(emb).astype(dtype))

        def _apply_partial_rope(x, cos, sin):
            x_rot, x_pass = (x[..., :RD], x[..., RD:])
            half = RD // 2
            rot = jnp.concatenate([-x_rot[..., half:], x_rot[..., :half]], axis=-1)
            x_rot = x_rot * cos[None, None] + rot * sin[None, None]
            return jnp.concatenate([x_rot, x_pass], axis=-1)
        key = jax.random.key(seed)
        ks = jax.random.split(key, 5)
        B, S, hid = (4, 256, 128)
        s = 0.02
        return {'hidden_states': jax.random.normal(ks[0], (B, S, hid), jnp.float32), 'Wq': jax.random.normal(ks[1], (hid, H * D * 2), jnp.float32) * s, 'Wk': jax.random.normal(ks[2], (hid, KV * D), jnp.float32) * s, 'Wv': jax.random.normal(ks[3], (hid, KV * D), jnp.float32) * s, 'Wo': jax.random.normal(ks[4], (H * D, hid), jnp.float32) * s}
    _L2_attn_all = _L2_attn_setup()
    _L2_attn_in = {k: v for k, v in _L2_attn_all.items() if k in ('Wq', 'Wk', 'Wv', 'Wo')}
    del _L2_attn_all

    def _L2_xattn_setup():
        import jax, jax.numpy as jnp
        import numpy as np
        EMBED_DIM = 128
        NUM_HEADS = 16
        HEAD_DIM = EMBED_DIM // NUM_HEADS
        key = jax.random.key(seed)
        ks = jax.random.split(key, 11)
        B, Q, K = (4, 128, 256)
        s = 1.0 / np.sqrt(EMBED_DIM)
        return {'query': jax.random.normal(ks[0], (B, Q, EMBED_DIM), jnp.float32), 'key': jax.random.normal(ks[1], (B, K, EMBED_DIM), jnp.float32), 'value': jax.random.normal(ks[2], (B, K, EMBED_DIM), jnp.float32), 'Wq': jax.random.normal(ks[3], (EMBED_DIM, EMBED_DIM), jnp.float32) * s, 'bq': jnp.zeros((EMBED_DIM,), jnp.float32), 'Wk': jax.random.normal(ks[4], (EMBED_DIM, EMBED_DIM), jnp.float32) * s, 'bk': jnp.zeros((EMBED_DIM,), jnp.float32), 'Wv': jax.random.normal(ks[5], (EMBED_DIM, EMBED_DIM), jnp.float32) * s, 'bv': jnp.zeros((EMBED_DIM,), jnp.float32), 'Wo': jax.random.normal(ks[6], (EMBED_DIM, EMBED_DIM), jnp.float32) * s, 'bo': jnp.zeros((EMBED_DIM,), jnp.float32)}
    _L2_xattn_all = _L2_xattn_setup()
    _L2_xattn_in = {k: v for k, v in _L2_xattn_all.items() if k in ('Wq', 'bq', 'Wk', 'bk', 'Wv', 'bv', 'Wo', 'bo')}
    del _L2_xattn_all

    def _L2_ffn_setup():
        import jax, jax.numpy as jnp
        import numpy as np
        H, I, E, K = (128, 64, 32, 8)
        B, S = (4, 128)

        def silu(x):
            return x * jax.nn.sigmoid(x)
        key = jax.random.key(seed)
        ks = jax.random.split(key, 14)

        def w(k, shape, fan_in):
            return jax.random.normal(k, shape, jnp.float32) / np.float32(np.sqrt(fan_in))
        return {'hidden_states': jax.random.normal(ks[0], (B, S, H), jnp.float32), 'Wr': w(ks[1], (H, E), H), 'br': jnp.zeros((E,), jnp.float32), 'Wg_s': w(ks[2], (H, I), H), 'bg_s': jnp.zeros((I,), jnp.float32), 'Wu_s': w(ks[3], (H, I), H), 'bu_s': jnp.zeros((I,), jnp.float32), 'Wd_s': w(ks[4], (I, H), I), 'bd_s': jnp.zeros((H,), jnp.float32), 'Wg': w(ks[5], (E, H, I), H), 'bg': jnp.zeros((E, I), jnp.float32), 'Wu': w(ks[6], (E, H, I), H), 'bu': jnp.zeros((E, I), jnp.float32), 'Wd': w(ks[7], (E, I, H), I), 'bd': jnp.zeros((E, H), jnp.float32)}
    _L2_ffn_all = _L2_ffn_setup()
    _L2_ffn_in = {k: v for k, v in _L2_ffn_all.items() if k in ('Wr', 'br', 'Wg_s', 'bg_s', 'Wu_s', 'bu_s', 'Wd_s', 'bd_s', 'Wg', 'bg', 'Wu', 'bu', 'Wd', 'bd')}
    del _L2_ffn_all

    def _L3_attn_setup():
        import jax, jax.numpy as jnp
        import numpy as np
        N_EMBD = 128
        N_HEAD = 16
        HEAD = N_EMBD // N_HEAD
        key = jax.random.key(seed)
        k1, k2, k3 = jax.random.split(key, 3)
        x = jax.random.normal(k1, (2, 256, N_EMBD), dtype=jnp.float32)
        W_attn = jax.random.normal(k2, (N_EMBD, 3 * N_EMBD), dtype=jnp.float32) * (1.0 / np.sqrt(N_EMBD))
        W_proj = jax.random.normal(k3, (N_EMBD, N_EMBD), dtype=jnp.float32) * (1.0 / np.sqrt(N_EMBD))
        return {'x': x, 'W_attn': W_attn, 'W_proj': W_proj}
    _L3_attn_all = _L3_attn_setup()
    _L3_attn_in = {k: v for k, v in _L3_attn_all.items() if k in ('W_attn', 'W_proj')}
    del _L3_attn_all

    def _L3_xattn_setup():
        import jax, jax.numpy as jnp
        import numpy as np
        D_MODEL = 128
        NUM_HEADS = 16
        D_K = D_MODEL // NUM_HEADS
        key = jax.random.key(seed)
        ks = jax.random.split(key, 7)
        B, S = (2, 256)
        query = jax.random.normal(ks[0], (B, S, D_MODEL), dtype=jnp.float32)
        key_t = jax.random.normal(ks[1], (B, S, D_MODEL), dtype=jnp.float32)
        value = jax.random.normal(ks[2], (B, S, D_MODEL), dtype=jnp.float32)
        attention_mask = jnp.ones((B, S), dtype=jnp.int32)
        limit = np.sqrt(6.0 / (D_MODEL + D_MODEL)).astype(np.float32)

        def xav(k):
            return jax.random.uniform(k, (D_MODEL, D_MODEL), dtype=jnp.float32, minval=-limit, maxval=limit)
        return {'query': query, 'key': key_t, 'value': value, 'attention_mask': attention_mask, 'w_q': xav(ks[3]), 'w_k': xav(ks[4]), 'w_v': xav(ks[5]), 'w_o': xav(ks[6])}
    _L3_xattn_all = _L3_xattn_setup()
    _L3_xattn_in = {k: v for k, v in _L3_xattn_all.items() if k in ('w_q', 'w_k', 'w_v', 'w_o')}
    del _L3_xattn_all

    def _L3_ffn_setup():
        import jax, jax.numpy as jnp
        import numpy as np
        B, T, C, H, E = (4, 256, 128, 256, 8)
        CAPACITY_FACTOR = 1.0
        key = jax.random.key(seed)
        ks = jax.random.split(key, 5)
        scale = 0.02
        return {'x': jax.random.normal(ks[0], (B, T, C), dtype=jnp.float32), 'Wg': jax.random.normal(ks[1], (E, C), dtype=jnp.float32) * scale, 'W1': jax.random.normal(ks[2], (E, H, C), dtype=jnp.float32) * scale, 'W2': jax.random.normal(ks[3], (E, C, H), dtype=jnp.float32) * scale, 'W3': jax.random.normal(ks[4], (E, H, C), dtype=jnp.float32) * scale}
    _L3_ffn_all = _L3_ffn_setup()
    _L3_ffn_in = {k: v for k, v in _L3_ffn_all.items() if k in ('Wg', 'W1', 'W2', 'W3')}
    del _L3_ffn_all
    return {'x': x, 'ctx_1024': ctx_1024, 'mask_BxS2_if1': mask_BxS2_if1, 'L0_attn_w_in': _L0_attn_in['w_in'], 'L0_attn_b_in': _L0_attn_in['b_in'], 'L0_attn_w_conv': _L0_attn_in['w_conv'], 'L0_attn_b_conv': _L0_attn_in['b_conv'], 'L0_attn_w_x': _L0_attn_in['w_x'], 'L0_attn_b_x': _L0_attn_in['b_x'], 'L0_attn_w_out': _L0_attn_in['w_out'], 'L0_attn_b_out': _L0_attn_in['b_out'], 'L0_xattn_ln_gamma': _L0_xattn_in['ln_gamma'], 'L0_xattn_ln_beta': _L0_xattn_in['ln_beta'], 'L0_xattn_w_q': _L0_xattn_in['w_q'], 'L0_xattn_w_kv': _L0_xattn_in['w_kv'], 'L0_xattn_w_out': _L0_xattn_in['w_out'], 'L0_xattn_b_out': _L0_xattn_in['b_out'], 'L0_xattn_gate': _L0_xattn_in['gate'], 'L0_ffn_W_r': _L0_ffn_in['W_r'], 'L0_ffn_W_k': _L0_ffn_in['W_k'], 'L0_ffn_W_v': _L0_ffn_in['W_v'], 'L0_ffn_mu_r': _L0_ffn_in['mu_r'], 'L0_ffn_mu_k': _L0_ffn_in['mu_k'], 'L1_attn_Q': _L1_attn_in['Q'], 'L1_attn_K': _L1_attn_in['K'], 'L1_attn_V': _L1_attn_in['V'], 'L1_attn_W': _L1_attn_in['W'], 'L1_xattn_igate_w': _L1_xattn_in['igate_w'], 'L1_xattn_igate_b': _L1_xattn_in['igate_b'], 'L1_xattn_fgate_w': _L1_xattn_in['fgate_w'], 'L1_xattn_fgate_b': _L1_xattn_in['fgate_b'], 'L1_xattn_ln_scale': _L1_xattn_in['ln_scale'], 'L1_ffn_Wv': _L1_ffn_in['Wv'], 'L1_ffn_bv': _L1_ffn_in['bv'], 'L1_ffn_Wg': _L1_ffn_in['Wg'], 'L1_ffn_bg': _L1_ffn_in['bg'], 'L1_ffn_Wp': _L1_ffn_in['Wp'], 'L1_ffn_alpha': _L1_ffn_in['alpha'], 'L1_ffn_g_r': _L1_ffn_in['g_r'], 'L1_ffn_b_r': _L1_ffn_in['b_r'], 'L1_ffn_g_c': _L1_ffn_in['g_c'], 'L1_ffn_b_c': _L1_ffn_in['b_c'], 'L1_ffn_W1': _L1_ffn_in['W1'], 'L1_ffn_b1': _L1_ffn_in['b1'], 'L1_ffn_W2': _L1_ffn_in['W2'], 'L1_ffn_b2': _L1_ffn_in['b2'], 'L2_attn_Wq': _L2_attn_in['Wq'], 'L2_attn_Wk': _L2_attn_in['Wk'], 'L2_attn_Wv': _L2_attn_in['Wv'], 'L2_attn_Wo': _L2_attn_in['Wo'], 'L2_xattn_Wq': _L2_xattn_in['Wq'], 'L2_xattn_bq': _L2_xattn_in['bq'], 'L2_xattn_Wk': _L2_xattn_in['Wk'], 'L2_xattn_bk': _L2_xattn_in['bk'], 'L2_xattn_Wv': _L2_xattn_in['Wv'], 'L2_xattn_bv': _L2_xattn_in['bv'], 'L2_xattn_Wo': _L2_xattn_in['Wo'], 'L2_xattn_bo': _L2_xattn_in['bo'], 'L2_ffn_Wr': _L2_ffn_in['Wr'], 'L2_ffn_br': _L2_ffn_in['br'], 'L2_ffn_Wg_s': _L2_ffn_in['Wg_s'], 'L2_ffn_bg_s': _L2_ffn_in['bg_s'], 'L2_ffn_Wu_s': _L2_ffn_in['Wu_s'], 'L2_ffn_bu_s': _L2_ffn_in['bu_s'], 'L2_ffn_Wd_s': _L2_ffn_in['Wd_s'], 'L2_ffn_bd_s': _L2_ffn_in['bd_s'], 'L2_ffn_Wg': _L2_ffn_in['Wg'], 'L2_ffn_bg': _L2_ffn_in['bg'], 'L2_ffn_Wu': _L2_ffn_in['Wu'], 'L2_ffn_bu': _L2_ffn_in['bu'], 'L2_ffn_Wd': _L2_ffn_in['Wd'], 'L2_ffn_bd': _L2_ffn_in['bd'], 'L3_attn_W_attn': _L3_attn_in['W_attn'], 'L3_attn_W_proj': _L3_attn_in['W_proj'], 'L3_xattn_w_q': _L3_xattn_in['w_q'], 'L3_xattn_w_k': _L3_xattn_in['w_k'], 'L3_xattn_w_v': _L3_xattn_in['w_v'], 'L3_xattn_w_o': _L3_xattn_in['w_o'], 'L3_ffn_Wg': _L3_ffn_in['Wg'], 'L3_ffn_W1': _L3_ffn_in['W1'], 'L3_ffn_W2': _L3_ffn_in['W2'], 'L3_ffn_W3': _L3_ffn_in['W3']}

def reference(x, ctx_1024, mask_BxS2_if1, L0_attn_w_in, L0_attn_b_in, L0_attn_w_conv, L0_attn_b_conv, L0_attn_w_x, L0_attn_b_x, L0_attn_w_out, L0_attn_b_out, L0_xattn_ln_gamma, L0_xattn_ln_beta, L0_xattn_w_q, L0_xattn_w_kv, L0_xattn_w_out, L0_xattn_b_out, L0_xattn_gate, L0_ffn_W_r, L0_ffn_W_k, L0_ffn_W_v, L0_ffn_mu_r, L0_ffn_mu_k, L1_attn_Q, L1_attn_K, L1_attn_V, L1_attn_W, L1_xattn_igate_w, L1_xattn_igate_b, L1_xattn_fgate_w, L1_xattn_fgate_b, L1_xattn_ln_scale, L1_ffn_Wv, L1_ffn_bv, L1_ffn_Wg, L1_ffn_bg, L1_ffn_Wp, L1_ffn_alpha, L1_ffn_g_r, L1_ffn_b_r, L1_ffn_g_c, L1_ffn_b_c, L1_ffn_W1, L1_ffn_b1, L1_ffn_W2, L1_ffn_b2, L2_attn_Wq, L2_attn_Wk, L2_attn_Wv, L2_attn_Wo, L2_xattn_Wq, L2_xattn_bq, L2_xattn_Wk, L2_xattn_bk, L2_xattn_Wv, L2_xattn_bv, L2_xattn_Wo, L2_xattn_bo, L2_ffn_Wr, L2_ffn_br, L2_ffn_Wg_s, L2_ffn_bg_s, L2_ffn_Wu_s, L2_ffn_bu_s, L2_ffn_Wd_s, L2_ffn_bd_s, L2_ffn_Wg, L2_ffn_bg, L2_ffn_Wu, L2_ffn_bu, L2_ffn_Wd, L2_ffn_bd, L3_attn_W_attn, L3_attn_W_proj, L3_xattn_w_q, L3_xattn_w_k, L3_xattn_w_v, L3_xattn_w_o, L3_ffn_Wg, L3_ffn_W1, L3_ffn_W2, L3_ffn_W3):
    import jax
    import jax.numpy as jnp

    def _L0_attn_ref(x, w_in, b_in, w_conv, b_conv, w_x, b_x, w_out, b_out):
        import jax, jax.numpy as jnp
        import numpy as np
        D_MODEL, D_STATE, D_INNER = (128, 16, 256)
        EPS = 1e-05

        def bit_linear(x, w, b):
            scale = jnp.maximum(jnp.mean(jnp.abs(w)), EPS)
            ws = w / scale
            wq = ws + jax.lax.stop_gradient(jnp.clip(jnp.round(ws), -1.0, 1.0) - ws)
            return jnp.einsum('bsd,od->bso', x, wq) * scale + b

        def causal_dwconv(x, w, b):
            xc = jnp.transpose(x, (0, 2, 1))
            y = jax.lax.conv_general_dilated(xc, w, window_strides=(1,), padding=[(3, 0)], feature_group_count=w.shape[0], dimension_numbers=('NCH', 'OIH', 'NCH'))
            y = y + b[None, :, None]
            return jnp.transpose(y, (0, 2, 1))
        x_and_res = bit_linear(x, w_in, b_in)
        x_inner = x_and_res[..., :D_INNER]
        x_conv = jax.nn.silu(causal_dwconv(x_inner, w_conv, b_conv))
        ssm_params = bit_linear(x_conv, w_x, b_x)
        delta = ssm_params[..., :D_INNER]
        gate = jax.nn.sigmoid(delta)
        y = x_conv * gate
        return bit_linear(y, w_out, b_out)

    def _L0_xattn_ref(x, context, ln_gamma, ln_beta, w_q, w_kv, w_out, b_out, gate):
        import jax, jax.numpy as jnp
        import numpy as np
        DIM = 128
        NUM_HEADS = 16
        DIM_HEAD = 64
        INNER = NUM_HEADS * DIM_HEAD
        SCALE = DIM_HEAD ** (-0.5)

        def _layernorm(x, gamma, beta, eps=1e-05):
            mu = jnp.mean(x, axis=-1, keepdims=True)
            var = jnp.mean(jnp.square(x - mu), axis=-1, keepdims=True)
            return (x - mu) * jax.lax.rsqrt(var + eps) * gamma + beta
        B, SQ, _ = x.shape
        SK = context.shape[1]
        xn = _layernorm(x, ln_gamma, ln_beta)
        q = (xn @ w_q).reshape(B, SQ, NUM_HEADS, DIM_HEAD)
        kv = context @ w_kv
        k, v = jnp.split(kv, 2, axis=-1)
        k = k.reshape(B, SK, NUM_HEADS, DIM_HEAD)
        v = v.reshape(B, SK, NUM_HEADS, DIM_HEAD)
        scores = jnp.einsum('bqhd,bkhd->bhqk', q * SCALE, k)
        attn = jax.nn.softmax(scores, axis=-1)
        out = jnp.einsum('bhqk,bkhd->bqhd', attn, v).reshape(B, SQ, INNER)
        out = out @ w_out + b_out
        return out * jnp.tanh(gate[0])

    def _L0_ffn_ref(x, W_r, W_k, W_v, mu_r, mu_k):
        import jax, jax.numpy as jnp
        import numpy as np
        DIM = 128

        def _reference_tuple_inner(x, W_r, W_k, W_v, mu_r, mu_k):
            B, T, C = x.shape
            x_prev = jnp.concatenate([jnp.zeros((B, 1, C), x.dtype), x[:, :-1, :]], axis=1)
            xr = mu_r * x + (1.0 - mu_r) * x_prev
            xk = mu_k * x + (1.0 - mu_k) * x_prev
            r = jax.nn.sigmoid(jnp.einsum('btc,dc->btd', xr, W_r))
            k = jnp.einsum('btc,dc->btd', xk, W_k)
            k_act = jnp.square(jax.nn.relu(k))
            out = r * jnp.einsum('btc,dc->btd', k_act, W_v)
            new_state = x[:, -1, :]
            return (out, new_state)
        return _reference_tuple_inner(x, W_r, W_k, W_v, mu_r, mu_k)[0]

    def _L1_attn_ref(x, Q, K, V, W):
        import math
        import jax, jax.numpy as jnp
        import numpy as np
        B, C, D = (4, 256, 128)
        DQ = DV = 64
        H = 16
        d_query, d_embed, num_heads = Q.shape
        d_value = V.shape[0]
        sq = math.sqrt(d_query / d_embed)
        sv = math.sqrt(d_value / d_embed)
        q = jnp.einsum('qdh,bcd->bhcq', Q, x) * sq
        k = jnp.einsum('qdh,bcd->bhcq', K, x) * sq
        v = jnp.einsum('vdh,bcd->bhcv', V, x) * sv
        att = jnp.einsum('bhcq,bhCq->bhcC', q, k) / d_query
        T = x.shape[1]
        causal = jnp.arange(T)[:, None] >= jnp.arange(T)[None, :]
        att = jnp.where(causal, att, -jnp.inf)
        p = jax.nn.softmax(att, axis=-1)
        y = jnp.einsum('bhcC,bhCv->bhcv', p, v)
        z = jnp.einsum('dvh,bhcv->bcd', W, y) * (math.sqrt(d_embed / d_value) / num_heads)
        return z

    def _L1_xattn_ref(q, k, v, igate_w, igate_b, fgate_w, fgate_b, ln_scale):
        import jax, jax.numpy as jnp
        import numpy as np
        B, S, D, NH = (2, 256, 128, 8)
        DH = D // NH
        EPS = 1e-06
        LN_EPS = 1e-05

        def _mlstm_cell(q, k, v, igate_w, igate_b, fgate_w, fgate_b, ln_scale):
            Slen = q.shape[0]
            ifg = jnp.concatenate([q, k, v], axis=-1)
            ig = (ifg @ igate_w.T + igate_b).T
            fg = (ifg @ fgate_w.T + fgate_b).T
            qh = q.reshape(Slen, NH, DH).transpose(1, 0, 2)
            kh = k.reshape(Slen, NH, DH).transpose(1, 0, 2)
            vh = v.reshape(Slen, NH, DH).transpose(1, 0, 2)
            log_f = jax.nn.log_sigmoid(fg)
            cs = jnp.cumsum(log_f, axis=1)
            fg_mat = cs[:, :, None] - cs[:, None, :]
            mask = jnp.tril(jnp.ones((Slen, Slen), dtype=bool))
            log_fg_mat = jnp.where(mask, fg_mat, -jnp.inf)
            log_D = log_fg_mat + ig[:, None, :]
            max_log_D = jnp.max(log_D, axis=-1, keepdims=True)
            D_mat = jnp.exp(log_D - max_log_D)
            qk = jnp.einsum('hsd,htd->hst', qh, kh) / np.sqrt(DH)
            C = qk * D_mat
            normalizer = jnp.maximum(jnp.abs(C.sum(axis=-1, keepdims=True)), jnp.exp(-max_log_D))
            h = jnp.einsum('hst,htd->hsd', C / (normalizer + EPS), vh)
            h = h.transpose(1, 0, 2).reshape(Slen, D)
            mu = h.mean(axis=-1, keepdims=True)
            var = h.var(axis=-1, keepdims=True)
            return (h - mu) / jnp.sqrt(var + LN_EPS) * ln_scale
        return jax.vmap(lambda qq, kk, vv: _mlstm_cell(qq, kk, vv, igate_w, igate_b, fgate_w, fgate_b, ln_scale))(q, k, v)

    def _L1_ffn_ref(x, Wv, bv, Wg, bg, Wp, alpha, g_r, b_r, g_c, b_c, W1, b1, W2, b2):
        import jax, jax.numpy as jnp
        import numpy as np
        B, S, H, DV = (4, 512, 128, 128)
        E, INNER, P, K = (8, 32, 8, 2)

        def _ln(v, g, b, eps=1e-05):
            m = jnp.mean(v, axis=-1, keepdims=True)
            var = jnp.var(v, axis=-1, keepdims=True)
            return (v - m) * jax.lax.rsqrt(var + eps) * g + b
        V = jnp.einsum('bsh,dh->bsd', x, Wv) + bv
        Vf = V.reshape(-1, DV)
        r = Vf @ Wg.T + bg
        pv = jnp.einsum('epd,nd->nep', Wp, Vf)
        c = jnp.sqrt(jnp.sum(pv * pv, axis=-1)) / np.sqrt(P)
        s = _ln(r, g_r, b_r) + jax.nn.sigmoid(alpha) * _ln(c, g_c, b_c)
        topv, sel = jax.lax.top_k(s, K)
        w = jax.nn.softmax(topv, axis=-1)
        delta = jnp.zeros_like(Vf)
        for e in range(E):
            h = jax.nn.silu(Vf @ W1[e].T + b1[e])
            out = h @ W2[e].T + b2[e]
            we = jnp.sum(jnp.where(sel == e, w, 0.0), axis=-1)
            delta = delta + out * we[:, None]
        return (Vf + delta).reshape(V.shape)

    def _L2_attn_ref(hidden_states, Wq, Wk, Wv, Wo):
        import jax, jax.numpy as jnp
        import numpy as np
        H, KV, D = (8, 2, 32)
        RD = D // 4
        ROPE_THETA = 10000.0

        def _rope_cos_sin(seq_len, dtype):
            inv_freq = 1.0 / ROPE_THETA ** (jnp.arange(0, RD, 2, dtype=jnp.float32) / RD)
            pos = jnp.arange(seq_len, dtype=jnp.float32)
            freqs = pos[:, None] * inv_freq[None, :]
            emb = jnp.concatenate([freqs, freqs], axis=-1)
            return (jnp.cos(emb).astype(dtype), jnp.sin(emb).astype(dtype))

        def _apply_partial_rope(x, cos, sin):
            x_rot, x_pass = (x[..., :RD], x[..., RD:])
            half = RD // 2
            rot = jnp.concatenate([-x_rot[..., half:], x_rot[..., :half]], axis=-1)
            x_rot = x_rot * cos[None, None] + rot * sin[None, None]
            return jnp.concatenate([x_rot, x_pass], axis=-1)
        B, S, _ = hidden_states.shape
        G = H // KV
        qg = hidden_states @ Wq
        q, gate = (qg[..., :H * D], qg[..., H * D:])
        k = hidden_states @ Wk
        v = hidden_states @ Wv
        q = q.reshape(B, S, H, D).transpose(0, 2, 1, 3)
        k = k.reshape(B, S, KV, D).transpose(0, 2, 1, 3)
        v = v.reshape(B, S, KV, D).transpose(0, 2, 1, 3)
        cos, sin = _rope_cos_sin(S, q.dtype)
        q = _apply_partial_rope(q, cos, sin)
        k = _apply_partial_rope(k, cos, sin)
        qg4 = q.reshape(B, KV, G, S, D)
        scores = jnp.einsum('bkgsd,bktd->bkgst', qg4, k) / jnp.sqrt(jnp.asarray(D, q.dtype))
        attn = jax.nn.softmax(scores, axis=-1)
        out = jnp.einsum('bkgst,bktd->bkgsd', attn, v)
        out = out.reshape(B, H, S, D).transpose(0, 2, 1, 3).reshape(B, S, H * D)
        out = out * jax.nn.silu(gate)
        return out @ Wo

    def _L2_xattn_ref(query, key, value, Wq, bq, Wk, bk, Wv, bv, Wo, bo):
        import jax, jax.numpy as jnp
        import numpy as np
        EMBED_DIM = 128
        NUM_HEADS = 16
        HEAD_DIM = EMBED_DIM // NUM_HEADS
        B = query.shape[0]
        q = query @ Wq.T + bq
        k = key @ Wk.T + bk
        v = value @ Wv.T + bv
        q = q.reshape(B, -1, NUM_HEADS, HEAD_DIM)
        k = k.reshape(B, -1, NUM_HEADS, HEAD_DIM)
        v = v.reshape(B, -1, NUM_HEADS, HEAD_DIM)
        scores = jnp.einsum('bqhd,bkhd->bhqk', q, k) / np.sqrt(HEAD_DIM).astype(np.float32)
        probs = jax.nn.softmax(scores, axis=-1)
        out = jnp.einsum('bhqk,bkhd->bqhd', probs, v)
        out = out.reshape(B, -1, EMBED_DIM)
        return out @ Wo.T + bo

    def _L2_ffn_ref(hidden_states, Wr, br, Wg_s, bg_s, Wu_s, bu_s, Wd_s, bd_s, Wg, bg, Wu, bu, Wd, bd):
        import jax, jax.numpy as jnp
        import numpy as np
        H, I, E, K = (128, 64, 32, 8)
        B, S = (4, 128)

        def silu(x):
            return x * jax.nn.sigmoid(x)
        b, s, h = hidden_states.shape
        T = b * s
        x = hidden_states.reshape(T, h)
        logits = jnp.dot(x.astype(jnp.float32), Wr) + br
        aff = jax.nn.sigmoid(logits)
        top_v, top_i = jax.lax.top_k(aff, K)
        top_w = top_v / (jnp.sum(top_v, axis=-1, keepdims=True) + 1e-09)
        top_w = top_w.astype(hidden_states.dtype)
        e_total = Wr.shape[1]
        w_full = jnp.zeros((T, e_total), hidden_states.dtype)
        w_full = w_full.at[jnp.arange(T)[:, None], top_i].set(top_w)
        shared = jnp.dot(silu(jnp.dot(x, Wg_s) + bg_s) * (jnp.dot(x, Wu_s) + bu_s), Wd_s) + bd_s
        gate = silu(jnp.einsum('th,ehi->eti', x, Wg) + bg[:, None, :])
        up = jnp.einsum('th,ehi->eti', x, Wu) + bu[:, None, :]
        down = jnp.einsum('eti,eih->eth', gate * up, Wd) + bd[:, None, :]
        routed = jnp.einsum('te,eth->th', w_full, down)
        return (shared + routed).reshape(b, s, h)

    def _L3_attn_ref(x, W_attn, W_proj):
        import jax, jax.numpy as jnp
        import numpy as np
        N_EMBD = 128
        N_HEAD = 16
        HEAD = N_EMBD // N_HEAD
        B, T, C = x.shape
        qkv = x @ W_attn
        q, k, v = jnp.split(qkv, 3, axis=-1)
        q = q.reshape(B, T, N_HEAD, HEAD).transpose(0, 2, 1, 3)
        k = k.reshape(B, T, N_HEAD, HEAD).transpose(0, 2, 1, 3)
        v = v.reshape(B, T, N_HEAD, HEAD).transpose(0, 2, 1, 3)
        att = jnp.einsum('bhqd,bhkd->bhqk', q, k) * (1.0 / np.sqrt(HEAD))
        causal = jnp.tril(jnp.ones((T, T), dtype=bool))
        att = jnp.where(causal[None, None], att, jnp.float32(-jnp.inf))
        att = jax.nn.softmax(att, axis=-1)
        y = jnp.einsum('bhqk,bhkd->bhqd', att, v)
        y = y.transpose(0, 2, 1, 3).reshape(B, T, C)
        return y @ W_proj

    def _L3_xattn_ref(query, key, value, attention_mask, w_q, w_k, w_v, w_o):
        import jax, jax.numpy as jnp
        import numpy as np
        D_MODEL = 128
        NUM_HEADS = 16
        D_K = D_MODEL // NUM_HEADS
        B, S, _ = query.shape

        def proj(x, w):
            y = jnp.einsum('bsd,ed->bse', x, w)
            return y.reshape(B, S, NUM_HEADS, D_K).transpose(0, 2, 1, 3)
        q = proj(query, w_q)
        k = proj(key, w_k)
        v = proj(value, w_v)
        scores = jnp.einsum('bhqd,bhkd->bhqk', q, k) / jnp.sqrt(jnp.float32(D_K))
        mask = attention_mask[:, None, None, :] == 0
        scores = jnp.where(mask, jnp.float32(-1000000000.0), scores)
        attn = jax.nn.softmax(scores, axis=-1)
        context = jnp.einsum('bhqk,bhkd->bhqd', attn, v)
        context = context.transpose(0, 2, 1, 3).reshape(B, S, D_MODEL)
        return jnp.einsum('bsd,ed->bse', context, w_o)

    def _L3_ffn_ref(x, Wg, W1, W2, W3):
        import jax, jax.numpy as jnp
        import numpy as np
        B, T, C, H, E = (4, 256, 128, 256, 8)
        CAPACITY_FACTOR = 1.0
        b, t, c = x.shape
        e = Wg.shape[0]
        n = b * t
        capacity = max(1, int(CAPACITY_FACTOR * n / e))
        x_flat = x.reshape(n, c)
        scores = (x_flat @ Wg.T).T
        top_vals, token_idx = jax.lax.top_k(scores, capacity)
        token_w = jax.nn.softmax(top_vals, axis=-1)
        xg = x_flat[token_idx]
        h = jax.nn.silu(jnp.einsum('eic,ehc->eih', xg, W1)) * jnp.einsum('eic,ehc->eih', xg, W3)
        y = jnp.einsum('eih,ech->eic', h, W2) * token_w[..., None]
        out = jnp.zeros_like(x_flat).at[token_idx.reshape(-1)].add(y.reshape(-1, c))
        return out.reshape(b, t, c)
    x = x + _L0_attn_ref(_layernorm(x, axis=-1), L0_attn_w_in, L0_attn_b_in, L0_attn_w_conv, L0_attn_b_conv, L0_attn_w_x, L0_attn_b_x, L0_attn_w_out, L0_attn_b_out)
    x = x + _L0_xattn_ref(_layernorm(x, axis=-1), ctx_1024, L0_xattn_ln_gamma, L0_xattn_ln_beta, L0_xattn_w_q, L0_xattn_w_kv, L0_xattn_w_out, L0_xattn_b_out, L0_xattn_gate)
    x = x + _L0_ffn_ref(_layernorm(x, axis=-1), L0_ffn_W_r, L0_ffn_W_k, L0_ffn_W_v, L0_ffn_mu_r, L0_ffn_mu_k)
    x = x + _L1_attn_ref(_layernorm(x, axis=-1), L1_attn_Q, L1_attn_K, L1_attn_V, L1_attn_W)
    x = x + _L1_xattn_ref(_layernorm(x, axis=-1), ctx_1024, ctx_1024, L1_xattn_igate_w, L1_xattn_igate_b, L1_xattn_fgate_w, L1_xattn_fgate_b, L1_xattn_ln_scale)
    x = x + _L1_ffn_ref(_layernorm(x, axis=-1), L1_ffn_Wv, L1_ffn_bv, L1_ffn_Wg, L1_ffn_bg, L1_ffn_Wp, L1_ffn_alpha, L1_ffn_g_r, L1_ffn_b_r, L1_ffn_g_c, L1_ffn_b_c, L1_ffn_W1, L1_ffn_b1, L1_ffn_W2, L1_ffn_b2)
    x = x + _L2_attn_ref(_layernorm(x, axis=-1), L2_attn_Wq, L2_attn_Wk, L2_attn_Wv, L2_attn_Wo)
    x = x + _L2_xattn_ref(_layernorm(x, axis=-1), ctx_1024, ctx_1024, L2_xattn_Wq, L2_xattn_bq, L2_xattn_Wk, L2_xattn_bk, L2_xattn_Wv, L2_xattn_bv, L2_xattn_Wo, L2_xattn_bo)
    x = x + _L2_ffn_ref(_layernorm(x, axis=-1), L2_ffn_Wr, L2_ffn_br, L2_ffn_Wg_s, L2_ffn_bg_s, L2_ffn_Wu_s, L2_ffn_bu_s, L2_ffn_Wd_s, L2_ffn_bd_s, L2_ffn_Wg, L2_ffn_bg, L2_ffn_Wu, L2_ffn_bu, L2_ffn_Wd, L2_ffn_bd)
    x = x + _L3_attn_ref(_layernorm(x, axis=-1), L3_attn_W_attn, L3_attn_W_proj)
    x = x + _L3_xattn_ref(_layernorm(x, axis=-1), ctx_1024, ctx_1024, mask_BxS2_if1, L3_xattn_w_q, L3_xattn_w_k, L3_xattn_w_v, L3_xattn_w_o)
    x = x + _L3_ffn_ref(_layernorm(x, axis=-1), L3_ffn_Wg, L3_ffn_W1, L3_ffn_W2, L3_ffn_W3)
    return x

_drawn_inputs = setup_inputs


def setup_inputs(seed=0):
    import zlib

    import numpy as np

    out = dict(_drawn_inputs(seed))
    spreads = {'L0_xattn_ln_gamma': (1.0, 0.2),
     'L0_xattn_ln_beta': (0.0, 0.1),
     'L0_xattn_b_out': (0.0, 0.1),
     'L1_xattn_ln_scale': (1.0, 0.2),
     'L1_ffn_bv': (0.0, 0.1),
     'L1_ffn_bg': (0.0, 0.1),
     'L1_ffn_g_r': (1.0, 0.2),
     'L1_ffn_b_r': (0.0, 0.1),
     'L1_ffn_g_c': (1.0, 0.2),
     'L1_ffn_b_c': (0.0, 0.289),
     'L1_ffn_b1': (0.0, 0.306),
     'L1_ffn_b2': (0.0, 0.1),
     'L2_xattn_bq': (0.0, 0.518),
     'L2_xattn_bk': (0.0, 2.0),
     'L2_xattn_bv': (0.0, 0.1),
     'L2_xattn_bo': (0.0, 0.1),
     'L2_ffn_br': (0.0, 0.269),
     'L2_ffn_bg_s': (0.0, 0.289),
     'L2_ffn_bu_s': (0.0, 0.294),
     'L2_ffn_bd_s': (0.0, 0.308),
     'L2_ffn_bg': (0.0, 0.8),
     'L2_ffn_bu': (0.0, 0.8),
     'L2_ffn_bd': (0.0, 0.507)}
    factors = {'L0_attn_b_in': 6.618,
     'L0_attn_b_conv': 5.817,
     'L0_attn_w_x': 45.238,
     'L0_attn_b_x': 31.05,
     'L1_attn_Q': 2.879,
     'L1_attn_K': 2.869,
     'L2_attn_Wq': 8.0,
     'L2_attn_Wk': 8.0,
     'L2_attn_Wv': 8.0,
     'L2_attn_Wo': 8.0,
     'L3_ffn_Wg': 8.0,
     'L3_ffn_W1': 8.0,
     'L3_ffn_W2': 8.0,
     'L3_ffn_W3': 8.0}
    for name, (base, spread) in spreads.items():
        noise = np.random.default_rng([zlib.crc32(name.encode()), seed]).standard_normal(out[name].shape)
        drawn = base * np.exp(spread * noise) if base else spread * noise
        out[name] = jnp.asarray(drawn.astype(out[name].dtype))
    for name, factor in factors.items():
        out[name] = (out[name] * factor).astype(out[name].dtype)
    return out
```

```python
from contextlib import ExitStack

import numpy as np

import concourse.bass as bass
from concourse import mybir

F32 = mybir.dt.float32
BF16 = mybir.dt.bfloat16
I32 = mybir.dt.int32
U32 = mybir.dt.uint32
ALU = mybir.AluOpType
ACT = mybir.ActivationFunctionType
AX = mybir.AxisListType

B, S, D = 8, 128, 128
P = 128
HALF = B // 2
TOK = B * S
NEG = -1.0e30
PLACES = (("l0a", "l2a"), ("l0x", "l3f"), ("l1a", "l2f"))
SUBLAYERS = ("l0a", "l0x", "l0f", "l1a", "l1x", "l1f", "l2a", "l2x", "l2f", "l3a", "l3x", "l3f")
STOP = 12
BIG_PARTS = np.array([[999292928.0], [704512.0], [2560.0]])


def spread(ap, count, at=1):
    u = ap.unsqueeze(at)
    shape = list(u.shape)
    shape[at] = count
    return u.to_broadcast(shape)


class Count:

    def __init__(self, sem, keys):
        self.sem, self.value, self.last = sem, {k: n + 1 for n, k in enumerate(keys)}, 0

    def inc(self, key):
        assert self.value[key] == self.last + 1, (key, self.last)
        self.last += 1
        return self.sem, 1

    def at(self, key):
        return self.sem, self.value[key]


class Ring:

    def __init__(self, banks, filled, emptied):
        self.banks, self.filled, self.emptied, self.use, self.taken = banks, filled, emptied, {}, 0

    def open(self, pe, name):
        assert name not in self.use, name
        n = len(self.use)
        self.use[name] = n + 1
        if n >= len(self.banks):
            pe.wait_ge(self.emptied, n - len(self.banks) + 1)
        return self.bank(name)

    def take(self, eng, name):
        self.taken = self.use[name]
        eng.wait_ge(self.filled, self.taken)
        return self.bank(name)

    def bank(self, name):
        return self.banks[(self.use[name] - 1) % len(self.banks)]

    def nth(self, name):
        return self.use[name]


def bass_decoder_kernel(nc, groups, ctx_dram, x_dram, mask_dram, rowconst_dram, out_dram):
    with ExitStack() as stack:
        def sb(name, shape, dt=F32):
            return stack.enter_context(nc.sbuf_tensor(name, shape, dt))[(slice(None),) * len(shape)]

        def sem(name):
            return stack.enter_context(nc.semaphore(name))

        store, piece = {}, {}
        widths = {g: dram.shape[1] for g, (dram, _) in groups.items()}
        shared = {}
        for first, later in PLACES:
            shared[first] = shared[later] = sb(f"w_{first}_{later}", [P, max(widths.get(first, 1), widths.get(later, 1))])
        for g, (dram, names) in groups.items():
            if g in ("sel32", "small"):
                continue
            store[g] = shared[g][:, 0:widths[g]] if g in shared else sb(f"w_{g}", [P, widths[g]], dram.dtype)
            for name, (off, rows, cols) in names.items():
                piece[name] = store[g][0:rows, off:off + cols]
        w = piece
        const_bf = sb("const_bf", [P, widths["sel32"] + widths["small"]], BF16)
        for name in ("sel32", "small"):
            for part, (off, rows, cols) in groups[name][1].items():
                w[part] = const_bf[0:rows, off:off + cols] if name == "sel32" else \
                    const_bf[0:rows, widths["sel32"] + off:widths["sel32"] + off + cols]

        x = sb("x", [P, B, D])
        ctx = sb("ctx", [P, B, D])
        ctxT = sb("ctxT", [P, B, S])
        xT_pair = [sb("xT_even", [P, B, S]), sb("xT_odd", [P, B, S])]
        xT_of = {s: xT_pair[i % 2] for i, s in enumerate(SUBLAYERS)}
        xpad = sb("xpad", [P, B, S + 1])
        xT_of["l0f"] = xpad[:, :, 1:S + 1]
        stats = sb("stats", [P, B, 6])
        mv = sb("mv", [P, B, 2])
        veps = sb("veps", [P, B, 1])
        rstd = sb("rstd", [P, B, 1])
        xhat = sb("xhat", [P, B, D])
        power = sb("power", [P, 2])

        big = [sb(f"big{i}", [P, 2, 8, 132]) for i in range(2)]
        qT = sb("qT", [P, 2, 8, S])
        kT = sb("kT", [P, 2, 8, S])
        V = sb("V", [P, 2, 16 * 65])
        V9 = sb("V9", [P, 3, 16, 9])
        V33 = sb("V33", [P, 3, 2, 33])
        prob = sb("prob", [P, 4, 4, S])
        probT = sb("probT", [P, 2, 4, S])
        V17 = prob.rearrange("p m c s -> p (m c s)")[:, 0:B * 136].rearrange("p (b h e) -> p b h e", b=B, e=17)
        store["sel32"] = prob.rearrange("p m c s -> p (m c s)")[:, 0:widths["sel32"]]
        store["small"] = probT.rearrange("p m c s -> p (m c s)")[:, 0:widths["small"]]
        nmax = sb("nmax", [P, 4, 4])
        rden = sb("rden", [P, 4])
        O = sb("O", [P, 2, 16 * 64])
        OT = sb("OT", [P, 2, 8, S])
        small = sb("small", [P, 32])
        wcol = sb("wcol", [P, B, 32])

        psum = stack.enter_context(nc.psum_tensor("psum", [P, 8, 512], F32))
        ring_act = Ring([psum[:, 0, :], psum[:, 1, :]], sem("act_bank_filled"), sem("act_bank_emptied"))
        ring_dve = Ring([psum[:, 2, :], psum[:, 3, :]], sem("dve_bank_filled"), sem("dve_bank_emptied"))
        ring_score = Ring([psum[:, 4, :], psum[:, 5, :]], sem("scores_filled"), sem("scores_emptied"))
        ring_prob = Ring([psum[:, 6, :], psum[:, 7, :]], sem("probT_filled"), sem("probT_emptied"))

        loaded = {g: sem(f"loaded_{g}") for g in groups}
        rowconst_loaded = sem("rowconst_loaded")
        x_loaded, ctx_loaded, mask_loaded, stored = sem("x_loaded"), sem("ctx_loaded"), sem("mask_loaded"), sem("stored")

        subs = SUBLAYERS[:STOP]
        UNITS = {"l0x": 4, "l1a": 4, "l2a": 2, "l2x": 4, "l3a": 4, "l3x": 4}
        norms = [(s, r, b) for s in subs for h in (0, 1) for r in ((0, 1) if s == "l0x" else (0,))
                 for b in range(HALF * h, HALF * h + HALF)]
        stats_ready = Count(sem("stats_ready"), norms)
        rstd_ready = Count(sem("rstd_ready"), norms)
        xhat_ready = Count(sem("xhat_ready"), norms)
        x_final = sem("x_final")
        units = [(s, b, g) for s in subs if s in UNITS for b in range(B) for g in range(UNITS[s])]
        exped = Count(sem("probs_exped"), units)
        pool_ready = sem("pool_ready")
        dve_chain, act_chain, pool_chain = sem("dve_chain"), sem("act_chain"), sem("pool_chain")
        k_masked = Count(sem("k_masked"), [(s, b) for s in subs if s in ("l2a", "l2x", "l3a", "l3x") for b in range(B)])
        roped = Count(sem("rope_products"), [(b,) for b in range(B)])
        tern = sem("ternary_ready")
        const_cast = sem("const_cast")
        mask_ready = sem("mask_ready")
        act_side = sem("act_side")
        dve_side = sem("dve_side")
        act_log, dve_log = [], []
        chains = {"dve": 0, "act": 0, "pool": 0}

        def events(sem_, keys):
            return Count(sem_, keys)

        l0a_conv = events(sem("l0a_conv"), [(c, n) for n in range(2) for c in range(2)])
        l0a_silu = events(sem("l0a_silu_tanh"), [(c, n) for n in range(2) for c in range(2)])
        l0a_xc = events(sem("l0a_xc"), [(c, n) for n in range(2) for c in range(2)])
        l0a_gate = events(sem("l0a_gate_tanh"), [(c, n) for n in range(2) for c in range(2)])
        l0a_y = events(sem("l0a_y"), [(c, n) for n in range(2) for c in range(2)])
        l0a_in = events(sem("l0a_in"), [(c, n) for n in range(2) for c in range(2)])
        scales_ready = sem("scales_ready")
        gate_l0x = sem("gate_l0x")
        l0f_mix = events(sem("l0f_mix"), [(n,) for n in range(2)])
        l0f_r = events(sem("l0f_r_tanh"), [(b,) for b in range(B)])
        mix_k = events(sem("l0f_kact"), [(n,) for n in range(2)])
        lstm_f = sem("lstm_f")
        lstm_e = sem("lstm_e")
        lstm_D = events(sem("lstm_D"), [(b,) for b in range(B)])
        lstm_q = events(sem("lstm_q"), [(b,) for b in range(B)])
        lstm_C = events(sem("lstm_C"), [(b,) for b in range(B)])
        lstm_var = events(sem("lstm_var"), [(b,) for b in range(B)])
        lstm_rstd = events(sem("lstm_rstd"), [(b,) for b in range(B)])
        v_ready = sem("v_ready")
        rt = sem("router_dve")
        rp = sem("router_pool")
        ra = sem("router_act")
        rt_n, rp_n, ra_n = [0], [0], [0]

        def ln_stats(dve, s, b, r=0):
            src = x if r == 0 else xhat
            link(dve, nc.vector.bn_stats(stats[:, b, :], src[:, b, :]))
            nc.vector.bn_aggr(mv[:, b, :], stats[:, b, :]).then_inc(*stats_ready.inc((s, r, b)))
            dve.wait_ge(*stats_ready.at((s, r, b)))

        def ln_rstd(pool, s, b, r=0):
            pool.wait_ge(*stats_ready.at((s, r, b)))
            plink(pool, nc.gpsimd.tensor_scalar(veps[:, b, :], mv[:, b, 1:2], 1e-5, None, ALU.add))
            nc.gpsimd.tensor_tensor(rstd[:, b, :], veps[:, b, :], power[:, 0:1], ALU.pow).then_inc(
                *rstd_ready.inc((s, r, b)))
            pool.wait_ge(*rstd_ready.at((s, r, b)))

        def ln_xhat(dve, s, b, r=0):
            src = x if r == 0 else xhat
            dve.wait_ge(*rstd_ready.at((s, r, b)))
            nc.vector.tensor_scalar(xhat[:, b, :], src[:, b, :], mv[:, b, 0:1], rstd[:, b, :], ALU.subtract,
                                    ALU.mult).then_inc(*xhat_ready.inc((s, r, b)))
            dve.wait_ge(*xhat_ready.at((s, r, b)))
            if s == "l0x" and r == 0:
                dve.wait_ge(*xhat_ready.at((s, r, b)))

        def ln_transpose(pe, s, bs):
            bank = ring_act.open(pe, ("xT", s, bs))
            for i, b in enumerate(bs):
                pe.wait_ge(*xhat_ready.at((s, 1 if s == "l0x" else 0, b)))
                last = nc.tensor.transpose(bank[:, i * S:(i + 1) * S], xhat[:, b, :], w["ident"])
            last.then_inc(ring_act.filled, 1)

        def ln_copy(act, s, bs):
            bank = ring_act.take(act, ("xT", s, bs))
            src = bank[:, 0:len(bs) * S].rearrange("p (b t) -> p b t", t=S)
            dst = xT_of[s][:, bs[0]:bs[-1] + 1, :]
            if s == "l0x":
                act.wait_ge(loaded["l0x"], 16)
                nc.scalar.activation(dst, src, ACT.Identity, scale=w["x0_gamma"],
                                     bias=w["x0_beta"]).then_inc(ring_act.emptied, 1)
            else:
                nc.scalar.activation(dst, src, ACT.Copy).then_inc(ring_act.emptied, 1)

        def xT_use(s, b):
            return next(n for name, n in ring_act.use.items() if name[0:2] == ("xT", s) and b in name[2])

        def xT_wait(pe, s, b):
            pe.wait_ge(ring_act.emptied, xT_use(s, b))

        def link(dve, ins):
            chains["dve"] += 1
            ins.then_inc(dve_chain, 1)
            dve.wait_ge(dve_chain, chains["dve"])

        def alink(act, ins):
            chains["act"] += 1
            ins.then_inc(act_chain, 1)
            act.wait_ge(act_chain, chains["act"])

        def plink(pool, ins):
            chains["pool"] += 1
            ins.then_inc(pool_chain, 1)
            pool.wait_ge(pool_chain, chains["pool"])

        halves = [tuple(range(HALF * n, HALF * n + HALF)) for n in range(2)]

        def next_of(s):
            i = SUBLAYERS.index(s) + 1
            return SUBLAYERS[i] if i < STOP else None

        def finish_stats(dve, s, b):
            if next_of(s):
                ln_stats(dve, next_of(s), b)

        xin = big[0][:, :, :, 0:131]
        ycv = big[1][:, :, :, 0:S]
        xc2 = qT
        y4 = kT
        tin = OT[:, 0, 0:2, :].rearrange("p c s -> p (c s)")
        tx = OT[:, 0, 2:6, :].rearrange("p (c o) s -> p c (o s)", c=2)
        tout = OT[:, 0, 6:8, :]
        tern_w = [("l0a_win", 512 * 128, slice(0, 256)), ("l0a_wx", 400 * 256, None), ("l0a_wout", 128 * 256, None)]
        absum = small[:, 0:3]
        scl = small[:, 4:7]
        thr = small[:, 8:11]
        nthr = small[:, 12:15]
        lowmask = O[:, :, :].rearrange("p a (m c) -> p (a m) c", c=256)
        qscale = small[:, 16:20]
        hbias = small[:, 20:22]

        def tensor_l0a(pe):
            pe.wait_ge(scales_ready, 1)
            bank = ring_dve.open(pe, ("scales",))
            pe.wait_ge(loaded["const"], 16)
            nc.tensor.matmul(bank[:, 0:3], w["ones"], absum, start=True, stop=True).then_inc(ring_dve.filled, 1)
            for n in range(2):
                ln_transpose(pe, "l0a", halves[n])
            pe.wait_ge(tern, 1)
            for n in range(2):
                xT_wait(pe, "l0a", halves[n][0])
                for c in range(2):
                    bank = ring_act.open(pe, ("xin", c, n))
                    nc.tensor.matmul(bank, tin[:, c * P:(c + 1) * P], xT_of["l0a"][:, halves[n][0]:halves[n][0] + 4, :],
                                     start=True, stop=True).then_inc(ring_act.filled, 1)
            for n in range(2):
                for c2 in range(2):
                    bank = ring_act.open(pe, ("delta", c2, n))
                    for c in range(2):
                        pe.wait_ge(*l0a_xc.at((c, n)))
                        last = nc.tensor.matmul(bank, tx[:, c, c2 * P:(c2 + 1) * P], xc2[:, c, 4 * n:4 * n + 4, :],
                                                start=(c == 0), stop=(c == 1))
                    last.then_inc(ring_act.filled, 1)
            for n in range(2):
                bank = ring_dve.open(pe, ("out", "l0a", n))
                for c in range(2):
                    pe.wait_ge(*l0a_y.at((c, n)))
                for i in range(HALF):
                    for c in range(2):
                        last = nc.tensor.matmul(bank[:, i * D:(i + 1) * D], y4[:, c, 4 * n + i, :], tout[:, c, :],
                                                start=(c == 0), stop=(c == 1))
                last.then_inc(ring_dve.filled, 1)
            finish_pe(pe, "l0a")

        def finish_pe(pe, s):
            if next_of(s):
                for n in range(2):
                    ln_transpose(pe, next_of(s), halves[n])

        def finish_act(act, s):
            if next_of(s):
                for n in range(2):
                    ln_copy(act, next_of(s), halves[n])

        def finish_pool(pool, s):
            if next_of(s):
                for n in range(2):
                    for r in ((0, 1) if next_of(s) == "l0x" else (0,)):
                        for b in halves[n]:
                            ln_rstd(pool, next_of(s), b, r)

        def finish_dve(dve, s, n):
            if not next_of(s):
                return
            for b in halves[n]:
                ln_stats(dve, next_of(s), b)
            for b in halves[n]:
                ln_xhat(dve, next_of(s), b)
            if next_of(s) == "l0x":
                for b in halves[n]:
                    ln_stats(dve, "l0x", b, 1)
                for b in halves[n]:
                    ln_xhat(dve, "l0x", b, 1)

        def scalar_l0a(act):
            for n in range(2):
                ln_copy(act, "l0a", halves[n])
            act.wait_ge(loaded["l0a"], 16)
            act.wait_ge(tern, 1)
            act.wait_ge(pool_ready, 1)
            for n in range(2):
                for c in range(2):
                    bank = ring_act.take(act, ("xin", c, n))
                    nc.scalar.activation(xin[:, c, 4 * n:4 * n + 4, 3:131], bank.rearrange("p (b t) -> p b t", t=S),
                                         ACT.Identity, scale=scl[:, 0:1], bias=w["l0a_bin"][:, c:c + 1]
                                         ).then_inc(ring_act.emptied, 1)
            for n in range(2):
                for c in range(2):
                    act.wait_ge(*l0a_conv.at((c, n)))
                    nc.scalar.activation(xc2[:, c, 4 * n:4 * n + 4, :], ycv[:, c, 4 * n:4 * n + 4, :], ACT.Tanh,
                                         scale=0.5).then_inc(*l0a_silu.inc((c, n)))
            for n in range(2):
                for c in range(2):
                    bank = ring_act.take(act, ("delta", c, n))
                    nc.scalar.activation(y4[:, c, 4 * n:4 * n + 4, :], bank.rearrange("p (b t) -> p b t", t=S),
                                         ACT.Tanh, scale=qscale[:, 0:1], bias=hbias[:, c:c + 1]
                                         ).then_inc(ring_act.emptied, 1)
            finish_act(act, "l0a")

        def vector_l0a(dve):
            dve.wait_ge(x_loaded, 16)
            for n in range(2):
                for b in halves[n]:
                    ln_stats(dve, "l0a", b)
                for b in halves[n]:
                    ln_xhat(dve, "l0a", b)
            dve.wait_ge(loaded["l0a"], 16)
            for i, (name, _, _) in enumerate(tern_w):
                last = nc.vector.tensor_reduce(absum[:, i:i + 1], w[name], AX.X, ALU.add, apply_absolute_value=True)
            last.then_inc(scales_ready, 1)
            dve.wait_ge(scales_ready, 1)
            bank = ring_dve.take(dve, ("scales",))
            for i, (_, count, _) in enumerate(tern_w):
                last = nc.vector.tensor_scalar(scl[:, i:i + 1], bank[:, i:i + 1], 1.0 / count, 1e-5, ALU.mult, ALU.max)
            last.then_inc(ring_dve.emptied, 1)
            dve.wait_ge(ring_dve.emptied, ring_dve.nth(("scales",)))
            link(dve, nc.vector.tensor_scalar(thr, scl, 0.5, None, ALU.mult))
            link(dve, nc.vector.tensor_scalar(nthr, scl, -0.5, None, ALU.mult))
            link(dve, nc.vector.tensor_scalar(qscale[:, 0:1], scl[:, 1:2], 0.25, None, ALU.mult))
            link(dve, nc.vector.tensor_scalar(qscale[:, 1:2], scl[:, 2:3], 0.25, None, ALU.mult))
            link(dve, nc.vector.tensor_scalar(hbias, w["l0a_bx"], 0.5, None, ALU.mult))
            parts = [(tin, w["l0a_win"][:, 0:256], 0)]
            parts += [(tx[:, c, :], w["l0a_wx"][:, c * 400:c * 400 + 256], 1) for c in range(2)]
            parts += [(tout[:, c, :], w["l0a_wout"][:, c * P:(c + 1) * P], 2) for c in range(2)]
            for m, (dst, src, i) in enumerate(parts):
                low = lowmask[:, m, 0:src.shape[1]]
                link(dve, nc.vector.tensor_scalar(low, src, nthr[:, i:i + 1], None, ALU.is_lt))
                last = nc.vector.scalar_tensor_tensor(out=dst, in0=src, scalar=thr[:, i:i + 1], in1=low,
                                                      op0=ALU.is_gt, op1=ALU.subtract)
            last.then_inc(tern, 1)
            dve.wait_ge(tern, 1)
            for n in range(2):
                for c in range(2):
                    dve.wait_ge(ring_act.emptied, ring_act.nth(("xin", c, n)))
                    y = ycv[:, c, 4 * n:4 * n + 4, :]
                    xi = xin[:, c, 4 * n:4 * n + 4, :]
                    wc = w["l0a_wconv"]
                    link(dve, nc.vector.tensor_scalar(y, xi[:, :, 3:131], wc[:, 4 * c + 3:4 * c + 4],
                                                      w["l0a_bconv"][:, c:c + 1], ALU.mult, ALU.add))
                    for j in range(3):
                        ins = nc.vector.scalar_tensor_tensor(out=y, in0=xi[:, :, j:j + S],
                                                             scalar=wc[:, 4 * c + j:4 * c + j + 1], in1=y,
                                                             op0=ALU.mult, op1=ALU.add)
                        if j < 2:
                            link(dve, ins)
                    ins.then_inc(*l0a_conv.inc((c, n)))
                    dve.wait_ge(*l0a_conv.at((c, n)))
            for n in range(2):
                for c in range(2):
                    dve.wait_ge(*l0a_silu.at((c, n)))
                    t = xc2[:, c, 4 * n:4 * n + 4, :]
                    nc.vector.scalar_tensor_tensor(out=t, in0=t, scalar=1.0, in1=ycv[:, c, 4 * n:4 * n + 4, :],
                                                   op0=ALU.add, op1=ALU.mult).then_inc(*l0a_xc.inc((c, n)))
                    dve.wait_ge(*l0a_xc.at((c, n)))
            for n in range(2):
                for c in range(2):
                    dve.wait_ge(ring_act.emptied, ring_act.nth(("delta", c, n)))
                    dve.wait_ge(*l0a_xc.at((c, n)))
                    t = y4[:, c, 4 * n:4 * n + 4, :]
                    nc.vector.scalar_tensor_tensor(out=t, in0=t, scalar=1.0, in1=xc2[:, c, 4 * n:4 * n + 4, :],
                                                   op0=ALU.add, op1=ALU.mult).then_inc(*l0a_y.inc((c, n)))
                    dve.wait_ge(*l0a_y.at((c, n)))
            for n in range(2):
                bank = ring_dve.take(dve, ("out", "l0a", n))
                xs = x[:, 4 * n:4 * n + 4, :]
                ins = nc.vector.scalar_tensor_tensor(out=xs, in0=bank.rearrange("p (b d) -> p b d", d=D),
                                                     scalar=qscale[:, 1:2], in1=xs, op0=ALU.mult, op1=ALU.add)
                ins.then_inc(ring_dve.emptied, 1)
                dve.wait_ge(ring_dve.emptied, ring_dve.nth(("out", "l0a", n)))
                link(dve, nc.vector.tensor_tensor(xs, xs, spread(w["l0a_bout"], 4), ALU.add))
                finish_dve(dve, "l0a", n)

        def gpsimd_l0a(pool):
            plink(pool, nc.gpsimd.memset(power[:, 0:1], -0.5))
            plink(pool, nc.gpsimd.memset(power[:, 1:2], 0.5))
            plink(pool, nc.gpsimd.memset(xin[:, :, :, 0:3], 0.0))
            plink(pool, nc.gpsimd.memset(xpad[:, :, 0:1], 0.0))
            plink(pool, nc.gpsimd.memset(V[:, :, :], 1.0))
            plink(pool, nc.gpsimd.memset(V9[:, :, :, :], 1.0))
            nc.gpsimd.memset(V33[:, :, :, :], 1.0).then_inc(pool_ready, 1)
            pool.wait_ge(pool_ready, 1)
            for n in range(2):
                for b in halves[n]:
                    ln_rstd(pool, "l0a", b)
            pool.wait_ge(loaded["small"], 16)
            pool.wait_ge(loaded["sel32"], 16)
            nc.gpsimd.tensor_copy(const_bf[:, widths["sel32"]:], store["small"]).then_inc(const_cast, 1)
            nc.gpsimd.tensor_copy(const_bf[:, 0:widths["sel32"]], store["sel32"]).then_inc(const_cast, 1)
            pool.wait_ge(const_cast, 2)
            finish_pool(pool, "l0a")

        SPEC = {
            "l0x": dict(kind="wide", dh=64, wq="x0_wq", wk="x0_wk", wv="x0_wv", wo="x0_wo", kv="ctx", causal=False,
                        scale=64 ** -0.5),
            "l1a": dict(kind="wide", dh=64, wq="a1_wq", wk="a1_wk", wv="a1_wv", wo="a1_wo", kv="x", causal=True,
                        scale=0.5 / 64, alpha=0.5 ** 0.5 * 2 ** 0.5 / 16),
            "l2a": dict(kind="rope", dh=32, kv="x", causal=False, scale=32 ** -0.5, alpha=0.5),
            "l2x": dict(kind="narrow", dh=8, wq="x2_wq", wk="x2_wk", wv="x2_wv", wo="x2_wo", kv="ctx", causal=False,
                        scale=8 ** -0.5, alpha=1.0, bias=True),
            "l3a": dict(kind="narrow", dh=8, wq="a3_wq", wk="a3_wk", wv="a3_wv", wo="a3_wo", kv="x", causal=True,
                        scale=8 ** -0.5, alpha=1.0),
            "l3x": dict(kind="narrow", dh=8, wq="x3_wq", wk="x3_wk", wv="x3_wv", wo="x3_wo", kv="ctx", causal=False,
                        scale=1.0, qscale=8 ** -0.5, alpha=1.0, masked=True),
        }

        def attention_steps(s):
            U = UNITS[s]
            total = U * B
            later = {}
            for t in range(total + 9):
                if t == 0:
                    yield "project", 0, 0
                if t < total:
                    yield "score", t // U, t % U
                if 0 <= t - 2 < total:
                    yield "transpose", (t - 2) // U, (t - 2) % U
                if 0 <= t - 3 < total:
                    b, g = (t - 3) // U, (t - 3) % U
                    yield "value", b, g
                    if g == U - 1:
                        for d, step in ((1, "outT"), (2, "out"), (3, "norm")):
                            later.setdefault(t + d, []).append((step, b, 0))
                if t < total and t % U == U - 1 and t // U + 1 < B:
                    yield "project", t // U + 1, 0
                for step in later.pop(t, []):
                    yield step
            assert not later

        src_of = {"ctx": lambda s: ctxT, "x": lambda s: xT_of[s]}
        mask01 = big[0][:, 0, :, 0:S]
        maskrow = sb("maskrow", [P, B, S], BF16)
        mask_i = xpad[:, :, :].rearrange("p b t -> p (b t)").bitcast(I32)[:, 0:TOK].rearrange("p (b t) -> p b t", t=S)
        kraw = sb("kraw", [P, 3, 2, S])
        kmask = sb("kmask", [P, 3, 2, 4, S])
        rowconst = kmask[0:8, :, :, :, :].rearrange("p m a c s -> p m (a c s)")
        bdones, notfirst, negfirst = (rowconst[:, i, :] for i in range(3))
        rope1 = V[:, 0, 0:1024].rearrange("p (a c s) -> p a c s", a=2, s=S)
        rope2 = V[:, 1, 0:1024].rearrange("p (a c s) -> p a c s", a=2, s=S)
        gate2 = sb("gate2", [P, 3, 256])
        tgate = sb("tgate", [P, 1])

        def buf(s, b):
            return b % (2 if SPEC[s]["kind"] == "wide" else 3)

        def heads_of(s, g):
            if SPEC[s]["kind"] == "wide":
                return slice(8 * (g // 2) + g % 2, 8 * (g // 2) + g % 2 + 7, 2)
            return slice(4 * g, 4 * g + 4)

        def q3(b):
            return qT[:, b % 3 // 2, b % 3 % 2 * 4:b % 3 % 2 * 4 + 4, :]

        def v_view(s, b):
            return {"wide": V[:, b % 2, :].rearrange("p (h e) -> p h e", e=65), "narrow": V9[:, b % 3, :, :],
                    "rope": V33[:, b % 3, :, :]}[SPEC[s]["kind"]]

        def tensor_attention(pe, s):
            pe.wait_ge(const_cast, 2)
            sp = SPEC[s]
            kind, kvT = sp["kind"], src_of[sp["kv"]](s)
            xT = xT_of[s]
            pe.wait_ge(loaded[s], 16)
            pe.wait_ge(ctx_loaded, 32)
            for step, b, g in attention_steps(s):
                if step == "project" and kind == "wide":
                    xT_wait(pe, s, b)
                    for ring, what, wt, src in ((ring_act, "q", sp["wq"], xT), (ring_dve, "k", sp["wk"], kvT)):
                        for i in range(2):
                            bank = ring.open(pe, (what, s, b, i))
                            for c in range(4):
                                last = nc.tensor.matmul(bank[:, c * S:(c + 1) * S],
                                                        w[wt][:, (4 * i + c) * P:(4 * i + c + 1) * P], src[:, b, :],
                                                        start=True, stop=True)
                            last.then_inc(ring.filled, 1)
                    for i in range(2):
                        bank = ring_act.open(pe, ("v", s, b, i))
                        nc.tensor.matmul(bank, kvT[:, b, :], w[sp["wv"]][:, i * 512:(i + 1) * 512], start=True,
                                         stop=True).then_inc(ring_act.filled, 1)
                elif step == "project" and kind == "narrow":
                    xT_wait(pe, s, b)
                    bank = ring_act.open(pe, ("qkv", s, b))
                    nc.tensor.matmul(bank[:, 0:S], w[sp["wq"]], xT[:, b, :], start=True, stop=True)
                    nc.tensor.matmul(bank[:, S:2 * S], w[sp["wk"]], kvT[:, b, :], start=True, stop=True)
                    last = nc.tensor.matmul(bank[:, 2 * S:3 * S], kvT[:, b, :], w[sp["wv"]], start=True,
                                            stop=not sp.get("bias"))
                    if sp.get("bias"):
                        last = nc.tensor.matmul(bank[:, 2 * S:3 * S], w["ones"][0:1, :], w["x2_bv"], start=False,
                                                stop=True)
                    last.then_inc(ring_act.filled, 1)
                elif step == "project":
                    xT_wait(pe, s, b)
                    for what, wt in (("q", "a2_wq4"), ("k", "a2_wk4")):
                        bank = ring_dve.open(pe, (what, s, b))
                        for c in range(4):
                            last = nc.tensor.matmul(bank[:, c * S:(c + 1) * S], w[wt][:, c * P:(c + 1) * P],
                                                    xT[:, b, :], start=True, stop=True)
                        last.then_inc(ring_dve.filled, 1)
                    bank = ring_dve.open(pe, ("vg", s, b))
                    nc.tensor.matmul(bank[:, 0:320], xT[:, b, :], w["a2_wvg"], start=True, stop=True).then_inc(
                        ring_dve.filled, 1)
                elif step == "score":
                    if g == 0:
                        if kind == "wide":
                            pe.wait_ge(ring_act.emptied, ring_act.nth(("v", s, b, 1)))
                            pe.wait_ge(ring_dve.emptied, ring_dve.nth(("k", s, b, 1)))
                        else:
                            if kind == "narrow":
                                pe.wait_ge(ring_act.emptied, ring_act.nth(("qkv", s, b)))
                            else:
                                pe.wait_ge(ring_dve.emptied, ring_dve.nth(("vg", s, b)))
                            pe.wait_ge(*k_masked.at((s, b)))
                    bank = ring_score.open(pe, ("S", s, b, g))
                    open_ = True
                    if sp["causal"]:
                        nc.tensor.matmul(bank, w["ident_bf"], spread(w["causal_bf"], 4), start=True, stop=False)
                        open_ = False
                    if sp.get("masked"):
                        if b == 0 and g == 0:
                            pe.wait_ge(mask_ready, 1)
                        nc.tensor.matmul(bank, w["ones_bf"][32 * g:32 * g + 3, :],
                                         spread(maskrow[32 * g:32 * g + 3, b, :], 4), start=True, stop=False)
                        open_ = False
                    if kind == "wide":
                        i, p = g // 2, g % 2
                        for c in range(4):
                            last = nc.tensor.matmul(bank[:, c * S:(c + 1) * S], qT[64 * p:64 * p + 64, b % 2, 4 * i + c, :],
                                                    kT[64 * p:64 * p + 64, b % 2, 4 * i + c, :], start=open_,
                                                    stop=open_ or c == 3)
                    elif kind == "narrow":
                        last = nc.tensor.matmul(bank, q3(b)[32 * g:32 * g + 32, 0, :],
                                                kmask[32 * g:32 * g + 32, b % 3, 0, :, :], start=open_, stop=True)
                    else:
                        last = nc.tensor.matmul(bank, q3(b)[:, g, :], kmask[:, b % 3, g, :, :], start=True, stop=True)
                    last.then_inc(ring_score.filled, 1)
                elif step == "transpose":
                    bank = ring_prob.open(pe, ("T", s, b, g))
                    pe.wait_ge(*exped.at((s, b, g)))
                    n = units.index((s, b, g)) % 4
                    for c in range(4):
                        last = nc.tensor.transpose(bank[:, c * S:(c + 1) * S], prob[:, n, c, :], w["ident"])
                    last.then_inc(ring_prob.filled, 1)
                elif step == "value":
                    bank = ring_dve.open(pe, ("AV", s, b, g))
                    pe.wait_ge(ring_prob.emptied, ring_prob.nth(("T", s, b, g)))
                    n = units.index((s, b, g)) % 2
                    e = sp["dh"] + 1
                    hs = heads_of(s, g)
                    for c in range(4):
                        h = g if kind == "rope" else hs.start + (hs.step or 1) * c
                        last = nc.tensor.matmul(bank[:, c * e:(c + 1) * e], probT[:, n, c, :],
                                                v_view(s, b)[:, h, :], start=True, stop=True)
                    last.then_inc(ring_dve.filled, 1)
                elif step == "outT":
                    chunks = {"wide": 8, "rope": 2, "narrow": 1}[kind]
                    pe.wait_ge(ring_dve.emptied, ring_dve.nth(("AV", s, b, UNITS[s] - 1)))
                    for i in range(0, chunks, 4):
                        bank = ring_act.open(pe, ("OT", s, b, i))
                        for c in range(i, min(i + 4, chunks)):
                            last = nc.tensor.transpose(bank[:, (c - i) * S:(c - i + 1) * S],
                                                       O[:, b % 2, c * P:(c + 1) * P], w["ident"])
                        last.then_inc(ring_act.filled, 1)
                elif step == "out":
                    chunks = {"wide": 8, "rope": 2, "narrow": 1}[kind]
                    wo = {"rope": "a2_wo"}.get(kind) or sp["wo"]
                    bank = ring_dve.open(pe, ("out", s, b))
                    bias = {"l0x": "x0_bout", "l2x": "x2_bo"}.get(s)
                    pe.wait_ge(ring_act.emptied, ring_act.nth(("OT", s, b, 4 * ((chunks - 1) // 4))))
                    for c in range(chunks):
                        last = nc.tensor.matmul(bank[:, 0:D], OT[:, b % 2, c, :], w[wo][:, c * D:(c + 1) * D],
                                                start=(c == 0), stop=(c == chunks - 1) and not bias)
                    if bias:
                        last = nc.tensor.matmul(bank[:, 0:D], w["ones"][0:1, :], w[bias], start=False, stop=True)
                    last.then_inc(ring_dve.filled, 1)
                elif step == "norm" and next_of(s):
                    ln_transpose(pe, next_of(s), (b,))

        def scalar_attention(act, s):
            sp = SPEC[s]
            kind = sp["kind"]
            act.wait_ge(loaded[s], 16)
            if s == "l0x":
                nc.scalar.activation(tgate[:, :], w["x0_gate"], ACT.Tanh).then_inc(gate_l0x, 1)
            for step, b, g in attention_steps(s):
                if step == "project" and kind == "wide":
                    for i in range(2):
                        bank = ring_act.take(act, ("q", s, b, i))
                        nc.scalar.activation(qT[:, b % 2, 4 * i:4 * i + 4, :], bank.rearrange("p (c t) -> p c t", t=S),
                                             ACT.Copy).then_inc(ring_act.emptied, 1)
                    for i in range(2):
                        bank = ring_act.take(act, ("v", s, b, i))
                        nc.scalar.activation(v_view(s, b)[:, 8 * i:8 * i + 8, 0:64],
                                             bank.rearrange("p (h e) -> p h e", e=64), ACT.Copy
                                             ).then_inc(ring_act.emptied, 1)
                elif step == "project" and kind == "narrow":
                    bank = ring_act.take(act, ("qkv", s, b))
                    if sp.get("bias"):
                        nc.scalar.activation(kraw[:, b % 3, 0, :], bank[:, S:2 * S], ACT.Identity, bias=w["x2_bk"])
                        nc.scalar.activation(q3(b)[:, 0, :], bank[:, 0:S], ACT.Identity, bias=w["x2_bq"])
                    else:
                        nc.scalar.activation(kraw[:, b % 3, 0, :], bank[:, S:2 * S], ACT.Copy)
                        nc.scalar.activation(q3(b)[:, 0, :], bank[:, 0:S], ACT.Copy, scale=sp.get("qscale", 1.0))
                    nc.scalar.activation(v_view(s, b)[:, :, 0:8], bank[:, 2 * S:3 * S].rearrange("p (h e) -> p h e", e=8),
                                         ACT.Copy).then_inc(ring_act.emptied, 1)
                elif step == "project":
                    act.wait_ge(ring_dve.filled, ring_dve.nth(("vg", s, b)))
                    bank = ring_dve.bank(("vg", s, b))
                    nc.scalar.activation(v_view(s, b)[:, :, 0:32], bank[:, 0:64].rearrange("p (h e) -> p h e", e=32),
                                         ACT.Copy)
                    nc.scalar.activation(gate2[:, b % 3, :], bank[:, 64:320], ACT.Tanh, scale=0.5).then_inc(act_side, 1)
                elif step == "score":
                    n = units.index((s, b, g)) % 4
                    act.wait_ge(ring_score.emptied, ring_score.nth(("S", s, b, g)))
                    nc.scalar.activation(prob[:, n, :, :], prob[:, n, :, :], ACT.Exp, scale=sp["scale"]
                                         ).then_inc(*exped.inc((s, b, g)))
                elif step == "transpose":
                    bank = ring_prob.take(act, ("T", s, b, g))
                    n = units.index((s, b, g)) % 2
                    nc.scalar.activation(probT[:, n, :, :], bank.rearrange("p (c t) -> p c t", t=S), ACT.Copy
                                         ).then_inc(ring_prob.emptied, 1)
                elif step == "outT":
                    chunks = {"wide": 8, "rope": 2, "narrow": 1}[kind]
                    for i in range(0, chunks, 4):
                        m = min(4, chunks - i)
                        bank = ring_act.take(act, ("OT", s, b, i))
                        nc.scalar.activation(OT[:, b % 2, i:i + m, :],
                                             bank[:, 0:m * S].rearrange("p (c t) -> p c t", t=S), ACT.Copy
                                             ).then_inc(ring_act.emptied, 1)
                elif step == "norm" and next_of(s):
                    ln_copy(act, next_of(s), (b,))

        def vector_attention(dve, s):
            dve.wait_ge(const_cast, 2)
            sp = SPEC[s]
            kind = sp["kind"]
            dve.wait_ge(pool_ready, 1)
            if sp.get("masked"):
                dve.wait_ge(mask_loaded, 16)
                link(dve, nc.vector.tensor_scalar(mask01, mask_i[:, :, :], 0, None, ALU.not_equal))
                nc.vector.tensor_scalar(maskrow[:, :, :], mask01, 1.0, w["bigparts"], ALU.subtract,
                                        ALU.mult).then_inc(mask_ready, 1)
                dve.wait_ge(mask_ready, 1)
            if s == "l0x":
                dve.wait_ge(gate_l0x, 1)
            for step, b, g in attention_steps(s):
                if step == "project" and kind == "wide":
                    for i in range(2):
                        bank = ring_dve.take(dve, ("k", s, b, i))
                        nc.vector.tensor_copy(kT[:, b % 2, 4 * i:4 * i + 4, :], bank.rearrange("p (c t) -> p c t", t=S)
                                              ).then_inc(ring_dve.emptied, 1)
                        dve.wait_ge(ring_dve.emptied, ring_dve.taken)
                elif step == "project" and kind == "rope":
                    for j, what in enumerate(("q", "k")):
                        bank = ring_dve.take(dve, (what, s, b)).rearrange("p (c t) -> p c t", t=S)
                        if j == 0 and b >= 2:
                            dve.wait_ge(*k_masked.at((s, b - 2)))
                        link(dve, nc.vector.tensor_tensor(rope1[:, b % 2, 2 * j:2 * j + 2, :], bank[:, 0:2, :],
                                                spread(w["cos"], 2), ALU.mult))
                        nc.vector.tensor_tensor(rope2[:, b % 2, 2 * j:2 * j + 2, :], bank[:, 2:4, :],
                                                spread(w["sin"], 2), ALU.mult).then_inc(ring_dve.emptied, 1)
                        dve.wait_ge(ring_dve.emptied, ring_dve.taken)
                    dve.wait_ge(ring_dve.emptied, ring_dve.nth(("k", s, b)))
                    bank = ring_dve.take(dve, ("vg", s, b))
                    dve.wait_ge(act_side, b + 1)
                    nc.vector.scalar_tensor_tensor(out=gate2[:, b % 3, :], in0=gate2[:, b % 3, :], scalar=1.0,
                                                   in1=bank[:, 64:320], op0=ALU.add, op1=ALU.mult
                                                   ).then_inc(ring_dve.emptied, 1)
                    dve.wait_ge(ring_dve.emptied, ring_dve.taken)
                elif step == "score":
                    bank = ring_score.take(dve, ("S", s, b, g)).rearrange("p (c t) -> p c t", t=S)
                    n = units.index((s, b, g)) % 4
                    link(dve, nc.vector.tensor_reduce(nmax[:, n, :], bank, AX.X, ALU.max))
                    u = units.index((s, b, g))
                    if u >= 4:
                        dve.wait_ge(ring_prob.filled, ring_prob.nth(("T",) + units[u - 4]))
                    nc.vector.tensor_tensor(prob[:, n, :, :], bank, spread(nmax[:, n, :], S, 2), ALU.subtract
                                            ).then_inc(ring_score.emptied, 1)
                    dve.wait_ge(ring_score.emptied, ring_score.taken)
                elif step == "value":
                    e = sp["dh"] + 1
                    bank = ring_dve.take(dve, ("AV", s, b, g))[:, 0:4 * e].rearrange("p (c e) -> p c e", e=e)
                    link(dve, nc.vector.reciprocal(rden, bank[:, :, e - 1:e].rearrange("p c e -> p (c e)")))
                    o = O[:, b % 2, 0:{"wide": 1024, "rope": 256, "narrow": 128}[kind]].rearrange(
                        "p (h e) -> p h e", e=e - 1)[:, heads_of(s, g), :]
                    ins = nc.vector.tensor_tensor(o, bank[:, :, 0:e - 1], spread(rden, e - 1, 2), ALU.mult)
                    if kind == "rope":
                        link(dve, ins)
                        if g == 0:
                            dve.wait_ge(ring_dve.emptied, ring_dve.nth(("vg", s, b)))
                        ins = nc.vector.tensor_tensor(
                            o, o, gate2[:, b % 3, :].rearrange("p (h e) -> p h e", e=32)[:, heads_of(s, g), :], ALU.mult)
                    ins.then_inc(ring_dve.emptied, 1)
                    dve.wait_ge(ring_dve.emptied, ring_dve.taken)
                elif step == "out":
                    bank = ring_dve.take(dve, ("out", s, b))
                    scalar = tgate[:, :] if s == "l0x" else float(sp["alpha"])
                    ins = nc.vector.scalar_tensor_tensor(out=x[:, b, :], in0=bank[:, 0:D], scalar=scalar,
                                                         in1=x[:, b, :], op0=ALU.mult, op1=ALU.add)
                    ins.then_inc(ring_dve.emptied, 1)
                    dve.wait_ge(ring_dve.emptied, ring_dve.nth(("out", s, b)))
                    if next_of(s):
                        ln_stats(dve, next_of(s), b)
                elif step == "norm" and next_of(s):
                    ln_xhat(dve, next_of(s), b)

        def gpsimd_attention(pool, s):
            sp = SPEC[s]
            kind = sp["kind"]
            for step, b, g in attention_steps(s):
                if step == "project" and kind == "narrow":
                    pool.wait_ge(ring_act.emptied, ring_act.nth(("qkv", s, b)))
                    k = kraw[:, b % 3, 0, :]
                    if sp.get("masked"):
                        if b == 0:
                            pool.wait_ge(mask_ready, 1)
                        plink(pool, nc.gpsimd.tensor_tensor(k, k, mask01[:, b, :], ALU.mult))
                    nc.gpsimd.tensor_tensor(kmask[:, b % 3, 0, :, :], spread(k, 4), spread(w["mask8"], S, 2),
                                            ALU.mult).then_inc(*k_masked.inc((s, b)))
                    pool.wait_ge(*k_masked.at((s, b)))
                elif step == "project" and kind == "rope":
                    pool.wait_ge(ring_dve.emptied, ring_dve.nth(("k", s, b)))
                    plink(pool, nc.gpsimd.tensor_tensor(q3(b)[:, 0:2, :], rope1[:, b % 2, 0:2, :], rope2[:, b % 2, 0:2, :], ALU.add))
                    plink(pool, nc.gpsimd.tensor_tensor(kraw[:, b % 3, :, :], rope1[:, b % 2, 2:4, :],
                                                        rope2[:, b % 2, 2:4, :], ALU.add))
                    plink(pool, nc.gpsimd.tensor_tensor(kmask[:, b % 3, 0, :, :], spread(kraw[:, b % 3, 0, :], 4),
                                            spread(w["mask32"], S, 2), ALU.mult))
                    nc.gpsimd.tensor_tensor(kmask[:, b % 3, 1, :, :], spread(kraw[:, b % 3, 1, :], 4),
                                            spread(w["mask32"], S, 2), ALU.mult).then_inc(*k_masked.inc((s, b)))
                    pool.wait_ge(*k_masked.at((s, b)))
                elif step == "out" and next_of(s):
                    ln_rstd(pool, next_of(s), b)

        xr = big[0][:, 0, :, 0:S]
        xk = big[0][:, 1, :, 0:S]
        xd = big[1][:, 0, :, 0:S]
        kact = big[1][:, 1, :, 0:S]
        rgate = O[:, 0, :].rearrange("p (b d) -> p b d", d=D)

        def tensor_l0f(pe):
            pe.wait_ge(loaded["l0f"], 16)
            for n in range(2):
                pe.wait_ge(*l0f_mix.at((n,)))
                bank = ring_dve.open(pe, ("k", "l0f", n))
                nc.tensor.matmul(bank, w["f0_wk"], xk[:, 4 * n:4 * n + 4, :], start=True, stop=True).then_inc(
                    ring_dve.filled, 1)
                bank = ring_act.open(pe, ("r", n))
                for i in range(4):
                    last = nc.tensor.matmul(bank[:, i * D:(i + 1) * D], xr[:, 4 * n + i, :], w["f0_wr"], start=True,
                                            stop=True)
                last.then_inc(ring_act.filled, 1)
            for n in range(2):
                bank = ring_dve.open(pe, ("out", "l0f", n))
                pe.wait_ge(ring_dve.emptied, ring_dve.nth(("k", "l0f", n)))
                for i in range(4):
                    last = nc.tensor.matmul(bank[:, i * D:(i + 1) * D], kact[:, 4 * n + i, :], w["f0_wv"], start=True,
                                            stop=True)
                last.then_inc(ring_dve.filled, 1)
            finish_pe(pe, "l0f")

        def scalar_l0f(act):
            for n in range(2):
                bank = ring_act.take(act, ("r", n))
                nc.scalar.activation(rgate[:, 4 * n:4 * n + 4, :], bank.rearrange("p (b t) -> p b t", t=S), ACT.Tanh,
                                     scale=0.5).then_inc(ring_act.emptied, 1)
            finish_act(act, "l0f")

        def vector_l0f(dve):
            dve.wait_ge(loaded["l0f"], 16)
            for n in range(2):
                dve.wait_ge(ring_act.emptied, xT_use("l0f", 4 * n + 3))
                now, prev = xpad[:, 4 * n:4 * n + 4, 1:S + 1], xpad[:, 4 * n:4 * n + 4, 0:S]
                d = xd[:, 4 * n:4 * n + 4, :]
                link(dve, nc.vector.tensor_tensor(d, now, prev, ALU.subtract))
                link(dve, nc.vector.scalar_tensor_tensor(out=xk[:, 4 * n:4 * n + 4, :], in0=d, scalar=w["f0_muk"], in1=prev,
                                               op0=ALU.mult, op1=ALU.add))
                nc.vector.scalar_tensor_tensor(out=xr[:, 4 * n:4 * n + 4, :], in0=d, scalar=w["f0_mur"], in1=prev,
                                               op0=ALU.mult, op1=ALU.add).then_inc(*l0f_mix.inc((n,)))
                dve.wait_ge(*l0f_mix.at((n,)))
            for n in range(2):
                bank = ring_dve.take(dve, ("k", "l0f", n))
                kk = kact[:, 4 * n:4 * n + 4, :]
                link(dve, nc.vector.tensor_scalar(kk, bank.rearrange("p (b t) -> p b t", t=S), 0.0, None, ALU.max))
                nc.vector.tensor_tensor(kk, kk, kk, ALU.mult).then_inc(ring_dve.emptied, 1)
                dve.wait_ge(ring_dve.emptied, ring_dve.taken)
            for n in range(2):
                bank = ring_dve.take(dve, ("out", "l0f", n))
                dve.wait_ge(ring_act.emptied, ring_act.nth(("r", n)))
                r = rgate[:, 4 * n:4 * n + 4, :]
                xs = x[:, 4 * n:4 * n + 4, :]
                link(dve, nc.vector.scalar_tensor_tensor(out=r, in0=r, scalar=1.0,
                                                         in1=bank.rearrange("p (b t) -> p b t", t=S), op0=ALU.add,
                                                         op1=ALU.mult))
                nc.vector.scalar_tensor_tensor(out=xs, in0=r, scalar=0.5, in1=xs, op0=ALU.mult, op1=ALU.add
                                               ).then_inc(ring_dve.emptied, 1)
                dve.wait_ge(ring_dve.emptied, ring_dve.nth(("out", "l0f", n)))
                finish_dve(dve, "l0f", n)

        def gpsimd_l0f(pool):
            finish_pool(pool, "l0f")

        rows = [t[0:8, i, :] for t in (O,) for i in range(2)]
        rows += [t[0:8, i, :, :].rearrange("p c s -> p (c s)") for t in (qT, kT) for i in range(2)]
        rF, rI, rA, rCS, rG, rM = rows
        qm = [big[0][:, i, :, 0:S] for i in range(2)]
        DC = [big[1][:, i, :, 0:S] for i in range(2)]
        hbuf = OT[:, 0, 0:2, :]

        def lstm_steps():
            for t in range(B + 4):
                if t < B:
                    yield "weights", t
                if 0 <= t - 1 < B:
                    yield "value", t - 1
                if 0 <= t - 2 < B:
                    yield "add", t - 2
                if 0 <= t - 3 < B:
                    yield "norm", t - 3

        def tensor_l1x(pe):
            pe.wait_ge(loaded["l1x"], 16)
            pe.wait_ge(rowconst_loaded, 16)
            for b in range(B):
                xT_wait(pe, "l1x", b)
            for gate in ("f", "i"):
                for n in range(2):
                    bank = ring_dve.open(pe, (gate, "l1x", n))
                    for c, src in enumerate((xT_of["l1x"], ctxT, ctxT)):
                        last = nc.tensor.matmul(bank[0:8, :], w[f"x1_w{gate}"][:, 8 * c:8 * c + 8],
                                                src[:, 4 * n:4 * n + 4, :], start=(c == 0), stop=(c == 2))
                    last.then_inc(ring_dve.filled, 1)
            for step, b in lstm_steps():
                if step == "weights":
                    pe.wait_ge(*lstm_q.at((b,)))
                    for i in range(2):
                        bank = ring_score.open(pe, ("qk", b, i))
                        nc.tensor.matmul(bank, ctxT[:, b, :], qm[b % 2][:, 4 * i:4 * i + 4, :], start=True, stop=True
                                         ).then_inc(ring_score.filled, 1)
                    if b == 0:
                        pe.wait_ge(lstm_f, 3)
                    for i in range(2):
                        bank = ring_act.open(pe, ("arg", b, i))
                        nc.tensor.matmul(bank, w["ident_bf"], spread(w["causalT_bf"], 4), start=True, stop=False)
                        nc.tensor.matmul(bank, rG[:, b * S:(b + 1) * S], bdones[:, 512 * i:512 * i + 512],
                                         start=False, stop=False)
                        for c in range(4):
                            h = 4 * i + c
                            last = nc.tensor.matmul(bank[:, c * S:(c + 1) * S], bdones[:, h * S:(h + 1) * S],
                                                    rM[:, b * S:(b + 1) * S], start=False, stop=(c == 3))
                        last.then_inc(ring_act.filled, 1)
                elif step == "value":
                    bank = ring_dve.open(pe, ("h", b))
                    pe.wait_ge(*lstm_C.at((b,)))
                    if b == 0:
                        pe.wait_ge(v_ready, 1)
                        pe.wait_ge(lstm_e, 2)
                    for h in range(8):
                        nc.tensor.matmul(bank[:, 17 * h:17 * h + 17], DC[b % 2][:, h, :], V17[:, b, h, :], start=True,
                                         stop=True)
                    nc.tensor.transpose(bank[:, 136:144], rA[:, b * S:(b + 1) * S], w["ident"][0:8, 0:8]).then_inc(
                        ring_dve.filled, 1)
                elif step == "norm" and next_of("l1x"):
                    ln_transpose(pe, next_of("l1x"), (b,))

        def scalar_l1x(act):
            act.wait_ge(lstm_f, 1)
            alink(act, nc.scalar.activation(rA, rA, ACT.Exp, scale=-1.0))
            nc.scalar.activation(rA, rA, ACT.Ln, bias=1.0).then_inc(lstm_e, 1)
            act.wait_ge(lstm_f, 2)
            nc.scalar.activation(rA, rA, ACT.Exp, scale=-1.0).then_inc(lstm_e, 1)
            for step, b in lstm_steps():
                if step == "weights":
                    for i in range(2):
                        bank = ring_act.take(act, ("arg", b, i))
                        if b >= 2:
                            act.wait_ge(ring_dve.filled, ring_dve.nth(("h", b - 2)))
                        nc.scalar.activation(DC[b % 2][:, 4 * i:4 * i + 4, :], bank.rearrange("p (c t) -> p c t", t=S),
                                             ACT.Exp).then_inc(ring_act.emptied, 1)
                elif step == "norm" and next_of("l1x"):
                    ln_copy(act, next_of("l1x"), (b,))

        def vector_l1x(dve):
            dve.wait_ge(loaded["l1x"], 16)
            dve.wait_ge(rowconst_loaded, 16)
            for gate, row, bias in (("f", rF, "x1_bf"), ("i", rI, "x1_bi")):
                for n in range(2):
                    bank = ring_dve.take(dve, (gate, "l1x", n))
                    nc.vector.tensor_scalar(row[:, 512 * n:512 * n + 512], bank[0:8, :], w[bias], None, ALU.add
                                            ).then_inc(ring_dve.emptied, 1)
                    dve.wait_ge(ring_dve.emptied, ring_dve.taken)
            dve.wait_ge(ring_dve.emptied, ring_dve.nth(("i", "l1x", 1)))
            nc.vector.scalar_tensor_tensor(out=rA, in0=rF, scalar=-1.0, in1=rF, op0=ALU.mult, op1=ALU.max).then_inc(
                lstm_f, 1)
            dve.wait_ge(lstm_f, 1)
            link(dve, nc.vector.tensor_scalar(rF, rF, 0.0, None, ALU.min))
            dve.wait_ge(lstm_e, 1)
            link(dve, nc.vector.tensor_tensor(rF, rF, rA, ALU.subtract))
            link(dve, nc.vector.tensor_tensor_scan(rCS, notfirst, rF, 0.0, ALU.mult, ALU.add))
            link(dve, nc.vector.tensor_tensor(rG, rI, rCS, ALU.subtract))
            link(dve, nc.vector.tensor_tensor_scan(rM, negfirst, rG, NEG, ALU.add, ALU.max))
            nc.vector.tensor_tensor(rA, rCS, rM, ALU.add).then_inc(lstm_f, 1)
            dve.wait_ge(lstm_f, 2)
            nc.vector.tensor_scalar(rM, rM, -1.0, None, ALU.mult).then_inc(lstm_f, 1)
            dve.wait_ge(lstm_f, 3)
            for step, b in lstm_steps():
                if step == "weights":
                    for i in range(2):
                        bank = ring_score.take(dve, ("qk", b, i))
                        dve.wait_ge(ring_act.emptied, ring_act.nth(("arg", b, i)))
                        d = DC[b % 2][:, 4 * i:4 * i + 4, :]
                        nc.vector.tensor_tensor(d, bank.rearrange("p (c t) -> p c t", t=S), d, ALU.mult).then_inc(
                            ring_score.emptied, 1)
                        dve.wait_ge(ring_score.emptied, ring_score.taken)
                    dve.wait_ge(ring_score.emptied, ring_score.nth(("qk", b, 1)))
                    nc.vector.tensor_copy(rden[:, 0:1], rden[:, 0:1]).then_inc(*lstm_C.inc((b,)))
                    dve.wait_ge(*lstm_C.at((b,)))
                elif step == "value":
                    bank = ring_dve.take(dve, ("h", b))
                    hv = bank[:, 0:136].rearrange("p (h e) -> p h e", e=17)
                    den = small[:, 0:8]
                    link(dve, nc.vector.tensor_copy(den, hv[:, :, 16:17].rearrange("p h e -> p (h e)")))
                    link(dve, nc.vector.scalar_tensor_tensor(out=den, in0=den, scalar=-1.0, in1=den, op0=ALU.mult,
                                                             op1=ALU.max))
                    link(dve, nc.vector.tensor_tensor(den, den, bank[:, 136:144], ALU.max))
                    link(dve, nc.vector.tensor_scalar(den, den, 1e-6, None, ALU.add))
                    link(dve, nc.vector.reciprocal(den, den))
                    nc.vector.tensor_tensor(hbuf[:, b % 2, :].rearrange("p (h e) -> p h e", e=16), hv[:, :, 0:16],
                                            spread(den, 16, 2), ALU.mult).then_inc(ring_dve.emptied, 1)
                    dve.wait_ge(ring_dve.emptied, ring_dve.nth(("h", b)))
                    link(dve, nc.vector.bn_stats(stats[:, b, :], hbuf[:, b % 2, :]))
                    nc.vector.bn_aggr(mv[:, b, :], stats[:, b, :]).then_inc(*lstm_var.inc((b,)))
                    dve.wait_ge(*lstm_var.at((b,)))
                elif step == "add":
                    dve.wait_ge(*lstm_rstd.at((b,)))
                    h = hbuf[:, b % 2, :]
                    link(dve, nc.vector.tensor_scalar(h, h, mv[:, b, 0:1], rstd[:, b, :], ALU.subtract, ALU.mult))
                    link(dve, nc.vector.tensor_tensor(h, h, w["x1_lnscale"], ALU.mult))
                    link(dve, nc.vector.tensor_tensor(x[:, b, :], x[:, b, :], h, ALU.add))
                    if next_of("l1x"):
                        ln_stats(dve, next_of("l1x"), b)
                elif step == "norm" and next_of("l1x"):
                    ln_xhat(dve, next_of("l1x"), b)

        def gpsimd_l1x(pool):
            pool.wait_ge(ctx_loaded, 32)
            pool.wait_ge(ring_dve.emptied, ring_dve.nth(("out", "l1a", B - 1)))
            plink(pool, nc.gpsimd.memset(V17, 1.0))
            for b in range(B):
                ins = nc.gpsimd.tensor_copy(V17[:, b, :, 0:16], ctx[:, b, :].rearrange("p (h e) -> p h e", e=16))
            ins.then_inc(v_ready, 1)
            pool.wait_ge(v_ready, 1)
            for step, b in lstm_steps():
                if step == "weights":
                    pool.wait_ge(ring_act.emptied, xT_use("l1x", b))
                    if b >= 2:
                        pool.wait_ge(ring_score.filled, ring_score.nth(("qk", b - 2, 1)))
                    nc.gpsimd.tensor_tensor(qm[b % 2], spread(xT_of["l1x"][:, b, :], 8), spread(w["mask16"], S, 2),
                                            ALU.mult).then_inc(*lstm_q.inc((b,)))
                    pool.wait_ge(*lstm_q.at((b,)))
                elif step == "value":
                    pool.wait_ge(*lstm_var.at((b,)))
                    plink(pool, nc.gpsimd.tensor_scalar(veps[:, b, :], mv[:, b, 1:2], 1e-5, None, ALU.add))
                    nc.gpsimd.tensor_tensor(rstd[:, b, :], veps[:, b, :], power[:, 0:1], ALU.pow).then_inc(
                        *lstm_rstd.inc((b,)))
                    pool.wait_ge(*lstm_rstd.at((b,)))
                elif step == "add" and next_of("l1x"):
                    ln_rstd(pool, next_of("l1x"), b)

        VT = qT[:, 0, :, :]
        fth = kT[:, 0, 0:4, :].rearrange("p c s -> p (c s)")
        fu = [kT[:, 1, 4 * i:4 * i + 4, :].rearrange("p c s -> p (c s)") for i in range(2)]
        fh = big[0][:, :, :, 0:S]
        wT8 = O[0:8, 0, :]
        RC = sb("RC", [P, 2, B, 8])
        RQ = sb("RQ", [P, 2, B, 8])
        pvs = sb("pvs", [P, 4, 64])
        rm = sb("rm", [P, 2, B])
        mx = sb("mx", [P, B, 8])
        mi = sb("mi", [P, B, 8], U32)
        mif = sb("mif", [P, B, 2])
        sca = sb("sca", [P, B, 4])
        sigma = sb("sigma", [P, 2])
        hb = sb("hb", [P, 32])

        def tensor_l1f(pe):
            pe.wait_ge(loaded["l1f"], 16)
            for n in range(2):
                for b in halves[n]:
                    xT_wait(pe, "l1f", b)
                bank = ring_act.open(pe, ("VT", n))
                nc.tensor.matmul(bank, w["f1_wv"], xT_of["l1f"][:, 4 * n:4 * n + 4, :], start=True, stop=True
                                 ).then_inc(ring_act.filled, 1)
            for n in range(2):
                bank = ring_dve.open(pe, ("router", "l1f", n))
                pe.wait_ge(ring_act.emptied, ring_act.nth(("VT", n)))
                for i in range(4):
                    last = nc.tensor.matmul(bank[:, 72 * i:72 * i + 72], VT[:, 4 * n + i, :], w["f1_wgp"], start=True,
                                            stop=True)
                last.then_inc(ring_dve.filled, 1)
            for n in range(2):
                for c in range(2):
                    bank = ring_act.open(pe, ("h1", c, n))
                    nc.tensor.matmul(bank, w["f1_w1"][:, c * P:(c + 1) * P], VT[:, 4 * n:4 * n + 4, :], start=True,
                                     stop=True).then_inc(ring_act.filled, 1)
            pe.wait_ge(*l1f_w.at((0,)))
            for n in range(2):
                bank = ring_act.open(pe, ("wT", "l1f", n))
                for i in range(4):
                    last = nc.tensor.transpose(bank[0:8, i * S:(i + 1) * S], wcol[:, 4 * n + i, 0:8], w["ident"])
                last.then_inc(ring_act.filled, 1)
            for n in range(2):
                pe.wait_ge(ring_act.emptied, ring_act.nth(("wT", "l1f", n)))
                for c in range(2):
                    bank = ring_score.open(pe, ("wexp", c, n))
                    nc.tensor.matmul(bank, w["sel8"][:, c * P:(c + 1) * P], wT8[:, 512 * n:512 * n + 512], start=True,
                                     stop=True).then_inc(ring_score.filled, 1)
            for n in range(2):
                bank = ring_dve.open(pe, ("out", "l1f", n))
                nc.tensor.matmul(bank, w["ones"][0:1, :], spread(w["f1_bvr"], 4), start=True, stop=False)
                for c in range(2):
                    pe.wait_ge(*l1f_h.at((c, n)))
                for i in range(4):
                    b = 4 * n + i
                    o = bank[:, i * D:(i + 1) * D]
                    nc.tensor.matmul(o, xT_of["l1f"][:, b, :], w["f1_wv"], start=False, stop=False)
                    nc.tensor.matmul(o, wT8[:, b * S:(b + 1) * S], w["f1_b2"], start=False, stop=False)
                    for c in range(2):
                        last = nc.tensor.matmul(o, fh[:, c, b, :], w["f1_w2"][:, c * D:(c + 1) * D], start=False,
                                                stop=(i == 3 and c == 1))
                last.then_inc(ring_dve.filled, 1)
            finish_pe(pe, "l1f")

        l1f_w = events(sem("l1f_weights"), [(0,)])
        l1f_h = events(sem("l1f_hidden"), [(c, n) for n in range(2) for c in range(2)])
        l1f_u = events(sem("l1f_silu"), [(c, n) for n in range(2) for c in range(2)])
        l1f_d = sem("l1f_dve")
        l1f_p = sem("l1f_pool")
        l1f_a = sem("l1f_act")

        def scalar_l1f(act):
            act.wait_ge(loaded["l1f"], 16)
            for n in range(2):
                bank = ring_act.take(act, ("VT", n))
                nc.scalar.activation(VT[:, 4 * n:4 * n + 4, :], bank.rearrange("p (b t) -> p b t", t=S), ACT.Identity,
                                     bias=w["f1_bvc"]).then_inc(ring_act.emptied, 1)
            nc.scalar.activation(sigma[:, 0:1], w["f1_alpha"], ACT.Exp, scale=-1.0).then_inc(l1f_a, 1)
            act.wait_ge(l1f_d, 1)
            for n in range(2):
                for c in range(2):
                    bank = ring_act.take(act, ("h1", c, n))
                    if (c, n) != (0, 0):
                        act.wait_ge(*l1f_u.at((1 - c, n if c else n - 1)))
                    nc.scalar.activation(fth, bank, ACT.Tanh, scale=0.5, bias=hb[:, c:c + 1])
                    nc.scalar.activation(fu[c], bank, ACT.Identity, bias=w["f1_b1"][:, c:c + 1]).then_inc(
                        ring_act.emptied, 1)
            act.wait_ge(l1f_d, 3)
            nc.scalar.activation(sca[:, :, 1], sca[:, :, 0], ACT.Exp).then_inc(l1f_a, 1)
            for n in range(2):
                bank = ring_act.take(act, ("wT", "l1f", n))
                nc.scalar.activation(wT8[:, 512 * n:512 * n + 512], bank[0:8, :], ACT.Copy).then_inc(
                    ring_act.emptied, 1)
            finish_act(act, "l1f")

        def vector_l1f(dve):
            dve.wait_ge(loaded["l1f"], 16)
            nc.vector.tensor_scalar(hb[:, 0:2], w["f1_b1"], 0.5, None, ALU.mult).then_inc(l1f_d, 1)
            dve.wait_ge(l1f_d, 1)
            dve.wait_ge(l1f_a, 1)
            link(dve, nc.vector.tensor_scalar(sigma[:, 0:1], sigma[:, 0:1], 1.0, None, ALU.add))
            link(dve, nc.vector.reciprocal(sigma[:, 1:2], sigma[:, 0:1]))
            for n in range(2):
                bank = ring_dve.take(dve, ("router", "l1f", n))[:, 0:288].rearrange("p (b e) -> p b e", e=72)
                link(dve, nc.vector.tensor_tensor(RC[:, 0, 4 * n:4 * n + 4, :], bank[:, :, 0:8], spread(w["f1_bg"], 4), ALU.add))
                nc.vector.tensor_copy(pvs, bank[:, :, 8:72]).then_inc(ring_dve.emptied, 1)
                dve.wait_ge(ring_dve.emptied, ring_dve.nth(("router", "l1f", n)))
                link(dve, nc.vector.tensor_tensor(pvs, pvs, pvs, ALU.mult))
                link(dve, nc.vector.tensor_reduce(RQ[:, 1, 4 * n:4 * n + 4, :],
                                                  pvs.rearrange("p b (e k) -> p b e k", k=8), AX.X, ALU.add))
            nc.vector.tensor_scalar(RQ[:, 1, :, :], RQ[:, 1, :, :], 0.125, None, ALU.mult).then_inc(l1f_d, 1)
            dve.wait_ge(l1f_d, 2)
            for n in range(2):
                for c in range(2):
                    dve.wait_ge(ring_act.emptied, ring_act.nth(("h1", c, n)))
                    nc.vector.scalar_tensor_tensor(out=fh[:, c, 4 * n:4 * n + 4, :],
                                                   in0=fth.rearrange("p (b t) -> p b t", t=S), scalar=1.0,
                                                   in1=fu[c].rearrange("p (b t) -> p b t", t=S), op0=ALU.add,
                                                   op1=ALU.mult).then_inc(*l1f_u.inc((c, n)))
                    dve.wait_ge(*l1f_u.at((c, n)))
            dve.wait_ge(l1f_p, 1)
            rc = RC[:, :, :, :].rearrange("p a b e -> p (a b) e")
            rq = RQ[:, :, :, :].rearrange("p a b e -> p (a b) e")
            rms = rm[:, :, :].rearrange("p a b -> p (a b)")
            link(dve, nc.vector.tensor_reduce(rms, rc, AX.X, ALU.add))
            link(dve, nc.vector.tensor_scalar(rms, rms, 0.125, None, ALU.mult))
            link(dve, nc.vector.tensor_tensor(rc, rc, spread(rms, 8, 2), ALU.subtract))
            link(dve, nc.vector.tensor_tensor(rq, rc, rc, ALU.mult))
            link(dve, nc.vector.tensor_reduce(rms, rq, AX.X, ALU.add))
            nc.vector.tensor_scalar(rms, rms, 0.125, 1e-5, ALU.mult, ALU.add).then_inc(l1f_v, 1)
            dve.wait_ge(l1f_v, 1)
            dve.wait_ge(l1f_p, 2)
            link(dve, nc.vector.tensor_tensor(rc, rc, spread(rms, 8, 2), ALU.mult))
            for i, (gn, bn) in enumerate((("f1_gr", "f1_br"), ("f1_gc", "f1_bc"))):
                link(dve, nc.vector.tensor_tensor(RC[:, i, :, :], RC[:, i, :, :], spread(w[gn], B), ALU.mult))
                link(dve, nc.vector.tensor_tensor(RC[:, i, :, :], RC[:, i, :, :], spread(w[bn], B), ALU.add))
            link(dve, nc.vector.scalar_tensor_tensor(out=RC[:, 0, :, :], in0=RC[:, 1, :, :], scalar=sigma[:, 1:2],
                                                     in1=RC[:, 0, :, :], op0=ALU.mult, op1=ALU.add))
            for b in range(B):
                ins = nc.vector.max(mx[:, b, :], RC[:, 0, b, :])
            link(dve, ins)
            for b in range(B):
                ins = nc.vector.max_index(mi[:, b, :], mx[:, b, :], RC[:, 0, b, :])
            link(dve, ins)
            link(dve, nc.vector.tensor_copy(mif, mi[:, :, 0:2]))
            nc.vector.tensor_tensor(sca[:, :, 0], mx[:, :, 1], mx[:, :, 0], ALU.subtract).then_inc(l1f_d, 1)
            dve.wait_ge(l1f_d, 3)
            dve.wait_ge(l1f_a, 2)
            link(dve, nc.vector.tensor_scalar(sca[:, :, 2], sca[:, :, 1], 1.0, None, ALU.add))
            link(dve, nc.vector.reciprocal(sca[:, :, 2], sca[:, :, 2]))
            link(dve, nc.vector.tensor_tensor(sca[:, :, 3], sca[:, :, 1], sca[:, :, 2], ALU.mult))
            for i in range(2):
                link(dve, nc.vector.tensor_tensor(RQ[:, i, :, :], spread(w["iota8"], B), spread(mif[:, :, i], 8, 2),
                                                  ALU.is_equal))
                link(dve, nc.vector.tensor_tensor(RQ[:, i, :, :], RQ[:, i, :, :], spread(sca[:, :, 2 + i], 8, 2),
                                                  ALU.mult))
            nc.vector.tensor_tensor(wcol[:, :, 0:8], RQ[:, 0, :, :], RQ[:, 1, :, :], ALU.add).then_inc(
                *l1f_w.inc((0,)))
            dve.wait_ge(*l1f_w.at((0,)))
            for n in range(2):
                for c in range(2):
                    bank = ring_score.take(dve, ("wexp", c, n))
                    h = fh[:, c, 4 * n:4 * n + 4, :]
                    nc.vector.tensor_tensor(h, h, bank.rearrange("p (b t) -> p b t", t=S), ALU.mult).then_inc(
                        ring_score.emptied, 1)
                    dve.wait_ge(ring_score.emptied, ring_score.nth(("wexp", c, n)))
                    nc.vector.tensor_copy(rden[:, 0:1], rden[:, 0:1]).then_inc(*l1f_h.inc((c, n)))
                    dve.wait_ge(*l1f_h.at((c, n)))
            for n in range(2):
                bank = ring_dve.take(dve, ("out", "l1f", n))
                xs = x[:, 4 * n:4 * n + 4, :]
                nc.vector.tensor_tensor(xs, bank.rearrange("p (b d) -> p b d", d=D), xs, ALU.add).then_inc(
                    ring_dve.emptied, 1)
                dve.wait_ge(ring_dve.emptied, ring_dve.nth(("out", "l1f", n)))
                finish_dve(dve, "l1f", n)

        l1f_v = sem("l1f_variance")

        def gpsimd_l1f(pool):
            pool.wait_ge(l1f_d, 2)
            nc.gpsimd.tensor_tensor(RC[:, 1, :, :], RQ[:, 1, :, :],
                                    power[:, 1:2].unsqueeze(2).to_broadcast([P, B, 8]), ALU.pow).then_inc(l1f_p, 1)
            pool.wait_ge(l1f_p, 1)
            pool.wait_ge(l1f_v, 1)
            nc.gpsimd.tensor_tensor(rm[:, :, :], rm[:, :, :], power[:, 0:1].unsqueeze(2).to_broadcast([P, 2, B]),
                                    ALU.pow).then_inc(l1f_p, 1)
            pool.wait_ge(l1f_p, 2)
            finish_pool(pool, "l1f")

        aff = ctx[:, 0:2, :].rearrange("p a (b e) -> p (a b) e", e=32)
        rep = ctx[:, 2:4, :].rearrange("p a (b e) -> p (a b) e", e=32)
        whalf = sb("whalf", [P, B, 32], BF16)
        w96 = gate2.rearrange("p m (a e) -> p (m a) e", e=32).rearrange("p (b t) e -> p b (t e)", t=3)
        w96T = OT[0:96, 0, :, :]
        w3T = OT[0:96, 1, :, :].rearrange("p c s -> p (c s)").bitcast(BF16)[:, 0:TOK].rearrange("p (b t) -> p b t", t=S)
        f2_r = sem("f2_router")
        f2_a = sem("f2_router_act")
        f2_w = sem("f2_weights")
        f2_b = sem("f2_half_bias")
        NC2 = 17
        f2_seq = [(n, c) for n in range(2) for c in range(NC2)]
        f2_t = events(sem("f2_tanh"), f2_seq)
        f2_h = events(sem("f2_hidden"), f2_seq)
        hid = [kmask[:, i, :, :, :].rearrange("p a c s -> p (a c s)") for i in range(3)]

        def tensor_l2f(pe):
            pe.wait_ge(loaded["l2f"], 16)
            bank = ring_dve.open(pe, ("router", "l2f"))
            xT = xT_of["l2f"]
            for b in range(B):
                xT_wait(pe, "l2f", b)
                nc.tensor.matmul(bank[:, 32 * b:32 * b + 32], xT[:, b, :], w["f2_wr"], start=True, stop=False)
                last = nc.tensor.matmul(bank[:, 32 * b:32 * b + 32], w["ones"][0:1, :], w["f2_br"], start=False,
                                        stop=True)
            last.then_inc(ring_dve.filled, 1)
            pe.wait_ge(f2_w, 1)
            for n in range(2):
                bank = ring_act.open(pe, ("wT", "l2f", n))
                for i in range(4):
                    last = nc.tensor.transpose(bank[0:96, i * S:(i + 1) * S], w96[:, 4 * n + i, :], w["ident"])
                last.then_inc(ring_act.filled, 1)
            acc = [None, None]

            def down(n, c):
                rows = 64 if c == 16 else P
                rhs = w["f2_wds"] if c == 16 else w["f2_wd"][:, c * D:(c + 1) * D]
                pe.wait_ge(*f2_h.at((n, c)))
                for i in range(4):
                    last = nc.tensor.matmul(acc[n][:, i * D:(i + 1) * D],
                                            hid[(n * NC2 + c) % 3][0:rows, i * S:(i + 1) * S], rhs, start=False,
                                            stop=(c == 16 and i == 3))
                if c == 16:
                    last.then_inc(ring_dve.filled, 1)

            for m, (n, c) in enumerate(f2_seq + [(2, 0), (2, 1)]):
                if n < 2:
                    if c == 0:
                        pe.wait_ge(ring_act.emptied, ring_act.nth(("wT", "l2f", n)))
                    rows = 64 if c == 16 else P
                    wg = w["f2_wgs"] if c == 16 else w["f2_wg"][:, c * P:(c + 1) * P]
                    wu = w["f2_wus"] if c == 16 else w["f2_wu"][:, c * P:(c + 1) * P]
                    bank = ring_act.open(pe, ("up", "l2f", n, c))
                    nc.tensor.matmul(bank[0:rows, :], wu, xT[:, 4 * n:4 * n + 4, :], start=True, stop=True).then_inc(
                        ring_act.filled, 1)
                    bank = ring_score.open(pe, ("gate", "l2f", n, c))
                    nc.tensor.matmul(bank[0:rows, :], wg, xT[:, 4 * n:4 * n + 4, :], start=True, stop=True).then_inc(
                        ring_score.filled, 1)
                    if c < 16:
                        bank = ring_prob.open(pe, ("wexp", "l2f", n, c))
                        nc.tensor.matmul(bank, w["sel32_bf"][:, c * P:(c + 1) * P], w3T[:, 4 * n:4 * n + 4, :],
                                         start=True, stop=True).then_inc(ring_prob.filled, 1)
                if m >= 2:
                    pn, pc = f2_seq[m - 2]
                    if pc == 0:
                        acc[pn] = ring_dve.open(pe, ("out", "l2f", pn))
                        nc.tensor.matmul(acc[pn], w["ones"][0:1, :], spread(w["f2_bds"], 4), start=True, stop=False)
                        for i in range(4):
                            nc.tensor.matmul(acc[pn][:, i * D:(i + 1) * D], w96T[:, 4 * pn + i, :], w["f2_bd3"],
                                             start=False, stop=False)
                    down(pn, pc)
            finish_pe(pe, "l2f")

        def scalar_l2f(act):
            act.wait_ge(loaded["l2f"], 16)
            act.wait_ge(ring_dve.filled, ring_dve.nth(("router", "l2f")))
            nc.scalar.activation(aff[:, :, :].rearrange("p b e -> p (b e)"), ring_dve.bank(("router", "l2f"))[:, 0:256],
                                 ACT.Exp, scale=-1.0).then_inc(f2_a, 1)
            for n in range(2):
                bank = ring_act.take(act, ("wT", "l2f", n))
                src = bank[0:96, :].rearrange("p (b t) -> p b t", t=S)
                nc.scalar.activation(w96T[:, 4 * n:4 * n + 4, :], src, ACT.Copy)
                nc.scalar.activation(w3T[:, 4 * n:4 * n + 4, :], src, ACT.Copy).then_inc(ring_act.emptied, 1)
            act.wait_ge(f2_b, 1)
            for m, (n, c) in enumerate(f2_seq):
                rows = 64 if c == 16 else P
                if m >= 2:
                    act.wait_ge(*f2_h.at(f2_seq[m - 2]))
                bank = ring_act.take(act, ("up", "l2f", n, c))
                ub = w["f2_bus"] if c == 16 else w["f2_bu"][:, c:c + 1]
                hbias2 = hb[0:rows, c:c + 1]
                nc.scalar.activation(prob[0:rows, 2 + m % 2, :, :].rearrange("p c s -> p (c s)"), bank[0:rows, :],
                                     ACT.Identity, bias=ub).then_inc(ring_act.emptied, 1)
                act.wait_ge(ring_score.filled, ring_score.nth(("gate", "l2f", n, c)))
                nc.scalar.activation(prob[0:rows, m % 2, :, :].rearrange("p c s -> p (c s)"),
                                     ring_score.bank(("gate", "l2f", n, c))[0:rows, :], ACT.Tanh, scale=0.5,
                                     bias=hbias2).then_inc(*f2_t.inc((n, c)))
            finish_act(act, "l2f")

        def vector_l2f(dve):
            dve.wait_ge(loaded["l2f"], 16)
            link(dve, nc.vector.tensor_scalar(hb[:, 0:16], w["f2_bg"], 0.5, None, ALU.mult))
            nc.vector.tensor_scalar(hb[0:64, 16:17], w["f2_bgs"], 0.5, None, ALU.mult).then_inc(f2_b, 1)
            dve.wait_ge(f2_b, 1)
            dve.wait_ge(f2_a, 1)
            ring_dve.take(dve, ("router", "l2f"))
            a = aff[:, :, :]
            nc.vector.tensor_scalar(a, a, 1.0, None, ALU.add).then_inc(ring_dve.emptied, 1)
            dve.wait_ge(ring_dve.emptied, ring_dve.nth(("router", "l2f")))
            link(dve, nc.vector.reciprocal(a, a))
            for b in range(B):
                ins = nc.vector.max(mx[:, b, :], aff[:, b, :])
            link(dve, ins)
            for b in range(B):
                link(dve, nc.vector.match_replace(rep[:, b, :], mx[:, b, :], aff[:, b, :], -1.0))
            top = rm[:, 0, :]
            link(dve, nc.vector.tensor_reduce(top, mx, AX.X, ALU.add))
            link(dve, nc.vector.tensor_scalar(top, top, 1e-9, None, ALU.add))
            link(dve, nc.vector.reciprocal(top, top))
            link(dve, nc.vector.scalar_tensor_tensor(out=rep[:, :, :], in0=rep[:, :, :], scalar=0.0, in1=a,
                                                     op0=ALU.is_lt, op1=ALU.mult))
            link(dve, nc.vector.tensor_tensor(rep[:, :, :], rep[:, :, :], spread(top, 32, 2), ALU.mult))
            link(dve, nc.vector.tensor_copy(whalf[:, :, :], rep[:, :, :]))
            link(dve, nc.vector.tensor_copy(w96[:, :, 0:32], whalf[:, :, :]))
            link(dve, nc.vector.tensor_tensor(rep[:, :, :], rep[:, :, :], whalf[:, :, :], ALU.subtract))
            link(dve, nc.vector.tensor_copy(whalf[:, :, :], rep[:, :, :]))
            link(dve, nc.vector.tensor_copy(w96[:, :, 32:64], whalf[:, :, :]))
            nc.vector.tensor_tensor(w96[:, :, 64:96], rep[:, :, :], whalf[:, :, :], ALU.subtract).then_inc(f2_w, 1)
            dve.wait_ge(f2_w, 1)
            for m, (n, c) in enumerate(f2_seq):
                rows = 64 if c == 16 else P
                bank = ring_score.take(dve, ("gate", "l2f", n, c))
                dve.wait_ge(*f2_t.at((n, c)))
                th = prob[0:rows, m % 2, :, :].rearrange("p c s -> p (c s)")
                ub = prob[0:rows, 2 + m % 2, :, :].rearrange("p c s -> p (c s)")
                gb = w["f2_bgs"] if c == 16 else w["f2_bg"][:, c:c + 1]
                nc.vector.scalar_tensor_tensor(out=ub, in0=bank[0:rows, :], scalar=gb, in1=ub, op0=ALU.add,
                                               op1=ALU.mult).then_inc(ring_score.emptied, 1)
                dve.wait_ge(ring_score.emptied, ring_score.nth(("gate", "l2f", n, c)))
                link(dve, nc.vector.scalar_tensor_tensor(out=ub, in0=th, scalar=1.0, in1=ub, op0=ALU.add,
                                                         op1=ALU.mult))
                if m >= 3:
                    late = ring_score.nth(("gate", "l2f") + f2_seq[m - 1]) if False else None
                h = hid[m % 3][0:rows, 0:512]
                if c < 16:
                    wb = ring_prob.take(dve, ("wexp", "l2f", n, c))
                    nc.vector.tensor_tensor(h, ub, wb, ALU.mult).then_inc(ring_prob.emptied, 1)
                    dve.wait_ge(ring_prob.emptied, ring_prob.nth(("wexp", "l2f", n, c)))
                    nc.vector.tensor_copy(rden[:, 0:1], rden[:, 0:1]).then_inc(*f2_h.inc((n, c)))
                    dve.wait_ge(*f2_h.at((n, c)))
                else:
                    nc.vector.tensor_scalar(h, ub, 0.5, None, ALU.mult).then_inc(*f2_h.inc((n, c)))
                    dve.wait_ge(*f2_h.at((n, c)))
                if (n, c) == (1, 1):
                    finish_out(dve, 0)
            finish_out(dve, 1)

        def finish_out(dve, n):
            bank = ring_dve.take(dve, ("out", "l2f", n))
            xs = x[:, 4 * n:4 * n + 4, :]
            nc.vector.tensor_tensor(xs, bank.rearrange("p (b d) -> p b d", d=D), xs, ALU.add).then_inc(
                ring_dve.emptied, 1)
            dve.wait_ge(ring_dve.emptied, ring_dve.nth(("out", "l2f", n)))
            finish_dve(dve, "l2f", n)

        def gpsimd_l2f(pool):
            finish_pool(pool, "l2f")

        sc = O[0:8, 0, :]
        sw = [O[0:8, 1, :], qT[0:8, 0, :, :].rearrange("p c s -> p (c s)")]
        se = qT[0:8, 1, :, :].rearrange("p c s -> p (c s)")
        mx3 = sb("mx3", [8, 16, 8])
        s8 = sb("s8", [8, 4])
        f3_d = sem("f3_dve")
        f3_a = sem("f3_act")
        f3_seq = [(e, n, k) for e in range(8) for n in range(2) for k in range(2)]
        f3_t = events(sem("f3_tanh"), f3_seq)
        f3_h = events(sem("f3_hidden"), f3_seq)

        def tensor_l3f(pe):
            pe.wait_ge(loaded["l3f"], 16)
            xT = xT_of["l3f"]
            for n in range(2):
                for b in halves[n]:
                    xT_wait(pe, "l3f", b)
                bank = ring_dve.open(pe, ("sc", n))
                nc.tensor.matmul(bank[0:8, :], w["f3_wg"], xT[:, 4 * n:4 * n + 4, :], start=True, stop=True).then_inc(
                    ring_dve.filled, 1)

            def y(e, n):
                bank = ring_dve.open(pe, ("y", e, n))
                for k in range(2):
                    pe.wait_ge(*f3_h.at((e, n, k)))
                for i in range(4):
                    for k in range(2):
                        last = nc.tensor.matmul(bank[:, i * D:(i + 1) * D],
                                                hid[(2 * e + n) % 3][:, 512 * k + i * S:512 * k + (i + 1) * S],
                                                w["f3_w2"][:, (2 * e + k) * D:(2 * e + k + 1) * D], start=(k == 0),
                                                stop=(k == 1))
                last.then_inc(ring_dve.filled, 1)

            for e, n, k in f3_seq:
                c = 2 * e + k
                bank = ring_score.open(pe, ("gate", e, n, k))
                nc.tensor.matmul(bank, w["f3_w1"][:, c * P:(c + 1) * P], xT[:, 4 * n:4 * n + 4, :], start=True,
                                 stop=True).then_inc(ring_score.filled, 1)
                bank = ring_prob.open(pe, ("up", e, n, k))
                nc.tensor.matmul(bank, w["f3_w3"][:, c * P:(c + 1) * P], xT[:, 4 * n:4 * n + 4, :], start=True,
                                 stop=True).then_inc(ring_prob.filled, 1)
                if (e, n, k) == (0, 1, 0):
                    pe.wait_ge(f3_d, 2)
                    bank = ring_act.open(pe, ("wcol",))
                    for b in range(B):
                        last = nc.tensor.transpose(bank[:, 8 * b:8 * b + 8], se[:, b * S:(b + 1) * S],
                                                   w["ident"][0:8, 0:8])
                    last.then_inc(ring_act.filled, 1)
                if k == 1 and (e, n) != (0, 0):
                    y(*((e, 0) if n else (e - 1, 1)))
            y(7, 1)

        def scalar_l3f(act):
            act.wait_ge(f3_d, 1)
            nc.scalar.activation(se, sc, ACT.Exp, bias=s8[:, 0:1]).then_inc(f3_a, 1)
            for m, (e, n, k) in enumerate(f3_seq):
                if m >= 4:
                    act.wait_ge(*f3_h.at(f3_seq[m - 4]))
                act.wait_ge(ring_score.filled, ring_score.nth(("gate", e, n, k)))
                nc.scalar.activation(prob[:, m % 4, :, :].rearrange("p c s -> p (c s)"),
                                     ring_score.bank(("gate", e, n, k)), ACT.Tanh, scale=0.5).then_inc(
                    *f3_t.inc((e, n, k)))
                if m == 2:
                    bank = ring_act.take(act, ("wcol",))
                    nc.scalar.activation(wcol[:, :, 0:8], bank[:, 0:64].rearrange("p (b e) -> p b e", e=8), ACT.Copy
                                         ).then_inc(ring_act.emptied, 1)

        def vector_l3f(dve):
            for n in range(2):
                bank = ring_dve.take(dve, ("sc", n))
                nc.vector.tensor_copy(sc[:, 512 * n:512 * n + 512], bank[0:8, :]).then_inc(ring_dve.emptied, 1)
                dve.wait_ge(ring_dve.emptied, ring_dve.taken)
            dve.wait_ge(ring_dve.emptied, ring_dve.nth(("sc", 1)))
            src = sc
            for r in range(16):
                link(dve, nc.vector.max(mx3[:, r, :], src))
                if r == 0:
                    nc.vector.tensor_scalar(s8[:, 0:1], mx3[:, 0, 0:1], -1.0, None, ALU.mult).then_inc(f3_d, 1)
                    dve.wait_ge(f3_d, 1)
                link(dve, nc.vector.match_replace(sw[r % 2], mx3[:, r, :], src, -3.0e38))
                src = sw[r % 2]
            link(dve, nc.vector.tensor_tensor(src, src, sc, ALU.not_equal))
            dve.wait_ge(f3_a, 1)
            link(dve, nc.vector.tensor_tensor(se, se, src, ALU.mult))
            link(dve, nc.vector.tensor_reduce(s8[:, 1:2], se, AX.X, ALU.add))
            link(dve, nc.vector.reciprocal(s8[:, 2:3], s8[:, 1:2]))
            nc.vector.tensor_scalar(se, se, s8[:, 2:3], 0.5, ALU.mult, ALU.mult).then_inc(f3_d, 1)
            dve.wait_ge(f3_d, 2)

            def add(e, n):
                bank = ring_dve.take(dve, ("y", e, n))
                if (e, n) == (0, 0):
                    dve.wait_ge(ring_act.emptied, ring_act.nth(("wcol",)))
                for i in range(4):
                    b = 4 * n + i
                    ins = nc.vector.scalar_tensor_tensor(out=x[:, b, :], in0=bank[:, i * D:(i + 1) * D],
                                                         scalar=wcol[:, b, e:e + 1], in1=x[:, b, :], op0=ALU.mult,
                                                         op1=ALU.add)
                ins.then_inc(ring_dve.emptied, 1)
                dve.wait_ge(ring_dve.emptied, ring_dve.taken)

            for m, (e, n, k) in enumerate(f3_seq):
                dve.wait_ge(*f3_t.at((e, n, k)))
                g = ring_score.take(dve, ("gate", e, n, k))
                th = prob[:, m % 4, :, :].rearrange("p c s -> p (c s)")
                nc.vector.scalar_tensor_tensor(out=th, in0=th, scalar=1.0, in1=g, op0=ALU.add, op1=ALU.mult
                                               ).then_inc(ring_score.emptied, 1)
                dve.wait_ge(ring_score.emptied, ring_score.nth(("gate", e, n, k)))
                u = ring_prob.take(dve, ("up", e, n, k))
                nc.vector.tensor_tensor(hid[(2 * e + n) % 3][:, 512 * k:512 * k + 512], th, u, ALU.mult).then_inc(
                    ring_prob.emptied, 1)
                dve.wait_ge(ring_prob.emptied, ring_prob.nth(("up", e, n, k)))
                nc.vector.tensor_copy(rden[:, 0:1], rden[:, 0:1]).then_inc(*f3_h.inc((e, n, k)))
                dve.wait_ge(*f3_h.at((e, n, k)))
                if k == 1 and (e, n) != (0, 0):
                    add(*((e, 0) if n else (e - 1, 1)))
            add(7, 1)

        def gpsimd_l3f(pool):
            pass

        PE = {"l0a": tensor_l0a, "l0f": tensor_l0f}
        SC = {"l0a": scalar_l0a, "l0f": scalar_l0f}
        VE = {"l0a": vector_l0a, "l0f": vector_l0f}
        PO = {"l0a": gpsimd_l0a, "l0f": gpsimd_l0f}
        PE.update(l1x=tensor_l1x, l1f=tensor_l1f, l2f=tensor_l2f, l3f=tensor_l3f)
        SC.update(l1x=scalar_l1x, l1f=scalar_l1f, l2f=scalar_l2f, l3f=scalar_l3f)
        VE.update(l1x=vector_l1x, l1f=vector_l1f, l2f=vector_l2f, l3f=vector_l3f)
        PO.update(l1x=gpsimd_l1x, l1f=gpsimd_l1f, l2f=gpsimd_l2f, l3f=gpsimd_l3f)
        block = stack.enter_context(nc.Block())

        @block.tensor
        def _(pe):
            for s in subs:
                PE[s](pe) if s in PE else tensor_attention(pe, s)

        @block.scalar
        def _(act):
            act.wait_ge(loaded["const"], 16)
            for s in subs:
                SC[s](act) if s in SC else scalar_attention(act, s)

        @block.vector
        def _(dve):
            dve.wait_ge(loaded["const"], 16)
            for s in subs:
                if s == subs[-1]:
                    pass
                VE[s](dve) if s in VE else vector_attention(dve, s)
            dve.drain().then_inc(x_final, 1)
            dve.wait_ge(x_final, 1)

        @block.gpsimd
        def _(pool):
            for s in subs:
                PO[s](pool) if s in PO else gpsimd_attention(pool, s)

        @block.sync
        def _(sp):
            sp.dma_start(x[:], x_dram.rearrange("b t d -> t b d")).then_inc(x_loaded, 16)
            order = ["l0a", "const", "small", "sel32"]
            order += [s for s in subs if s in groups and s not in order and s not in [later for _, later in PLACES]]
            for g in order:
                sp.dma_start(store[g], groups[g][0]).then_inc(loaded[g], 16)
                if g == "sel32":
                    for name, dst in (("ctxT", ctxT), ("ctx", ctx)):
                        sp.dma_start(dst[:], ctx_dram[name]).then_inc(ctx_loaded, 16)
                    sp.dma_start(rowconst, rowconst_dram).then_inc(rowconst_loaded, 16)
            if "l3x" in subs:
                sp.wait_ge(ring_dve.emptied, ring_dve.nth(("out", "l0f", 1)))
                sp.dma_start(mask_i, mask_dram).then_inc(mask_loaded, 16)
            for first, later in PLACES:
                if later in subs:
                    sp.wait_ge(ring_dve.emptied, ring_dve.nth(("out", first, 1 if first == "l0a" else B - 1)))
                    if first == "l0a":
                        sp.wait_ge(*stats_ready.at(("l0x", 0, B - 1)))
                    sp.dma_start(store[later], groups[later][0]).then_inc(loaded[later], 16)
            sp.wait_ge(x_final, 1)
            sp.dma_start(out_dram.rearrange("b t d -> t b d"), x[:]).then_inc(stored, 16)
            sp.wait_ge(stored, 16)
            sp.wait_ge(rowconst_loaded, 16)


def lay_out(inputs):
    def f(name):
        return np.asarray(inputs[name])

    def chunked(a):
        return np.concatenate([a[i:i + P] for i in range(0, a.shape[0], P)], axis=1)

    def col(a):
        return a.reshape(-1, P).T

    def rep(a):
        return np.broadcast_to(a.reshape(1, -1), (P, a.size))

    def row(a):
        return a.reshape(1, -1)

    p = np.arange(P)
    c1024 = np.arange(TOK)
    h8 = np.arange(8)[:, None]
    dim = p % 32
    freq = (1.0 / 10000.0 ** (np.arange(0, 8, 2, dtype=np.float32) / 8)).astype(np.float32)
    angle = np.arange(S, dtype=np.float32)[None, :] * freq[dim % 4][:, None]
    rotated = (dim < 8)[:, None]
    const = {
        "ident": np.eye(P),
        "ones": np.ones((P, P)),
        "mask8": (p[:, None] % 32) // 8 == np.arange(4),
        "mask32": p[:, None] // 32 == np.arange(4),
        "mask16": 0.25 * (p[:, None] // 16 == np.arange(8)),
        "iota8": np.broadcast_to(np.arange(8), (P, 8)),
        "sel8": 0.5 * (np.arange(256)[None, :] // 32 == h8),
        "cos": np.where(rotated, np.cos(angle), 1.0),
        "sin": np.where(rotated, np.sin(angle) * np.where(dim < 4, -1.0, 1.0)[:, None], 0.0),
        "bigparts": np.concatenate([np.pad(BIG_PARTS, ((0, 29), (0, 0)))] * 4),
    }
    rowconst = np.zeros((8, 3, TOK), np.float32)
    rowconst[:, 0] = c1024[None, :] // S == h8
    rowconst[:, 1] = c1024 % S != 0
    rowconst[:, 2] = np.where(c1024 % S == 0, NEG, 0.0)
    q, k = p[:, None], p[None, :]
    small = {
        "ident_bf": np.eye(P),
        "ones_bf": np.ones((P, P)),
        "causal_bf": np.where(k <= q, 0.0, NEG),
        "causalT_bf": np.where(q <= k, 0.0, NEG),
    }
    sel32 = {
        "sel32_bf": 0.5 * (np.arange(96)[:, None] % 32 == np.arange(2048)[None, :] // 64),
    }
    perm = np.arange(256).reshape(8, 32).copy()
    perm[:, 0:8] = perm[:, [4, 5, 6, 7, 0, 1, 2, 3]]
    perm = perm.reshape(-1)
    kperm = perm[0:64]
    wq, wk = f("L2_attn_Wq"), f("L2_attn_Wk")

    def rep4(a, kv):
        return np.concatenate([a[:, 32 * kv:32 * kv + 32]] * 4, axis=1)

    gate_cols = {"wi": f("L1_xattn_igate_w"), "wf": f("L1_xattn_fgate_w")}
    groups = {
        "l0a": {
            "l0a_win": f("L0_attn_w_in").T, "l0a_wx": chunked(f("L0_attn_w_x").T), "l0a_wout": chunked(f("L0_attn_w_out").T),
            "l0a_bin": col(f("L0_attn_b_in")[:256]),
            "l0a_wconv": f("L0_attn_w_conv")[:, 0, :].reshape(2, P, 4).transpose(1, 0, 2).reshape(P, 8),
            "l0a_bconv": col(f("L0_attn_b_conv")), "l0a_bx": col(f("L0_attn_b_x")[:256]),
            "l0a_bout": rep(f("L0_attn_b_out")),
        },
        "const": const,
        "l0x": {
            "x0_wq": f("L0_xattn_w_q"), "x0_wk": f("L0_xattn_w_kv")[:, :1024], "x0_wv": f("L0_xattn_w_kv")[:, 1024:],
            "x0_wo": chunked(f("L0_xattn_w_out")), "x0_gamma": col(f("L0_xattn_ln_gamma")),
            "x0_beta": col(f("L0_xattn_ln_beta")), "x0_bout": row(f("L0_xattn_b_out")), "x0_gate": rep(f("L0_xattn_gate")),
        },
        "l0f": {"f0_wr": f("L0_ffn_W_r").T, "f0_wk": f("L0_ffn_W_k").T, "f0_wv": f("L0_ffn_W_v").T,
                "f0_mur": col(f("L0_ffn_mu_r")), "f0_muk": col(f("L0_ffn_mu_k"))},
        "l1a": {
            "a1_wq": f("L1_attn_Q").transpose(1, 2, 0).reshape(D, 1024), "a1_wk": f("L1_attn_K").transpose(1, 2, 0).reshape(D, 1024),
            "a1_wv": f("L1_attn_V").transpose(1, 2, 0).reshape(D, 1024),
            "a1_wo": chunked(f("L1_attn_W").transpose(2, 1, 0).reshape(1024, D)),
        },
        "l1x": {
            "x1_wi": chunked(f("L1_xattn_igate_w").T), "x1_wf": chunked(f("L1_xattn_fgate_w").T),
            "x1_bi": f("L1_xattn_igate_b").reshape(8, 1), "x1_bf": f("L1_xattn_fgate_b").reshape(8, 1),
            "x1_lnscale": rep(f("L1_xattn_ln_scale")),
        },
        "l1f": {
            "f1_wv": f("L1_ffn_Wv").T, "f1_bvc": col(f("L1_ffn_bv")), "f1_bvr": row(f("L1_ffn_bv")),
            "f1_wgp": np.concatenate([f("L1_ffn_Wg").T, f("L1_ffn_Wp").reshape(64, D).T], axis=1),
            "f1_bg": rep(f("L1_ffn_bg")), "f1_gr": rep(f("L1_ffn_g_r")), "f1_br": rep(f("L1_ffn_b_r")),
            "f1_gc": rep(f("L1_ffn_g_c")), "f1_bc": rep(f("L1_ffn_b_c")), "f1_alpha": rep(f("L1_ffn_alpha")),
            "f1_w1": f("L1_ffn_W1").reshape(256, D).T, "f1_b1": col(f("L1_ffn_b1")),
            "f1_w2": chunked(f("L1_ffn_W2").transpose(0, 2, 1).reshape(256, D)), "f1_b2": f("L1_ffn_b2"),
        },
        "l2a": {
            "a2_wq4": np.concatenate([wq[:, 0:256], wq[:, 0:256][:, perm]], axis=1),
            "a2_wk4": np.concatenate([rep4(wk, 0), rep4(wk, 1), rep4(wk[:, kperm], 0), rep4(wk[:, kperm], 1)], axis=1),
            "a2_wvg": np.concatenate([f("L2_attn_Wv"), wq[:, 256:512]], axis=1), "a2_wo": chunked(f("L2_attn_Wo")),
        },
        "l2x": {
            "x2_wq": f("L2_xattn_Wq").T, "x2_wk": f("L2_xattn_Wk").T, "x2_wv": f("L2_xattn_Wv").T,
            "x2_wo": f("L2_xattn_Wo").T, "x2_bq": col(f("L2_xattn_bq")), "x2_bk": col(f("L2_xattn_bk")),
            "x2_bv": row(f("L2_xattn_bv")), "x2_bo": row(f("L2_xattn_bo")),
        },
        "l2f": {
            "f2_wr": f("L2_ffn_Wr"), "f2_br": row(f("L2_ffn_br")),
            "f2_wg": f("L2_ffn_Wg").transpose(1, 0, 2).reshape(D, 2048), "f2_wu": f("L2_ffn_Wu").transpose(1, 0, 2).reshape(D, 2048),
            "f2_wd": chunked(f("L2_ffn_Wd").reshape(2048, D)), "f2_bg": col(f("L2_ffn_bg")), "f2_bu": col(f("L2_ffn_bu")),
            "f2_bd3": np.concatenate([f("L2_ffn_bd")] * 3, axis=0), "f2_wgs": f("L2_ffn_Wg_s"), "f2_wus": f("L2_ffn_Wu_s"),
            "f2_wds": f("L2_ffn_Wd_s"), "f2_bgs": f("L2_ffn_bg_s").reshape(64, 1), "f2_bus": f("L2_ffn_bu_s").reshape(64, 1),
            "f2_bds": row(f("L2_ffn_bd_s")),
        },
        "l3a": {"a3_wq": f("L3_attn_W_attn")[:, 0:128], "a3_wk": f("L3_attn_W_attn")[:, 128:256],
                "a3_wv": f("L3_attn_W_attn")[:, 256:384], "a3_wo": f("L3_attn_W_proj")},
        "l3x": {"x3_wq": f("L3_xattn_w_q").T, "x3_wk": f("L3_xattn_w_k").T, "x3_wv": f("L3_xattn_w_v").T,
                "x3_wo": f("L3_xattn_w_o").T},
        "l3f": {
            "f3_wg": f("L3_ffn_Wg").T, "f3_w1": f("L3_ffn_W1").reshape(2048, D).T, "f3_w3": f("L3_ffn_W3").reshape(2048, D).T,
            "f3_w2": chunked(f("L3_ffn_W2").transpose(0, 2, 1).reshape(2048, D)),
        },
        "small": small, "sel32": sel32,
    }
    packed = {}
    for g, pieces in groups.items():
        width = sum(a.shape[1] for a in pieces.values())
        whole, off, names = np.zeros((P, width), np.float32), 0, {}
        for name, a in pieces.items():
            whole[0:a.shape[0], off:off + a.shape[1]] = a
            names[name] = (off, a.shape[0], a.shape[1])
            off += a.shape[1]
        packed[g] = (whole, names)
    return packed, rowconst


def kernel(**inputs):
    import concourse.bacc as bacc
    from concourse.bass_utils import run_bass_kernel_spmd

    nc = bacc.Bacc("TRN2", target_bir_lowering=False, num_devices=1)
    arrays, groups = {}, {}

    def dram(name, a):
        arrays[name] = np.ascontiguousarray(a)
        return nc.dram_tensor(name, a.shape, mybir.dt.from_np(a.dtype), kind="ExternalInput").ap()

    packed, rowconst = lay_out(inputs)
    for g, (whole, names) in packed.items():
        if g in SUBLAYERS[STOP:]:
            continue
        groups[g] = (dram(f"in_{g}", whole), names)
    x = np.asarray(inputs["x"])
    c = np.asarray(inputs["ctx_1024"])
    ctx = {"ctxT": dram("in_ctxT", c.transpose(2, 0, 1)), "ctx": dram("in_ctx", c.transpose(1, 0, 2))}
    m = np.asarray(inputs["mask_BxS2_if1"])
    mask = dram("in_mask", np.broadcast_to(m[None], (P, B, S)))
    out = nc.dram_tensor("out_x", x.shape, F32, kind="ExternalOutput").ap()
    bass_decoder_kernel(nc, groups, ctx, dram("in_x", x), mask, dram("in_rowconst", rowconst), out)
    r = run_bass_kernel_spmd(nc, [arrays], core_ids=[0])
    return r.results[0]["out_x"]
```

```python
from contextlib import ExitStack

import numpy as np

import concourse.bass as bass
from concourse import mybir

F32 = mybir.dt.float32
BF16 = mybir.dt.bfloat16
I32 = mybir.dt.int32
U32 = mybir.dt.uint32
ALU = mybir.AluOpType
ACT = mybir.ActivationFunctionType
AX = mybir.AxisListType

B, S, D = 8, 128, 128
P = 128
HALF = B // 2
TOK = B * S
NEG = -1.0e30
PLACES = (("l0a", "l2a"), ("l0x", "l3f"), ("l1a", "l2f"))
SUBLAYERS = ("l0a", "l0x", "l0f", "l1a", "l1x", "l1f", "l2a", "l2x", "l2f", "l3a", "l3x", "l3f")
STOP = 12
BIG_PARTS = np.array([[999292928.0], [704512.0], [2560.0]])


def spread(ap, count, at=1):
    u = ap.unsqueeze(at)
    shape = list(u.shape)
    shape[at] = count
    return u.to_broadcast(shape)


class Count:

    def __init__(self, sem, keys):
        self.sem, self.value, self.last = sem, {k: n + 1 for n, k in enumerate(keys)}, 0

    def inc(self, key):
        assert self.value[key] == self.last + 1, (key, self.last)
        self.last += 1
        return self.sem, 1

    def at(self, key):
        return self.sem, self.value[key]


class Ring:

    def __init__(self, banks, filled, emptied):
        self.banks, self.filled, self.emptied, self.use, self.taken = banks, filled, emptied, {}, 0

    def open(self, pe, name):
        assert name not in self.use, name
        n = len(self.use)
        self.use[name] = n + 1
        if n >= len(self.banks):
            pe.wait_ge(self.emptied, n - len(self.banks) + 1)
        return self.bank(name)

    def take(self, eng, name):
        self.taken = self.use[name]
        eng.wait_ge(self.filled, self.taken)
        return self.bank(name)

    def bank(self, name):
        return self.banks[(self.use[name] - 1) % len(self.banks)]

    def nth(self, name):
        return self.use[name]


def bass_decoder_kernel(nc, groups, ctx_dram, x_dram, mask_dram, rowconst_dram, out_dram):
    with ExitStack() as stack:
        def sb(name, shape, dt=F32):
            return stack.enter_context(nc.sbuf_tensor(name, shape, dt))[(slice(None),) * len(shape)]

        def sem(name):
            return stack.enter_context(nc.semaphore(name))

        store, piece = {}, {}
        widths = {g: dram.shape[1] for g, (dram, _) in groups.items()}
        shared = {}
        for first, later in PLACES:
            shared[first] = shared[later] = sb(f"w_{first}_{later}", [P, max(widths.get(first, 1), widths.get(later, 1))])
        for g, (dram, names) in groups.items():
            if g in ("sel32", "small"):
                continue
            store[g] = shared[g][:, 0:widths[g]] if g in shared else sb(f"w_{g}", [P, widths[g]], dram.dtype)
            for name, (off, rows, cols) in names.items():
                piece[name] = store[g][0:rows, off:off + cols]
        w = piece
        const_bf = sb("const_bf", [P, widths["sel32"] + widths["small"]], BF16)
        for name in ("sel32", "small"):
            for part, (off, rows, cols) in groups[name][1].items():
                w[part] = const_bf[0:rows, off:off + cols] if name == "sel32" else \
                    const_bf[0:rows, widths["sel32"] + off:widths["sel32"] + off + cols]

        x = sb("x", [P, B, D])
        ctx = sb("ctx", [P, B, D])
        ctxT = sb("ctxT", [P, B, S])
        xT_pair = [sb("xT_even", [P, B, S]), sb("xT_odd", [P, B, S])]
        xT_of = {s: xT_pair[i % 2] for i, s in enumerate(SUBLAYERS)}
        xpad = sb("xpad", [P, B, S + 1])
        xT_of["l0f"] = xpad[:, :, 1:S + 1]
        stats = sb("stats", [P, B, 6])
        mv = sb("mv", [P, B, 2])
        veps = sb("veps", [P, B, 1])
        rstd = sb("rstd", [P, B, 1])
        xhat = sb("xhat", [P, B, D])
        power = sb("power", [P, 2])

        big = [sb(f"big{i}", [P, 2, 8, 132]) for i in range(2)]
        qT = sb("qT", [P, 2, 8, S])
        kT = sb("kT", [P, 2, 8, S])
        V = sb("V", [P, 2, 16 * 65])
        V9 = sb("V9", [P, 4, 16 * 9 + 23])
        V33 = sb("V33", [P, 4, 2, 33])
        prob = sb("prob", [P, 4, 4, S])
        probT = sb("probT", [P, 2, 4, S])
        V17 = prob.rearrange("p m c s -> p (m c s)")[:, 0:B * 136].rearrange("p (b h e) -> p b h e", b=B, e=17)
        store["sel32"] = prob.rearrange("p m c s -> p (m c s)")[:, 0:widths["sel32"]]
        store["small"] = probT.rearrange("p m c s -> p (m c s)")[:, 0:widths["small"]]
        nmax = sb("nmax", [P, 4, 4])
        rden = sb("rden", [P, 4])
        O = sb("O", [P, 2, 16 * 64])
        OT = sb("OT", [P, 2, 8, S])
        small = sb("small", [P, 32])
        wcol = sb("wcol", [P, B, 32])

        psum = stack.enter_context(nc.psum_tensor("psum", [P, 8, 512], F32))
        ring_act = Ring([psum[:, 0, :], psum[:, 1, :]], sem("act_bank_filled"), sem("act_bank_emptied"))
        ring_dve = Ring([psum[:, 2, :], psum[:, 3, :]], sem("dve_bank_filled"), sem("dve_bank_emptied"))
        ring_score = Ring([psum[:, 4, :], psum[:, 5, :]], sem("scores_filled"), sem("scores_emptied"))
        ring_prob = Ring([psum[:, 6, :], psum[:, 7, :]], sem("probT_filled"), sem("probT_emptied"))

        loaded = {g: sem(f"loaded_{g}") for g in groups}
        rowconst_loaded = sem("rowconst_loaded")
        x_loaded, ctx_loaded, mask_loaded, stored = sem("x_loaded"), sem("ctx_loaded"), sem("mask_loaded"), sem("stored")

        subs = SUBLAYERS[:STOP]
        UNITS = {"l0x": 4, "l1a": 4, "l2a": 2, "l2x": 4, "l3a": 4, "l3x": 4}
        norms = [(s, r, b) for s in subs for h in (0, 1) for r in ((0, 1) if s == "l0x" else (0,))
                 for b in range(HALF * h, HALF * h + HALF)]
        stats_ready = Count(sem("stats_ready"), norms)
        rstd_ready = Count(sem("rstd_ready"), norms)
        xhat_ready = Count(sem("xhat_ready"), norms)
        x_final = sem("x_final")
        units = [(s, b, g) for s in subs if s in UNITS for b in range(B) for g in range(UNITS[s])]
        exped = Count(sem("probs_exped"), units)
        pool_ready = sem("pool_ready")
        dve_chain, act_chain, pool_chain = sem("dve_chain"), sem("act_chain"), sem("pool_chain")
        k_masked = Count(sem("k_masked"), [(s, b) for s in subs if s in ("l2a", "l2x", "l3a", "l3x") for b in range(B)])
        narrow = [(s, b) for s in subs if s in ("l2x", "l3a", "l3x") for b in range(B)]
        avT_filled, avT_copied = Count(sem("avT_filled"), narrow), Count(sem("avT_copied"), narrow)
        av_filled, av_scaled = Count(sem("av_filled"), narrow), Count(sem("av_scaled"), narrow)
        out_filled, out_added = Count(sem("out_filled"), narrow), Count(sem("out_added"), narrow)
        roped = Count(sem("rope_products"), [(b,) for b in range(B)])
        tern = sem("ternary_ready")
        const_cast = sem("const_cast")
        mask_ready = sem("mask_ready")
        act_side = sem("act_side")
        dve_side = sem("dve_side")
        act_log, dve_log = [], []
        chains = {"dve": 0, "act": 0, "pool": 0}

        def events(sem_, keys):
            return Count(sem_, keys)

        l0a_conv = events(sem("l0a_conv"), [(c, n) for n in range(2) for c in range(2)])
        l0a_silu = events(sem("l0a_silu_tanh"), [(c, n) for n in range(2) for c in range(2)])
        l0a_xc = events(sem("l0a_xc"), [(c, n) for n in range(2) for c in range(2)])
        l0a_gate = events(sem("l0a_gate_tanh"), [(c, n) for n in range(2) for c in range(2)])
        l0a_y = events(sem("l0a_y"), [(c, n) for n in range(2) for c in range(2)])
        l0a_in = events(sem("l0a_in"), [(c, n) for n in range(2) for c in range(2)])
        scales_ready = sem("scales_ready")
        gate_l0x = sem("gate_l0x")
        l0f_mix = events(sem("l0f_mix"), [(n,) for n in range(2)])
        l0f_r = events(sem("l0f_r_tanh"), [(b,) for b in range(B)])
        mix_k = events(sem("l0f_kact"), [(n,) for n in range(2)])
        lstm_wkv, lstm_cleared = sem("lstm_wkv"), sem("lstm_cleared")
        lstm_abs, lstm_log, lstm_G, lstm_A, lstm_M, lstm_expA = (
            events(sem(f"lstm_{name}"), [(0,), (1,)]) for name in ("abs", "log", "G", "A", "M", "expA"))
        lstm_q = events(sem("lstm_q"), [(b,) for b in range(B)])
        lstm_var = events(sem("lstm_var"), [(b,) for b in range(B)])
        lstm_rstd = events(sem("lstm_rstd"), [(b,) for b in range(B)])
        v_ready = sem("v_ready")
        rt = sem("router_dve")
        rp = sem("router_pool")
        ra = sem("router_act")
        rt_n, rp_n, ra_n = [0], [0], [0]

        def ln_stats(dve, s, b, r=0):
            src = x if r == 0 else xhat
            link(dve, nc.vector.bn_stats(stats[:, b, :], src[:, b, :]))
            nc.vector.bn_aggr(mv[:, b, :], stats[:, b, :]).then_inc(*stats_ready.inc((s, r, b)))
            dve.wait_ge(*stats_ready.at((s, r, b)))

        def ln_rstd(pool, s, b, r=0):
            pool.wait_ge(*stats_ready.at((s, r, b)))
            plink(pool, nc.gpsimd.tensor_scalar(veps[:, b, :], mv[:, b, 1:2], 1e-5, None, ALU.add))
            nc.gpsimd.tensor_tensor(rstd[:, b, :], veps[:, b, :], power[:, 0:1], ALU.pow).then_inc(
                *rstd_ready.inc((s, r, b)))
            pool.wait_ge(*rstd_ready.at((s, r, b)))

        def ln_xhat(dve, s, b, r=0):
            src = x if r == 0 else xhat
            dve.wait_ge(*rstd_ready.at((s, r, b)))
            nc.vector.tensor_scalar(xhat[:, b, :], src[:, b, :], mv[:, b, 0:1], rstd[:, b, :], ALU.subtract,
                                    ALU.mult).then_inc(*xhat_ready.inc((s, r, b)))
            dve.wait_ge(*xhat_ready.at((s, r, b)))
            if s == "l0x" and r == 0:
                dve.wait_ge(*xhat_ready.at((s, r, b)))

        def ln_transpose(pe, s, bs):
            bank = ring_act.open(pe, ("xT", s, bs))
            for i, b in enumerate(bs):
                pe.wait_ge(*xhat_ready.at((s, 1 if s == "l0x" else 0, b)))
                last = nc.tensor.transpose(bank[:, i * S:(i + 1) * S], xhat[:, b, :], w["ident"])
            last.then_inc(ring_act.filled, 1)

        def ln_copy(act, s, bs):
            bank = ring_act.take(act, ("xT", s, bs))
            src = bank[:, 0:len(bs) * S].rearrange("p (b t) -> p b t", t=S)
            dst = xT_of[s][:, bs[0]:bs[-1] + 1, :]
            if s == "l0x":
                act.wait_ge(loaded["l0x"], 16)
                nc.scalar.activation(dst, src, ACT.Identity, scale=w["x0_gamma"],
                                     bias=w["x0_beta"]).then_inc(ring_act.emptied, 1)
            else:
                nc.scalar.activation(dst, src, ACT.Copy).then_inc(ring_act.emptied, 1)

        def xT_use(s, b):
            return next(n for name, n in ring_act.use.items() if name[0:2] == ("xT", s) and b in name[2])

        def xT_wait(pe, s, b):
            pe.wait_ge(ring_act.emptied, xT_use(s, b))

        def link(dve, ins):
            chains["dve"] += 1
            ins.then_inc(dve_chain, 1)
            dve.wait_ge(dve_chain, chains["dve"])

        def alink(act, ins):
            chains["act"] += 1
            ins.then_inc(act_chain, 1)
            act.wait_ge(act_chain, chains["act"])

        def plink(pool, ins):
            chains["pool"] += 1
            ins.then_inc(pool_chain, 1)
            pool.wait_ge(pool_chain, chains["pool"])

        halves = [tuple(range(HALF * n, HALF * n + HALF)) for n in range(2)]

        def next_of(s):
            i = SUBLAYERS.index(s) + 1
            return SUBLAYERS[i] if i < STOP else None

        def finish_stats(dve, s, b):
            if next_of(s):
                ln_stats(dve, next_of(s), b)

        xin = big[0][:, :, :, 0:131]
        ycv = big[1][:, :, :, 0:S]
        xc2 = qT
        y4 = kT
        tin = OT[:, 0, 0:2, :].rearrange("p c s -> p (c s)")
        tx = OT[:, 0, 2:6, :].rearrange("p (c o) s -> p c (o s)", c=2)
        tout = OT[:, 0, 6:8, :]
        tern_w = [("l0a_win", 512 * 128, slice(0, 256)), ("l0a_wx", 400 * 256, None), ("l0a_wout", 128 * 256, None)]
        absum = small[:, 0:3]
        scl = small[:, 4:7]
        thr = small[:, 8:11]
        nthr = small[:, 12:15]
        lowmask = O[:, :, :].rearrange("p a (m c) -> p (a m) c", c=256)
        qscale = small[:, 16:20]
        hbias = small[:, 20:22]

        def tensor_l0a(pe):
            pe.wait_ge(scales_ready, 1)
            bank = ring_dve.open(pe, ("scales",))
            pe.wait_ge(loaded["const"], 16)
            nc.tensor.matmul(bank[:, 0:3], w["ones"], absum, start=True, stop=True).then_inc(ring_dve.filled, 1)
            for n in range(2):
                ln_transpose(pe, "l0a", halves[n])
            pe.wait_ge(tern, 1)
            for n in range(2):
                xT_wait(pe, "l0a", halves[n][0])
                for c in range(2):
                    bank = ring_act.open(pe, ("xin", c, n))
                    nc.tensor.matmul(bank, tin[:, c * P:(c + 1) * P], xT_of["l0a"][:, halves[n][0]:halves[n][0] + 4, :],
                                     start=True, stop=True).then_inc(ring_act.filled, 1)
            for n in range(2):
                for c2 in range(2):
                    bank = ring_act.open(pe, ("delta", c2, n))
                    for c in range(2):
                        pe.wait_ge(*l0a_xc.at((c, n)))
                        last = nc.tensor.matmul(bank, tx[:, c, c2 * P:(c2 + 1) * P], xc2[:, c, 4 * n:4 * n + 4, :],
                                                start=(c == 0), stop=(c == 1))
                    last.then_inc(ring_act.filled, 1)
            for n in range(2):
                bank = ring_dve.open(pe, ("out", "l0a", n))
                for c in range(2):
                    pe.wait_ge(*l0a_y.at((c, n)))
                for i in range(HALF):
                    for c in range(2):
                        last = nc.tensor.matmul(bank[:, i * D:(i + 1) * D], y4[:, c, 4 * n + i, :], tout[:, c, :],
                                                start=(c == 0), stop=(c == 1))
                last.then_inc(ring_dve.filled, 1)
            finish_pe(pe, "l0a")

        def finish_pe(pe, s):
            if next_of(s):
                for n in range(2):
                    ln_transpose(pe, next_of(s), halves[n])

        def finish_act(act, s):
            if next_of(s):
                for n in range(2):
                    ln_copy(act, next_of(s), halves[n])

        def finish_pool(pool, s):
            if next_of(s):
                for n in range(2):
                    for r in ((0, 1) if next_of(s) == "l0x" else (0,)):
                        for b in halves[n]:
                            ln_rstd(pool, next_of(s), b, r)

        def finish_dve(dve, s, n):
            if not next_of(s):
                return
            for b in halves[n]:
                ln_stats(dve, next_of(s), b)
            for b in halves[n]:
                ln_xhat(dve, next_of(s), b)
            if next_of(s) == "l0x":
                for b in halves[n]:
                    ln_stats(dve, "l0x", b, 1)
                for b in halves[n]:
                    ln_xhat(dve, "l0x", b, 1)

        def scalar_l0a(act):
            for n in range(2):
                ln_copy(act, "l0a", halves[n])
            act.wait_ge(loaded["l0a"], 16)
            act.wait_ge(tern, 1)
            act.wait_ge(pool_ready, 1)
            for n in range(2):
                for c in range(2):
                    bank = ring_act.take(act, ("xin", c, n))
                    nc.scalar.activation(xin[:, c, 4 * n:4 * n + 4, 3:131], bank.rearrange("p (b t) -> p b t", t=S),
                                         ACT.Identity, scale=scl[:, 0:1], bias=w["l0a_bin"][:, c:c + 1]
                                         ).then_inc(ring_act.emptied, 1)
            for n in range(2):
                for c in range(2):
                    act.wait_ge(*l0a_conv.at((c, n)))
                    nc.scalar.activation(xc2[:, c, 4 * n:4 * n + 4, :], ycv[:, c, 4 * n:4 * n + 4, :], ACT.Tanh,
                                         scale=0.5).then_inc(*l0a_silu.inc((c, n)))
            for n in range(2):
                for c in range(2):
                    bank = ring_act.take(act, ("delta", c, n))
                    nc.scalar.activation(y4[:, c, 4 * n:4 * n + 4, :], bank.rearrange("p (b t) -> p b t", t=S),
                                         ACT.Tanh, scale=qscale[:, 0:1], bias=hbias[:, c:c + 1]
                                         ).then_inc(ring_act.emptied, 1)
            finish_act(act, "l0a")

        def vector_l0a(dve):
            dve.wait_ge(x_loaded, 16)
            for n in range(2):
                for b in halves[n]:
                    ln_stats(dve, "l0a", b)
                for b in halves[n]:
                    ln_xhat(dve, "l0a", b)
            dve.wait_ge(loaded["l0a"], 16)
            for i, (name, _, _) in enumerate(tern_w):
                last = nc.vector.tensor_reduce(absum[:, i:i + 1], w[name], AX.X, ALU.add, apply_absolute_value=True)
            last.then_inc(scales_ready, 1)
            dve.wait_ge(scales_ready, 1)
            bank = ring_dve.take(dve, ("scales",))
            for i, (_, count, _) in enumerate(tern_w):
                last = nc.vector.tensor_scalar(scl[:, i:i + 1], bank[:, i:i + 1], 1.0 / count, 1e-5, ALU.mult, ALU.max)
            last.then_inc(ring_dve.emptied, 1)
            dve.wait_ge(ring_dve.emptied, ring_dve.nth(("scales",)))
            link(dve, nc.vector.tensor_scalar(thr, scl, 0.5, None, ALU.mult))
            link(dve, nc.vector.tensor_scalar(nthr, scl, -0.5, None, ALU.mult))
            link(dve, nc.vector.tensor_scalar(qscale[:, 0:1], scl[:, 1:2], 0.25, None, ALU.mult))
            link(dve, nc.vector.tensor_scalar(qscale[:, 1:2], scl[:, 2:3], 0.25, None, ALU.mult))
            link(dve, nc.vector.tensor_scalar(hbias, w["l0a_bx"], 0.5, None, ALU.mult))
            parts = [(tin, w["l0a_win"][:, 0:256], 0)]
            parts += [(tx[:, c, :], w["l0a_wx"][:, c * 400:c * 400 + 256], 1) for c in range(2)]
            parts += [(tout[:, c, :], w["l0a_wout"][:, c * P:(c + 1) * P], 2) for c in range(2)]
            for m, (dst, src, i) in enumerate(parts):
                low = lowmask[:, m, 0:src.shape[1]]
                link(dve, nc.vector.tensor_scalar(low, src, nthr[:, i:i + 1], None, ALU.is_lt))
                last = nc.vector.scalar_tensor_tensor(out=dst, in0=src, scalar=thr[:, i:i + 1], in1=low,
                                                      op0=ALU.is_gt, op1=ALU.subtract)
            last.then_inc(tern, 1)
            dve.wait_ge(tern, 1)
            for n in range(2):
                for c in range(2):
                    dve.wait_ge(ring_act.emptied, ring_act.nth(("xin", c, n)))
                    y = ycv[:, c, 4 * n:4 * n + 4, :]
                    xi = xin[:, c, 4 * n:4 * n + 4, :]
                    wc = w["l0a_wconv"]
                    link(dve, nc.vector.tensor_scalar(y, xi[:, :, 3:131], wc[:, 4 * c + 3:4 * c + 4],
                                                      w["l0a_bconv"][:, c:c + 1], ALU.mult, ALU.add))
                    for j in range(3):
                        ins = nc.vector.scalar_tensor_tensor(out=y, in0=xi[:, :, j:j + S],
                                                             scalar=wc[:, 4 * c + j:4 * c + j + 1], in1=y,
                                                             op0=ALU.mult, op1=ALU.add)
                        if j < 2:
                            link(dve, ins)
                    ins.then_inc(*l0a_conv.inc((c, n)))
                    dve.wait_ge(*l0a_conv.at((c, n)))
            for n in range(2):
                for c in range(2):
                    dve.wait_ge(*l0a_silu.at((c, n)))
                    t = xc2[:, c, 4 * n:4 * n + 4, :]
                    nc.vector.scalar_tensor_tensor(out=t, in0=t, scalar=1.0, in1=ycv[:, c, 4 * n:4 * n + 4, :],
                                                   op0=ALU.add, op1=ALU.mult).then_inc(*l0a_xc.inc((c, n)))
                    dve.wait_ge(*l0a_xc.at((c, n)))
            for n in range(2):
                for c in range(2):
                    dve.wait_ge(ring_act.emptied, ring_act.nth(("delta", c, n)))
                    dve.wait_ge(*l0a_xc.at((c, n)))
                    t = y4[:, c, 4 * n:4 * n + 4, :]
                    nc.vector.scalar_tensor_tensor(out=t, in0=t, scalar=1.0, in1=xc2[:, c, 4 * n:4 * n + 4, :],
                                                   op0=ALU.add, op1=ALU.mult).then_inc(*l0a_y.inc((c, n)))
                    dve.wait_ge(*l0a_y.at((c, n)))
            for n in range(2):
                bank = ring_dve.take(dve, ("out", "l0a", n))
                xs = x[:, 4 * n:4 * n + 4, :]
                ins = nc.vector.scalar_tensor_tensor(out=xs, in0=bank.rearrange("p (b d) -> p b d", d=D),
                                                     scalar=qscale[:, 1:2], in1=xs, op0=ALU.mult, op1=ALU.add)
                ins.then_inc(ring_dve.emptied, 1)
                dve.wait_ge(ring_dve.emptied, ring_dve.nth(("out", "l0a", n)))
                link(dve, nc.vector.tensor_tensor(xs, xs, spread(w["l0a_bout"], 4), ALU.add))
                finish_dve(dve, "l0a", n)

        def gpsimd_l0a(pool):
            plink(pool, nc.gpsimd.memset(power[:, 0:1], -0.5))
            plink(pool, nc.gpsimd.memset(power[:, 1:2], 0.5))
            plink(pool, nc.gpsimd.memset(xin[:, :, :, 0:3], 0.0))
            plink(pool, nc.gpsimd.memset(xpad[:, :, 0:1], 0.0))
            plink(pool, nc.gpsimd.memset(V[:, :, :], 1.0))
            plink(pool, nc.gpsimd.memset(V9[:, :, :], 1.0))
            nc.gpsimd.memset(V33[:, :, :, :], 1.0).then_inc(pool_ready, 1)
            pool.wait_ge(pool_ready, 1)
            for n in range(2):
                for b in halves[n]:
                    ln_rstd(pool, "l0a", b)
            pool.wait_ge(loaded["small"], 16)
            pool.wait_ge(loaded["sel32"], 16)
            nc.gpsimd.tensor_copy(const_bf[:, widths["sel32"]:], store["small"]).then_inc(const_cast, 1)
            nc.gpsimd.tensor_copy(const_bf[:, 0:widths["sel32"]], store["sel32"]).then_inc(const_cast, 1)
            pool.wait_ge(const_cast, 2)
            finish_pool(pool, "l0a")

        SPEC = {
            "l0x": dict(kind="wide", dh=64, wq="x0_wq", wk="x0_wk", wv="x0_wv", wo="x0_wo", kv="ctx", causal=False,
                        scale=64 ** -0.5),
            "l1a": dict(kind="wide", dh=64, wq="a1_wq", wk="a1_wk", wv="a1_wv", wo="a1_wo", kv="x", causal=True,
                        scale=0.5 / 64, alpha=0.5 ** 0.5 * 2 ** 0.5 / 16),
            "l2a": dict(kind="rope", dh=32, kv="x", causal=False, scale=32 ** -0.5, alpha=0.5),
            "l2x": dict(kind="narrow", dh=8, wq="x2_wq", wk="x2_wk", wv="x2_wv", wo="x2_wo", kv="ctx", causal=False,
                        scale=8 ** -0.5, alpha=1.0, bias=True),
            "l3a": dict(kind="narrow", dh=8, wq="a3_wq", wk="a3_wk", wv="a3_wv", wo="a3_wo", kv="x", causal=True,
                        scale=8 ** -0.5, alpha=1.0),
            "l3x": dict(kind="narrow", dh=8, wq="x3_wq", wk="x3_wk", wv="x3_wv", wo="x3_wo", kv="ctx", causal=False,
                        scale=1.0, qscale=8 ** -0.5, alpha=1.0, masked=True),
        }

        TAIL = {"wide": ((4, "outT"), (5, "out"), (6, "xhat"), (7, "norm"))}
        TAIL["rope"] = TAIL["wide"]
        TAIL["narrow"] = ((4, "back"), (5, "outT"), (6, "out"), (7, "xhat"), (8, "norm"))

        def attention_steps(s):
            U = UNITS[s]
            total = U * B
            kind = SPEC[s]["kind"]
            ahead, ahead_v = {"wide": (2, 0), "narrow": (3, None), "rope": (4, 1)}[kind]
            plan = {}
            for b in range(B):
                first = U * b - 1
                plan.setdefault(max(first - ahead, -1), []).append(("project", b, 0))
                if ahead_v is not None:
                    plan.setdefault(max(first - ahead_v, -1), []).append(("project_v", b, 0))
                last = U * b + U - 1
                for d, step in TAIL[kind]:
                    plan.setdefault(last + d, []).append((step, b, 0))
            for step in plan.pop(-1):
                yield step
            yield "score", 0, 0
            for t in range(total + TAIL[kind][-1][0]):
                if t + 1 < total:
                    yield "score", (t + 1) // U, (t + 1) % U
                if t < total:
                    yield "softmax", t // U, t % U
                for step in plan.pop(t, []):
                    yield step
                if 0 <= t - 2 < total:
                    yield "transpose", (t - 2) // U, (t - 2) % U
                if t < total:
                    yield "exp", t // U, t % U
                if 0 <= t - 3 < total:
                    yield "value", (t - 3) // U, (t - 3) % U
                    if kind == "narrow" and (t - 3) % U == U - 1:
                        yield "copy", (t - 3) // U, 0
            assert not plan

        src_of = {"ctx": lambda s: ctxT, "x": lambda s: xT_of[s]}
        mask01 = big[0][:, 0, :, 0:S]
        maskrow = sb("maskrow", [P, B, S], BF16)
        mask_i = xpad[:, :, :].rearrange("p b t -> p (b t)").bitcast(I32)[:, 0:TOK].rearrange("p (b t) -> p b t", t=S)
        kraw = sb("kraw", [P, 3, 2, S])
        kmask = sb("kmask", [P, 3, 2, 4, S])
        rowconst = kmask.rearrange("p m a c s -> p m (a c s)")
        headrows = rowconst[:, 0, :]
        notfirst, negfirst = (rowconst[0:8, i, :] for i in (1, 2))
        rope1 = V[:, 0, 0:1024].rearrange("p (a c s) -> p a c s", a=2, s=S)
        rope2 = V[:, 1, 0:1024].rearrange("p (a c s) -> p a c s", a=2, s=S)
        gate2 = kT[:, 1, :, :].rearrange("p (a c) s -> p a (c s)", a=4)
        tgate = sb("tgate", [P, 1])

        def buf(s, b):
            return b % (2 if SPEC[s]["kind"] == "wide" else 3)

        def heads_of(s, g):
            if SPEC[s]["kind"] == "wide":
                return slice(8 * (g // 2) + g % 2, 8 * (g // 2) + g % 2 + 7, 2)
            return slice(4 * g, 4 * g + 4)

        def q3(b):
            return qT[:, b % 4 // 2, b % 4 % 2 * 4:b % 4 % 2 * 4 + 4, :]

        def kmask_of(b):
            return kmask[:, b % 4, :, :, :] if b % 4 < 3 else kT[:, 0, :, :].rearrange("p (a c) s -> p a c s", a=2)

        def v_view(s, b):
            return {"wide": V[:, b % 2, :].rearrange("p (h e) -> p h e", e=65), "narrow": V9[:, b % 4, 0:144].rearrange("p (h e) -> p h e", e=9),
                    "rope": V33[:, b % 4, :, :]}[SPEC[s]["kind"]]

        def seq_bank(b):
            return psum[:, 2 + b % 2, :]

        avT = O[:, :, 512:1024]

        def tensor_attention(pe, s):
            pe.wait_ge(const_cast, 2)
            sp = SPEC[s]
            kind, kvT = sp["kind"], src_of[sp["kv"]](s)
            xT = xT_of[s]
            pe.wait_ge(loaded[s], 16)
            pe.wait_ge(ctx_loaded, 32)
            if kind == "narrow":
                pe.wait_ge(ring_dve.emptied, len(ring_dve.use))
            for step, b, g in attention_steps(s):
                if step == "project" and kind == "wide":
                    xT_wait(pe, s, b)
                    for ring, what, wt, src in ((ring_act, "q", sp["wq"], xT), (ring_dve, "k", sp["wk"], kvT)):
                        for i in range(2):
                            bank = ring.open(pe, (what, s, b, i))
                            for c in range(4):
                                last = nc.tensor.matmul(bank[:, c * S:(c + 1) * S],
                                                        w[wt][:, (4 * i + c) * P:(4 * i + c + 1) * P], src[:, b, :],
                                                        start=True, stop=True)
                            last.then_inc(ring.filled, 1)
                elif step == "project_v" and kind == "wide":
                    for i in range(2):
                        bank = ring_act.open(pe, ("v", s, b, i))
                        nc.tensor.matmul(bank, kvT[:, b, :], w[sp["wv"]][:, i * 512:(i + 1) * 512], start=True,
                                         stop=True).then_inc(ring_act.filled, 1)
                elif step == "project" and kind == "narrow":
                    xT_wait(pe, s, b)
                    bank = ring_act.open(pe, ("qkv", s, b))
                    nc.tensor.matmul(bank[:, 0:S], w[sp["wq"]], xT[:, b, :], start=True, stop=True)
                    nc.tensor.matmul(bank[:, S:2 * S], w[sp["wk"]], kvT[:, b, :], start=True, stop=True)
                    last = nc.tensor.matmul(bank[:, 2 * S:3 * S], kvT[:, b, :], w[sp["wv"]], start=True,
                                            stop=not sp.get("bias"))
                    if sp.get("bias"):
                        last = nc.tensor.matmul(bank[:, 2 * S:3 * S], w["ones"][0:1, :], w["x2_bv"], start=False,
                                                stop=True)
                    last.then_inc(ring_act.filled, 1)
                elif step == "project":
                    xT_wait(pe, s, b)
                    for what, wt in (("q", "a2_wq4"), ("k", "a2_wk4")):
                        bank = ring_dve.open(pe, (what, s, b))
                        for c in range(4):
                            last = nc.tensor.matmul(bank[:, c * S:(c + 1) * S], w[wt][:, c * P:(c + 1) * P],
                                                    xT[:, b, :], start=True, stop=True)
                        last.then_inc(ring_dve.filled, 1)
                elif step == "project_v" and kind == "rope":
                    bank = ring_dve.open(pe, ("vg", s, b))
                    nc.tensor.matmul(bank[:, 0:320], xT[:, b, :], w["a2_wvg"], start=True, stop=True).then_inc(
                        ring_dve.filled, 1)
                elif step == "score":
                    if g == 0:
                        if kind == "wide":
                            pe.wait_ge(ring_act.emptied, ring_act.nth(("q", s, b, 1)))
                            pe.wait_ge(ring_dve.emptied, ring_dve.nth(("k", s, b, 1)))
                        else:
                            if kind == "narrow":
                                pe.wait_ge(ring_act.emptied, ring_act.nth(("qkv", s, b)))
                            else:
                                pe.wait_ge(ring_dve.emptied, ring_dve.nth(("k", s, b)))
                            pe.wait_ge(*k_masked.at((s, b)))
                    bank = ring_score.open(pe, ("S", s, b, g))
                    open_ = True
                    if sp["causal"]:
                        nc.tensor.matmul(bank, w["ident_bf"], spread(w["causal_bf"], 4), start=True, stop=False)
                        open_ = False
                    if sp.get("masked"):
                        if b == 0 and g == 0:
                            pe.wait_ge(mask_ready, 1)
                        nc.tensor.matmul(bank, w["ones_bf"], spread(maskrow[:, b, :], 4), start=True, stop=False)
                        open_ = False
                    if kind == "wide":
                        i, p = g // 2, g % 2
                        for c in range(4):
                            last = nc.tensor.matmul(bank[:, c * S:(c + 1) * S], qT[64 * p:64 * p + 64, b % 2, 4 * i + c, :],
                                                    kT[64 * p:64 * p + 64, b % 2, 4 * i + c, :], start=open_,
                                                    stop=open_ or c == 3)
                    elif kind == "narrow":
                        low = 64 * (g // 2)
                        last = nc.tensor.matmul(bank, q3(b)[low:low + 64, 0, :],
                                                kmask_of(b)[low:low + 64, g % 2, :, :], start=open_, stop=True)
                    else:
                        last = nc.tensor.matmul(bank, q3(b)[:, g, :], kmask_of(b)[:, g, :, :], start=True, stop=True)
                    last.then_inc(ring_score.filled, 1)
                elif step == "transpose":
                    bank = ring_prob.open(pe, ("T", s, b, g))
                    pe.wait_ge(*exped.at((s, b, g)))
                    n = units.index((s, b, g)) % 4
                    for c in range(4):
                        last = nc.tensor.transpose(bank[:, c * S:(c + 1) * S], prob[:, n, c, :], w["ident"])
                    last.then_inc(ring_prob.filled, 1)
                elif step == "value" and kind == "narrow":
                    bank = seq_bank(b)
                    if g == 0 and b >= 2:
                        pe.wait_ge(*out_added.at((s, b - 2)))
                    pe.wait_ge(ring_prob.emptied, ring_prob.nth(("T", s, b, g)))
                    n = units.index((s, b, g)) % 2
                    for c in range(4):
                        h = 4 * g + c
                        last = nc.tensor.matmul(bank[32 * c:32 * c + 32, g * S:(g + 1) * S],
                                                V9[:, b % 4, 9 * h:9 * h + 32], probT[:, n, c, :], start=True,
                                                stop=True)
                    if g == 3:
                        last.then_inc(*avT_filled.inc((s, b)))
                elif step == "back":
                    pe.wait_ge(*avT_copied.at((s, b)))
                    for i in range(4):
                        last = nc.tensor.transpose(seq_bank(b)[:, i * S:(i + 1) * S], avT[:, b % 2, i * S:(i + 1) * S],
                                                   w["ident"])
                    last.then_inc(*av_filled.inc((s, b)))
                elif step == "value":
                    bank = ring_dve.open(pe, ("AV", s, b, g))
                    pe.wait_ge(ring_prob.emptied, ring_prob.nth(("T", s, b, g)))
                    if kind == "wide" and g == 0:
                        pe.wait_ge(ring_act.emptied, ring_act.nth(("v", s, b, 1)))
                    if kind == "rope" and g == 0:
                        pe.wait_ge(ring_dve.emptied, ring_dve.nth(("vg", s, b)))
                    n = units.index((s, b, g)) % 2
                    e = sp["dh"] + 1
                    hs = heads_of(s, g)
                    for c in range(4):
                        h = g if kind == "rope" else hs.start + (hs.step or 1) * c
                        last = nc.tensor.matmul(bank[:, c * e:(c + 1) * e], probT[:, n, c, :],
                                                v_view(s, b)[:, h, :], start=True, stop=True)
                    last.then_inc(ring_dve.filled, 1)
                elif step == "outT":
                    chunks = {"wide": 8, "rope": 2, "narrow": 1}[kind]
                    if kind == "narrow":
                        pe.wait_ge(*av_scaled.at((s, b)))
                    else:
                        pe.wait_ge(ring_dve.emptied, ring_dve.nth(("AV", s, b, UNITS[s] - 1)))
                    for i in range(0, chunks, 4):
                        bank = ring_act.open(pe, ("OT", s, b, i))
                        for c in range(i, min(i + 4, chunks)):
                            last = nc.tensor.transpose(bank[:, (c - i) * S:(c - i + 1) * S],
                                                       O[:, b % 2, c * P:(c + 1) * P], w["ident"])
                        last.then_inc(ring_act.filled, 1)
                elif step == "out":
                    chunks = {"wide": 8, "rope": 2, "narrow": 1}[kind]
                    wo = {"rope": "a2_wo"}.get(kind) or sp["wo"]
                    bank = seq_bank(b) if kind == "narrow" else ring_dve.open(pe, ("out", s, b))
                    bias = {"l0x": "x0_bout", "l2x": "x2_bo"}.get(s)
                    pe.wait_ge(ring_act.emptied, ring_act.nth(("OT", s, b, 4 * ((chunks - 1) // 4))))
                    for c in range(chunks):
                        last = nc.tensor.matmul(bank[:, 0:D], OT[:, b % 2, c, :], w[wo][:, c * D:(c + 1) * D],
                                                start=(c == 0), stop=(c == chunks - 1) and not bias)
                    if bias:
                        last = nc.tensor.matmul(bank[:, 0:D], w["ones"][0:1, :], w[bias], start=False, stop=True)
                    if kind == "narrow":
                        last.then_inc(*out_filled.inc((s, b)))
                    else:
                        last.then_inc(ring_dve.filled, 1)
                elif step == "norm" and next_of(s):
                    ln_transpose(pe, next_of(s), (b,))
            if kind == "narrow":
                for b in (B - 2, B - 1):
                    pe.wait_ge(*out_added.at((s, b)))

        def scalar_attention(act, s):
            sp = SPEC[s]
            kind = sp["kind"]
            act.wait_ge(loaded[s], 16)
            if s == "l0x":
                nc.scalar.activation(tgate[:, :], w["x0_gate"], ACT.Tanh).then_inc(gate_l0x, 1)
            for step, b, g in attention_steps(s):
                if step == "project" and kind == "wide":
                    for i in range(2):
                        bank = ring_act.take(act, ("q", s, b, i))
                        nc.scalar.activation(qT[:, b % 2, 4 * i:4 * i + 4, :], bank.rearrange("p (c t) -> p c t", t=S),
                                             ACT.Copy).then_inc(ring_act.emptied, 1)
                elif step == "project_v" and kind == "wide":
                    for i in range(2):
                        bank = ring_act.take(act, ("v", s, b, i))
                        nc.scalar.activation(v_view(s, b)[:, 8 * i:8 * i + 8, 0:64],
                                             bank.rearrange("p (h e) -> p h e", e=64), ACT.Copy
                                             ).then_inc(ring_act.emptied, 1)
                elif step == "project" and kind == "narrow":
                    bank = ring_act.take(act, ("qkv", s, b))
                    if sp.get("bias"):
                        nc.scalar.activation(kraw[:, b % 3, 0, :], bank[:, S:2 * S], ACT.Identity, bias=w["x2_bk"])
                        nc.scalar.activation(q3(b)[:, 0, :], bank[:, 0:S], ACT.Identity, bias=w["x2_bq"])
                    else:
                        nc.scalar.activation(kraw[:, b % 3, 0, :], bank[:, S:2 * S], ACT.Copy)
                        nc.scalar.activation(q3(b)[:, 0, :], bank[:, 0:S], ACT.Copy, scale=sp.get("qscale", 1.0))
                    nc.scalar.activation(v_view(s, b)[:, :, 0:8], bank[:, 2 * S:3 * S].rearrange("p (h e) -> p h e", e=8),
                                         ACT.Copy).then_inc(ring_act.emptied, 1)
                elif step == "project_v":
                    act.wait_ge(ring_dve.filled, ring_dve.nth(("vg", s, b)))
                    bank = ring_dve.bank(("vg", s, b))
                    nc.scalar.activation(v_view(s, b)[:, :, 0:32], bank[:, 0:64].rearrange("p (h e) -> p h e", e=32),
                                         ACT.Copy)
                    nc.scalar.activation(gate2[:, b % 4, :], bank[:, 64:320], ACT.Tanh, scale=0.5).then_inc(act_side, 1)
                elif step == "exp":
                    n = units.index((s, b, g)) % 4
                    act.wait_ge(ring_score.emptied, ring_score.nth(("S", s, b, g)))
                    nc.scalar.activation(prob[:, n, :, :], prob[:, n, :, :], ACT.Exp, scale=sp["scale"]
                                         ).then_inc(*exped.inc((s, b, g)))
                elif step == "transpose":
                    bank = ring_prob.take(act, ("T", s, b, g))
                    n = units.index((s, b, g)) % 2
                    nc.scalar.activation(probT[:, n, :, :], bank.rearrange("p (c t) -> p c t", t=S), ACT.Copy
                                         ).then_inc(ring_prob.emptied, 1)
                elif step == "copy":
                    act.wait_ge(*avT_filled.at((s, b)))
                    nc.scalar.activation(avT[:, b % 2, :], seq_bank(b), ACT.Copy).then_inc(*avT_copied.inc((s, b)))
                elif step == "outT":
                    chunks = {"wide": 8, "rope": 2, "narrow": 1}[kind]
                    for i in range(0, chunks, 4):
                        m = min(4, chunks - i)
                        bank = ring_act.take(act, ("OT", s, b, i))
                        nc.scalar.activation(OT[:, b % 2, i:i + m, :],
                                             bank[:, 0:m * S].rearrange("p (c t) -> p c t", t=S), ACT.Copy
                                             ).then_inc(ring_act.emptied, 1)
                elif step == "norm" and next_of(s):
                    ln_copy(act, next_of(s), (b,))

        def vector_attention(dve, s):
            dve.wait_ge(const_cast, 2)
            sp = SPEC[s]
            kind = sp["kind"]
            dve.wait_ge(pool_ready, 1)
            if sp.get("masked"):
                dve.wait_ge(mask_loaded, 16)
                link(dve, nc.vector.tensor_scalar(mask01, mask_i[:, :, :], 0, None, ALU.not_equal))
                nc.vector.tensor_scalar(maskrow[:, :, :], mask01, 1.0, w["bigparts"], ALU.subtract,
                                        ALU.mult).then_inc(mask_ready, 1)
                dve.wait_ge(mask_ready, 1)
            if s == "l0x":
                dve.wait_ge(gate_l0x, 1)
            for step, b, g in attention_steps(s):
                if step == "project" and kind == "wide":
                    for i in range(2):
                        bank = ring_dve.take(dve, ("k", s, b, i))
                        nc.vector.tensor_copy(kT[:, b % 2, 4 * i:4 * i + 4, :], bank.rearrange("p (c t) -> p c t", t=S)
                                              ).then_inc(ring_dve.emptied, 1)
                        dve.wait_ge(ring_dve.emptied, ring_dve.taken)
                elif step == "project" and kind == "rope":
                    for j, what in enumerate(("q", "k")):
                        bank = ring_dve.take(dve, (what, s, b)).rearrange("p (c t) -> p c t", t=S)
                        if j == 0 and b >= 2:
                            dve.wait_ge(*k_masked.at((s, b - 2)))
                        link(dve, nc.vector.tensor_tensor(rope1[:, b % 2, 2 * j:2 * j + 2, :], bank[:, 0:2, :],
                                                spread(w["cos"], 2), ALU.mult))
                        nc.vector.tensor_tensor(rope2[:, b % 2, 2 * j:2 * j + 2, :], bank[:, 2:4, :],
                                                spread(w["sin"], 2), ALU.mult).then_inc(ring_dve.emptied, 1)
                        dve.wait_ge(ring_dve.emptied, ring_dve.taken)
                elif step == "project_v" and kind == "rope":
                    bank = ring_dve.take(dve, ("vg", s, b))
                    dve.wait_ge(act_side, b + 1)
                    nc.vector.scalar_tensor_tensor(out=gate2[:, b % 4, :], in0=gate2[:, b % 4, :], scalar=1.0,
                                                   in1=bank[:, 64:320], op0=ALU.add, op1=ALU.mult
                                                   ).then_inc(ring_dve.emptied, 1)
                    dve.wait_ge(ring_dve.emptied, ring_dve.taken)
                elif step == "softmax":
                    bank = ring_score.take(dve, ("S", s, b, g)).rearrange("p (c t) -> p c t", t=S)
                    n = units.index((s, b, g)) % 4
                    link(dve, nc.vector.tensor_reduce(nmax[:, n, :], bank, AX.X, ALU.max))
                    u = units.index((s, b, g))
                    if u >= 4:
                        dve.wait_ge(ring_prob.filled, ring_prob.nth(("T",) + units[u - 4]))
                    nc.vector.tensor_tensor(prob[:, n, :, :], bank, spread(nmax[:, n, :], S, 2), ALU.subtract
                                            ).then_inc(ring_score.emptied, 1)
                    dve.wait_ge(ring_score.emptied, ring_score.taken)
                elif step == "back":
                    dve.wait_ge(*av_filled.at((s, b)))
                    av = seq_bank(b).rearrange("p (h e) -> p h e", e=32)
                    den = small[:, 0:16]
                    link(dve, nc.vector.reciprocal(den, av[:, :, 8:9].rearrange("p h e -> p (h e)")))
                    nc.vector.tensor_tensor(O[:, b % 2, 0:128].rearrange("p (h e) -> p h e", e=8), av[:, :, 0:8],
                                            spread(den, 8, 2), ALU.mult).then_inc(*av_scaled.inc((s, b)))
                    dve.wait_ge(*av_scaled.at((s, b)))
                elif step == "value" and kind != "narrow":
                    e = sp["dh"] + 1
                    bank = ring_dve.take(dve, ("AV", s, b, g))[:, 0:4 * e].rearrange("p (c e) -> p c e", e=e)
                    link(dve, nc.vector.reciprocal(rden, bank[:, :, e - 1:e].rearrange("p c e -> p (c e)")))
                    o = O[:, b % 2, 0:{"wide": 1024, "rope": 256, "narrow": 128}[kind]].rearrange(
                        "p (h e) -> p h e", e=e - 1)[:, heads_of(s, g), :]
                    ins = nc.vector.tensor_tensor(o, bank[:, :, 0:e - 1], spread(rden, e - 1, 2), ALU.mult)
                    if kind == "rope":
                        link(dve, ins)
                        if g == 0:
                            dve.wait_ge(ring_dve.emptied, ring_dve.nth(("vg", s, b)))
                        ins = nc.vector.tensor_tensor(
                            o, o, gate2[:, b % 4, :].rearrange("p (h e) -> p h e", e=32)[:, heads_of(s, g), :], ALU.mult)
                    ins.then_inc(ring_dve.emptied, 1)
                    dve.wait_ge(ring_dve.emptied, ring_dve.taken)
                elif step == "out":
                    if kind == "narrow":
                        dve.wait_ge(*out_filled.at((s, b)))
                        bank = seq_bank(b)
                    else:
                        bank = ring_dve.take(dve, ("out", s, b))
                    scalar = tgate[:, :] if s == "l0x" else float(sp["alpha"])
                    ins = nc.vector.scalar_tensor_tensor(out=x[:, b, :], in0=bank[:, 0:D], scalar=scalar,
                                                         in1=x[:, b, :], op0=ALU.mult, op1=ALU.add)
                    if kind == "narrow":
                        ins.then_inc(*out_added.inc((s, b)))
                        dve.wait_ge(*out_added.at((s, b)))
                    else:
                        ins.then_inc(ring_dve.emptied, 1)
                        dve.wait_ge(ring_dve.emptied, ring_dve.nth(("out", s, b)))
                    if next_of(s):
                        ln_stats(dve, next_of(s), b)
                elif step == "xhat" and next_of(s):
                    ln_xhat(dve, next_of(s), b)

        def gpsimd_attention(pool, s):
            sp = SPEC[s]
            kind = sp["kind"]
            for step, b, g in attention_steps(s):
                if step == "project" and kind == "narrow":
                    pool.wait_ge(ring_act.emptied, ring_act.nth(("qkv", s, b)))
                    k = kraw[:, b % 3, 0, :]
                    if sp.get("masked"):
                        if b == 0:
                            pool.wait_ge(mask_ready, 1)
                        plink(pool, nc.gpsimd.tensor_tensor(k, k, mask01[:, b, :], ALU.mult))
                    nc.gpsimd.tensor_tensor(kmask_of(b).rearrange("p a c s -> p (a c) s"), spread(k, 8),
                                            spread(w["mask8"], S, 2),
                                            ALU.mult).then_inc(*k_masked.inc((s, b)))
                    pool.wait_ge(*k_masked.at((s, b)))
                elif step == "project" and kind == "rope":
                    pool.wait_ge(ring_dve.emptied, ring_dve.nth(("k", s, b)))
                    plink(pool, nc.gpsimd.tensor_tensor(q3(b)[:, 0:2, :], rope1[:, b % 2, 0:2, :], rope2[:, b % 2, 0:2, :], ALU.add))
                    plink(pool, nc.gpsimd.tensor_tensor(kraw[:, b % 3, :, :], rope1[:, b % 2, 2:4, :],
                                                        rope2[:, b % 2, 2:4, :], ALU.add))
                    plink(pool, nc.gpsimd.tensor_tensor(kmask_of(b)[:, 0, :, :], spread(kraw[:, b % 3, 0, :], 4),
                                            spread(w["mask32"], S, 2), ALU.mult))
                    nc.gpsimd.tensor_tensor(kmask_of(b)[:, 1, :, :], spread(kraw[:, b % 3, 1, :], 4),
                                            spread(w["mask32"], S, 2), ALU.mult).then_inc(*k_masked.inc((s, b)))
                    pool.wait_ge(*k_masked.at((s, b)))
                elif step == "out" and next_of(s):
                    ln_rstd(pool, next_of(s), b)

        xr = big[0][:, 0, :, 0:S]
        xk = big[0][:, 1, :, 0:S]
        xd = big[1][:, 0, :, 0:S]
        kact = big[1][:, 1, :, 0:S]
        rgate = O[:, 0, :].rearrange("p (b d) -> p b d", d=D)

        def tensor_l0f(pe):
            pe.wait_ge(loaded["l0f"], 16)
            for n in range(2):
                pe.wait_ge(*l0f_mix.at((n,)))
                bank = ring_dve.open(pe, ("k", "l0f", n))
                nc.tensor.matmul(bank, w["f0_wk"], xk[:, 4 * n:4 * n + 4, :], start=True, stop=True).then_inc(
                    ring_dve.filled, 1)
                bank = ring_act.open(pe, ("r", n))
                for i in range(4):
                    last = nc.tensor.matmul(bank[:, i * D:(i + 1) * D], xr[:, 4 * n + i, :], w["f0_wr"], start=True,
                                            stop=True)
                last.then_inc(ring_act.filled, 1)
            for n in range(2):
                bank = ring_dve.open(pe, ("out", "l0f", n))
                pe.wait_ge(ring_dve.emptied, ring_dve.nth(("k", "l0f", n)))
                for i in range(4):
                    last = nc.tensor.matmul(bank[:, i * D:(i + 1) * D], kact[:, 4 * n + i, :], w["f0_wv"], start=True,
                                            stop=True)
                last.then_inc(ring_dve.filled, 1)
            finish_pe(pe, "l0f")

        def scalar_l0f(act):
            for n in range(2):
                bank = ring_act.take(act, ("r", n))
                nc.scalar.activation(rgate[:, 4 * n:4 * n + 4, :], bank.rearrange("p (b t) -> p b t", t=S), ACT.Tanh,
                                     scale=0.5).then_inc(ring_act.emptied, 1)
            finish_act(act, "l0f")

        def vector_l0f(dve):
            dve.wait_ge(loaded["l0f"], 16)
            for n in range(2):
                dve.wait_ge(ring_act.emptied, xT_use("l0f", 4 * n + 3))
                now, prev = xpad[:, 4 * n:4 * n + 4, 1:S + 1], xpad[:, 4 * n:4 * n + 4, 0:S]
                d = xd[:, 4 * n:4 * n + 4, :]
                link(dve, nc.vector.tensor_tensor(d, now, prev, ALU.subtract))
                link(dve, nc.vector.scalar_tensor_tensor(out=xk[:, 4 * n:4 * n + 4, :], in0=d, scalar=w["f0_muk"], in1=prev,
                                               op0=ALU.mult, op1=ALU.add))
                nc.vector.scalar_tensor_tensor(out=xr[:, 4 * n:4 * n + 4, :], in0=d, scalar=w["f0_mur"], in1=prev,
                                               op0=ALU.mult, op1=ALU.add).then_inc(*l0f_mix.inc((n,)))
                dve.wait_ge(*l0f_mix.at((n,)))
            for n in range(2):
                bank = ring_dve.take(dve, ("k", "l0f", n))
                kk = kact[:, 4 * n:4 * n + 4, :]
                link(dve, nc.vector.tensor_scalar(kk, bank.rearrange("p (b t) -> p b t", t=S), 0.0, None, ALU.max))
                nc.vector.tensor_tensor(kk, kk, kk, ALU.mult).then_inc(ring_dve.emptied, 1)
                dve.wait_ge(ring_dve.emptied, ring_dve.taken)
            for n in range(2):
                bank = ring_dve.take(dve, ("out", "l0f", n))
                dve.wait_ge(ring_act.emptied, ring_act.nth(("r", n)))
                r = rgate[:, 4 * n:4 * n + 4, :]
                xs = x[:, 4 * n:4 * n + 4, :]
                link(dve, nc.vector.scalar_tensor_tensor(out=r, in0=r, scalar=1.0,
                                                         in1=bank.rearrange("p (b t) -> p b t", t=S), op0=ALU.add,
                                                         op1=ALU.mult))
                nc.vector.scalar_tensor_tensor(out=xs, in0=r, scalar=0.5, in1=xs, op0=ALU.mult, op1=ALU.add
                                               ).then_inc(ring_dve.emptied, 1)
                dve.wait_ge(ring_dve.emptied, ring_dve.nth(("out", "l0f", n)))
                finish_dve(dve, "l0f", n)

        def gpsimd_l0f(pool):
            finish_pool(pool, "l0f")

        rF, rI = O[0:8, 0, :], O[0:8, 1, :]
        rA, rCS = (qT[0:8, i, :, :].rearrange("p c s -> p (c s)") for i in range(2))
        rG = kT[0:8, 0, :, :].rearrange("p c s -> p (c s)")
        rM_all = kT[:, 1, :, :].rearrange("p c s -> p (c s)")
        rM = rM_all[0:8, :]
        qm = [big[0][:, i, :, 0:S] for i in range(2)]
        DC = [big[1][:, i, :, 0:S] for i in range(2)]
        hbuf = OT[:, 0, 0:2, :]
        wkv = small[:, 8:24].rearrange("p (g h) -> p g h", g=2)
        gcol, floor = wcol[:, :, 0:8], wcol[:, :, 8:16]

        def half(n):
            return slice(512 * n, 512 * n + 512)

        def lstm_steps():
            yield "gates", 0
            yield "scan", 0
            yield "scan2", 0
            yield "turn", 0
            yield "turned", 0
            for t in range(B + 4):
                if t < B:
                    yield "weights", t
                if t == 3:
                    yield "turn", 1
                if 0 <= t - 1 < B:
                    yield "value", t - 1
                if 0 <= t - 2 < B:
                    yield "normalise", t - 2
                if t == 3:
                    yield "turned", 1
                if 0 <= t - 3 < B:
                    yield "add", t - 3
                if 0 <= t - 4 < B:
                    yield "norm", t - 4
                if t < B:
                    yield "apply", t
                if t in (0, 1):
                    yield ("scan", "scan2")[t], 1

        def tensor_l1x(pe):
            pe.wait_ge(loaded["l1x"], 16)
            pe.wait_ge(rowconst_loaded, 16)
            pe.wait_ge(lstm_wkv, 1)
            for step, b in lstm_steps():
                if step == "gates":
                    for n in range(2):
                        xT_wait(pe, "l1x", halves[n][-1])
                        for ring, gate in ((ring_dve, "f"), (ring_act, "i")):
                            bank = ring.open(pe, (gate, "l1x", n))
                            nc.tensor.matmul(bank[0:8, :], w[f"x1_w{gate}"][:, 0:8],
                                             xT_of["l1x"][:, 4 * n:4 * n + 4, :], start=True, stop=False)
                            nc.tensor.matmul(bank[0:8, :], wkv[:, "fi".index(gate), :], ctxT[:, 4 * n:4 * n + 4, :],
                                             start=False, stop=True).then_inc(ring.filled, 1)
                elif step == "turn":
                    bank = ring_dve.open(pe, ("turn", b))
                    pe.wait_ge(*lstm_G.at((b,)))
                    pe.wait_ge(*lstm_expA.at((b,)))
                    for i in range(4):
                        for j, row in enumerate((rG, rA)):
                            last = nc.tensor.transpose(bank[:, 16 * i + 8 * j:16 * i + 8 * j + 8],
                                                       row[:, 512 * b + i * S:512 * b + (i + 1) * S],
                                                       w["ident"][0:8, 0:8])
                    last.then_inc(ring_dve.filled, 1)
                elif step == "weights":
                    if b % HALF == 0:
                        pe.wait_ge(*lstm_M.at((b // HALF,)))
                    for i in range(2):
                        bank = ring_act.open(pe, ("arg", b, i))
                        nc.tensor.matmul(bank, w["ident_bf"], spread(w["causalT_bf"], 4), start=True, stop=False)
                        for c in range(4):
                            h = 4 * i + c
                            last = nc.tensor.matmul(bank[:, c * S:(c + 1) * S], headrows[:, h * S:(h + 1) * S],
                                                    rM_all[:, b * S:(b + 1) * S], start=False, stop=(c == 3))
                        last.then_inc(ring_act.filled, 1)
                    pe.wait_ge(*lstm_q.at((b,)))
                    for i in range(2):
                        bank = ring_score.open(pe, ("qk", b, i))
                        nc.tensor.matmul(bank, ctxT[:, b, :], qm[b % 2][:, 4 * i:4 * i + 4, :], start=True, stop=True
                                         ).then_inc(ring_score.filled, 1)
                elif step == "value":
                    bank = ring_dve.open(pe, ("h", b))
                    pe.wait_ge(ring_score.emptied, ring_score.nth(("qk", b, 1)))
                    if b == 0:
                        pe.wait_ge(v_ready, 1)
                    for h in range(8):
                        last = nc.tensor.matmul(bank[:, 17 * h:17 * h + 17], DC[b % 2][:, h, :], V17[:, b, h, :],
                                                start=True, stop=True)
                    last.then_inc(ring_dve.filled, 1)
                elif step == "norm" and next_of("l1x"):
                    ln_transpose(pe, next_of("l1x"), (b,))

        def scalar_l1x(act):
            for step, b in lstm_steps():
                if step == "gates":
                    for n in range(2):
                        bank = ring_act.take(act, ("i", "l1x", n))
                        nc.scalar.activation(rI[:, half(n)], bank[0:8, :], ACT.Identity, bias=w["x1_bi"]).then_inc(
                            ring_act.emptied, 1)
                    for n in range(2):
                        act.wait_ge(*lstm_abs.at((n,)))
                        alink(act, nc.scalar.activation(rA[:, half(n)], rA[:, half(n)], ACT.Exp, scale=-1.0))
                    for n in range(2):
                        nc.scalar.activation(rA[:, half(n)], rA[:, half(n)], ACT.Ln, bias=1.0).then_inc(
                            *lstm_log.inc((n,)))
                elif step == "scan2":
                    act.wait_ge(*lstm_A.at((b,)))
                    nc.scalar.activation(rA[:, half(b)], rA[:, half(b)], ACT.Exp, scale=-1.0).then_inc(
                        *lstm_expA.inc((b,)))
                elif step == "weights":
                    if b % HALF == 0:
                        act.wait_ge(ring_dve.emptied, ring_dve.nth(("turn", b // HALF)))
                    for i in range(2):
                        bank = ring_act.take(act, ("arg", b, i))
                        if b >= 2 and i == 0:
                            act.wait_ge(ring_dve.filled, ring_dve.nth(("h", b - 2)))
                        for c in range(4):
                            h = 4 * i + c
                            last = nc.scalar.activation(DC[b % 2][:, h, :], bank[:, c * S:(c + 1) * S], ACT.Exp,
                                                        bias=gcol[:, b, h:h + 1])
                        last.then_inc(ring_act.emptied, 1)
                elif step == "norm" and next_of("l1x"):
                    ln_copy(act, next_of("l1x"), (b,))

        def vector_l1x(dve):
            dve.wait_ge(loaded["l1x"], 16)
            dve.wait_ge(rowconst_loaded, 16)
            for i, gate in enumerate("fi"):
                ins = nc.vector.tensor_tensor(wkv[:, i, :], w[f"x1_w{gate}"][:, 8:16], w[f"x1_w{gate}"][:, 16:24],
                                              ALU.add)
            ins.then_inc(lstm_wkv, 1)
            dve.wait_ge(lstm_wkv, 1)
            for step, b in lstm_steps():
                if step == "gates":
                    for n in range(2):
                        bank = ring_dve.take(dve, ("f", "l1x", n))
                        nc.vector.tensor_scalar(rF[:, half(n)], bank[0:8, :], w["x1_bf"], None, ALU.add
                                                ).then_inc(ring_dve.emptied, 1)
                        dve.wait_ge(ring_dve.emptied, ring_dve.taken)
                        nc.vector.scalar_tensor_tensor(out=rA[:, half(n)], in0=rF[:, half(n)], scalar=-1.0,
                                                       in1=rF[:, half(n)], op0=ALU.mult, op1=ALU.max
                                                       ).then_inc(*lstm_abs.inc((n,)))
                        dve.wait_ge(*lstm_abs.at((n,)))
                    link(dve, nc.vector.tensor_scalar(rF, rF, 0.0, None, ALU.min))
                elif step == "scan":
                    f, a, cs = rF[:, half(b)], rA[:, half(b)], rCS[:, half(b)]
                    dve.wait_ge(*lstm_log.at((b,)))
                    link(dve, nc.vector.tensor_tensor(f, f, a, ALU.subtract))
                    link(dve, nc.vector.tensor_tensor_scan(cs, notfirst[:, 0:512], f, 0.0, ALU.mult, ALU.add))
                    dve.wait_ge(ring_act.emptied, ring_act.nth(("i", "l1x", b)))
                    nc.vector.tensor_tensor(rG[:, half(b)], rI[:, half(b)], cs, ALU.subtract).then_inc(
                        *lstm_G.inc((b,)))
                    dve.wait_ge(*lstm_G.at((b,)))
                elif step == "scan2":
                    m = rM[:, half(b)]
                    dve.wait_ge(lstm_cleared, 1)
                    link(dve, nc.vector.tensor_tensor_scan(m, negfirst[:, 0:512], rG[:, half(b)], NEG, ALU.add,
                                                           ALU.max))
                    nc.vector.tensor_tensor(rA[:, half(b)], rCS[:, half(b)], m, ALU.add).then_inc(
                        *lstm_A.inc((b,)))
                    dve.wait_ge(*lstm_A.at((b,)))
                    nc.vector.tensor_scalar(m, m, -1.0, None, ALU.mult).then_inc(*lstm_M.inc((b,)))
                    dve.wait_ge(*lstm_M.at((b,)))
                elif step == "turned":
                    bank = ring_dve.take(dve, ("turn", b))[:, 0:64].rearrange("p (b e) -> p b e", e=16)
                    link(dve, nc.vector.tensor_scalar(floor[:, 4 * b:4 * b + 4, :], bank[:, :, 8:16], 1e-6, None,
                                                      ALU.add))
                    nc.vector.tensor_copy(gcol[:, 4 * b:4 * b + 4, :], bank[:, :, 0:8]).then_inc(ring_dve.emptied, 1)
                    dve.wait_ge(ring_dve.emptied, ring_dve.taken)
                elif step == "apply":
                    for i in range(2):
                        bank = ring_score.take(dve, ("qk", b, i))
                        dve.wait_ge(ring_act.emptied, ring_act.nth(("arg", b, i)))
                        d = DC[b % 2][:, 4 * i:4 * i + 4, :]
                        nc.vector.tensor_tensor(d, bank.rearrange("p (c t) -> p c t", t=S), d, ALU.mult).then_inc(
                            ring_score.emptied, 1)
                        dve.wait_ge(ring_score.emptied, ring_score.taken)
                elif step == "normalise":
                    bank = ring_dve.take(dve, ("h", b))
                    hv = bank[:, 0:136].rearrange("p (h e) -> p h e", e=17)
                    den = small[:, 0:8]
                    link(dve, nc.vector.tensor_copy(den, hv[:, :, 16:17].rearrange("p h e -> p (h e)")))
                    link(dve, nc.vector.scalar_tensor_tensor(out=den, in0=den, scalar=-1.0, in1=den, op0=ALU.mult,
                                                             op1=ALU.max))
                    link(dve, nc.vector.scalar_tensor_tensor(out=den, in0=den, scalar=1e-6, in1=floor[:, b, :],
                                                             op0=ALU.add, op1=ALU.max))
                    link(dve, nc.vector.reciprocal(den, den))
                    nc.vector.tensor_tensor(hbuf[:, b % 2, :].rearrange("p (h e) -> p h e", e=16), hv[:, :, 0:16],
                                            spread(den, 16, 2), ALU.mult).then_inc(ring_dve.emptied, 1)
                    dve.wait_ge(ring_dve.emptied, ring_dve.nth(("h", b)))
                    link(dve, nc.vector.bn_stats(stats[:, b, :], hbuf[:, b % 2, :]))
                    nc.vector.bn_aggr(mv[:, b, :], stats[:, b, :]).then_inc(*lstm_var.inc((b,)))
                    dve.wait_ge(*lstm_var.at((b,)))
                elif step == "add":
                    dve.wait_ge(*lstm_rstd.at((b,)))
                    h = hbuf[:, b % 2, :]
                    link(dve, nc.vector.scalar_tensor_tensor(out=h, in0=h, scalar=mv[:, b, 0:1], in1=w["x1_lnscale"],
                                                             op0=ALU.subtract, op1=ALU.mult))
                    link(dve, nc.vector.scalar_tensor_tensor(out=x[:, b, :], in0=h, scalar=rstd[:, b, :],
                                                             in1=x[:, b, :], op0=ALU.mult, op1=ALU.add))
                    if next_of("l1x"):
                        ln_stats(dve, next_of("l1x"), b)
                elif step == "norm" and next_of("l1x"):
                    ln_xhat(dve, next_of("l1x"), b)

        def gpsimd_l1x(pool):
            pool.wait_ge(ctx_loaded, 32)
            pool.wait_ge(ring_dve.emptied, ring_dve.nth(("out", "l1a", B - 1)))
            nc.gpsimd.memset(rM_all, 0.0).then_inc(lstm_cleared, 1)
            pool.wait_ge(lstm_cleared, 1)
            for step, b in lstm_steps():
                if step == "gates":
                    for q in range(2):
                        queries(pool, q)
                    plink(pool, nc.gpsimd.memset(V17, 1.0))
                    for i in range(B):
                        ins = nc.gpsimd.tensor_copy(V17[:, i, :, 0:16], ctx[:, i, :].rearrange("p (h e) -> p h e", e=16))
                    ins.then_inc(v_ready, 1)
                    pool.wait_ge(v_ready, 1)
                elif step == "normalise":
                    pool.wait_ge(*lstm_var.at((b,)))
                    plink(pool, nc.gpsimd.tensor_scalar(veps[:, b, :], mv[:, b, 1:2], 1e-5, None, ALU.add))
                    nc.gpsimd.tensor_tensor(rstd[:, b, :], veps[:, b, :], power[:, 0:1], ALU.pow).then_inc(
                        *lstm_rstd.inc((b,)))
                    pool.wait_ge(*lstm_rstd.at((b,)))
                elif step == "add" and next_of("l1x"):
                    ln_rstd(pool, next_of("l1x"), b)
                elif step == "apply" and 1 <= b < B - 1:
                    queries(pool, b + 1)

        def queries(pool, b):
            pool.wait_ge(ring_act.emptied, xT_use("l1x", b))
            if b >= 2:
                pool.wait_ge(ring_score.filled, ring_score.nth(("qk", b - 2, 1)))
            nc.gpsimd.tensor_tensor(qm[b % 2], spread(xT_of["l1x"][:, b, :], 8), spread(w["mask16"], S, 2),
                                    ALU.mult).then_inc(*lstm_q.inc((b,)))
            pool.wait_ge(*lstm_q.at((b,)))

        VT = qT[:, 0, :, :]
        fth = kT[:, 0, 0:4, :].rearrange("p c s -> p (c s)")
        fu = [kT[:, 1, 4 * i:4 * i + 4, :].rearrange("p c s -> p (c s)") for i in range(2)]
        fh = big[0][:, :, :, 0:S]
        wT8 = O[0:8, 0, :]
        RC = sb("RC", [P, 2, B, 8])
        RQ = sb("RQ", [P, 2, B, 8])
        pvs = sb("pvs", [P, 4, 64])
        rm = sb("rm", [P, 2, B])
        mx = sb("mx", [P, B, 8])
        mi = sb("mi", [P, B, 8], U32)
        mif = sb("mif", [P, B, 2])
        sca = sb("sca", [P, B, 4])
        sigma = sb("sigma", [P, 2])
        hb = sb("hb", [P, 32])

        def tensor_l1f(pe):
            pe.wait_ge(loaded["l1f"], 16)
            for n in range(2):
                for b in halves[n]:
                    xT_wait(pe, "l1f", b)
                bank = ring_act.open(pe, ("VT", n))
                nc.tensor.matmul(bank, w["f1_wv"], xT_of["l1f"][:, 4 * n:4 * n + 4, :], start=True, stop=True
                                 ).then_inc(ring_act.filled, 1)
            for n in range(2):
                bank = ring_dve.open(pe, ("router", "l1f", n))
                pe.wait_ge(ring_act.emptied, ring_act.nth(("VT", n)))
                for i in range(4):
                    last = nc.tensor.matmul(bank[:, 72 * i:72 * i + 72], VT[:, 4 * n + i, :], w["f1_wgp"], start=True,
                                            stop=True)
                last.then_inc(ring_dve.filled, 1)
            for n in range(2):
                for c in range(2):
                    bank = ring_act.open(pe, ("h1", c, n))
                    nc.tensor.matmul(bank, w["f1_w1"][:, c * P:(c + 1) * P], VT[:, 4 * n:4 * n + 4, :], start=True,
                                     stop=True).then_inc(ring_act.filled, 1)
            pe.wait_ge(*l1f_w.at((0,)))
            for n in range(2):
                bank = ring_act.open(pe, ("wT", "l1f", n))
                for i in range(4):
                    last = nc.tensor.transpose(bank[0:8, i * S:(i + 1) * S], wcol[:, 4 * n + i, 0:8], w["ident"])
                last.then_inc(ring_act.filled, 1)
            for n in range(2):
                pe.wait_ge(ring_act.emptied, ring_act.nth(("wT", "l1f", n)))
                for c in range(2):
                    bank = ring_score.open(pe, ("wexp", c, n))
                    nc.tensor.matmul(bank, w["sel8"][:, c * P:(c + 1) * P], wT8[:, 512 * n:512 * n + 512], start=True,
                                     stop=True).then_inc(ring_score.filled, 1)
            for n in range(2):
                bank = ring_dve.open(pe, ("out", "l1f", n))
                nc.tensor.matmul(bank, w["ones"][0:1, :], spread(w["f1_bvr"], 4), start=True, stop=False)
                for c in range(2):
                    pe.wait_ge(*l1f_h.at((c, n)))
                for i in range(4):
                    b = 4 * n + i
                    o = bank[:, i * D:(i + 1) * D]
                    nc.tensor.matmul(o, xT_of["l1f"][:, b, :], w["f1_wv"], start=False, stop=False)
                    nc.tensor.matmul(o, wT8[:, b * S:(b + 1) * S], w["f1_b2"], start=False, stop=False)
                    for c in range(2):
                        last = nc.tensor.matmul(o, fh[:, c, b, :], w["f1_w2"][:, c * D:(c + 1) * D], start=False,
                                                stop=(i == 3 and c == 1))
                last.then_inc(ring_dve.filled, 1)
            finish_pe(pe, "l1f")

        l1f_w = events(sem("l1f_weights"), [(0,)])
        l1f_h = events(sem("l1f_hidden"), [(c, n) for n in range(2) for c in range(2)])
        l1f_u = events(sem("l1f_silu"), [(c, n) for n in range(2) for c in range(2)])
        l1f_d = sem("l1f_dve")
        l1f_p = sem("l1f_pool")
        l1f_a = sem("l1f_act")

        def scalar_l1f(act):
            act.wait_ge(loaded["l1f"], 16)
            for n in range(2):
                bank = ring_act.take(act, ("VT", n))
                nc.scalar.activation(VT[:, 4 * n:4 * n + 4, :], bank.rearrange("p (b t) -> p b t", t=S), ACT.Identity,
                                     bias=w["f1_bvc"]).then_inc(ring_act.emptied, 1)
            nc.scalar.activation(sigma[:, 0:1], w["f1_alpha"], ACT.Exp, scale=-1.0).then_inc(l1f_a, 1)
            act.wait_ge(l1f_d, 1)
            for n in range(2):
                for c in range(2):
                    bank = ring_act.take(act, ("h1", c, n))
                    if (c, n) != (0, 0):
                        act.wait_ge(*l1f_u.at((1 - c, n if c else n - 1)))
                    nc.scalar.activation(fth, bank, ACT.Tanh, scale=0.5, bias=hb[:, c:c + 1])
                    nc.scalar.activation(fu[c], bank, ACT.Identity, bias=w["f1_b1"][:, c:c + 1]).then_inc(
                        ring_act.emptied, 1)
            act.wait_ge(l1f_d, 3)
            nc.scalar.activation(sca[:, :, 1], sca[:, :, 0], ACT.Exp).then_inc(l1f_a, 1)
            for n in range(2):
                bank = ring_act.take(act, ("wT", "l1f", n))
                nc.scalar.activation(wT8[:, 512 * n:512 * n + 512], bank[0:8, :], ACT.Copy).then_inc(
                    ring_act.emptied, 1)
            finish_act(act, "l1f")

        def vector_l1f(dve):
            dve.wait_ge(loaded["l1f"], 16)
            nc.vector.tensor_scalar(hb[:, 0:2], w["f1_b1"], 0.5, None, ALU.mult).then_inc(l1f_d, 1)
            dve.wait_ge(l1f_d, 1)
            dve.wait_ge(l1f_a, 1)
            link(dve, nc.vector.tensor_scalar(sigma[:, 0:1], sigma[:, 0:1], 1.0, None, ALU.add))
            link(dve, nc.vector.reciprocal(sigma[:, 1:2], sigma[:, 0:1]))
            for n in range(2):
                bank = ring_dve.take(dve, ("router", "l1f", n))[:, 0:288].rearrange("p (b e) -> p b e", e=72)
                link(dve, nc.vector.tensor_tensor(RC[:, 0, 4 * n:4 * n + 4, :], bank[:, :, 0:8], spread(w["f1_bg"], 4), ALU.add))
                nc.vector.tensor_copy(pvs, bank[:, :, 8:72]).then_inc(ring_dve.emptied, 1)
                dve.wait_ge(ring_dve.emptied, ring_dve.nth(("router", "l1f", n)))
                link(dve, nc.vector.tensor_tensor(pvs, pvs, pvs, ALU.mult))
                link(dve, nc.vector.tensor_reduce(RQ[:, 1, 4 * n:4 * n + 4, :],
                                                  pvs.rearrange("p b (e k) -> p b e k", k=8), AX.X, ALU.add))
            nc.vector.tensor_scalar(RQ[:, 1, :, :], RQ[:, 1, :, :], 0.125, None, ALU.mult).then_inc(l1f_d, 1)
            dve.wait_ge(l1f_d, 2)
            for n in range(2):
                for c in range(2):
                    dve.wait_ge(ring_act.emptied, ring_act.nth(("h1", c, n)))
                    nc.vector.scalar_tensor_tensor(out=fh[:, c, 4 * n:4 * n + 4, :],
                                                   in0=fth.rearrange("p (b t) -> p b t", t=S), scalar=1.0,
                                                   in1=fu[c].rearrange("p (b t) -> p b t", t=S), op0=ALU.add,
                                                   op1=ALU.mult).then_inc(*l1f_u.inc((c, n)))
                    dve.wait_ge(*l1f_u.at((c, n)))
            dve.wait_ge(l1f_p, 1)
            rc = RC[:, :, :, :].rearrange("p a b e -> p (a b) e")
            rq = RQ[:, :, :, :].rearrange("p a b e -> p (a b) e")
            rms = rm[:, :, :].rearrange("p a b -> p (a b)")
            link(dve, nc.vector.tensor_reduce(rms, rc, AX.X, ALU.add))
            link(dve, nc.vector.tensor_scalar(rms, rms, 0.125, None, ALU.mult))
            link(dve, nc.vector.tensor_tensor(rc, rc, spread(rms, 8, 2), ALU.subtract))
            link(dve, nc.vector.tensor_tensor(rq, rc, rc, ALU.mult))
            link(dve, nc.vector.tensor_reduce(rms, rq, AX.X, ALU.add))
            nc.vector.tensor_scalar(rms, rms, 0.125, 1e-5, ALU.mult, ALU.add).then_inc(l1f_v, 1)
            dve.wait_ge(l1f_v, 1)
            dve.wait_ge(l1f_p, 2)
            link(dve, nc.vector.tensor_tensor(rc, rc, spread(rms, 8, 2), ALU.mult))
            for i, (gn, bn) in enumerate((("f1_gr", "f1_br"), ("f1_gc", "f1_bc"))):
                link(dve, nc.vector.tensor_tensor(RC[:, i, :, :], RC[:, i, :, :], spread(w[gn], B), ALU.mult))
                link(dve, nc.vector.tensor_tensor(RC[:, i, :, :], RC[:, i, :, :], spread(w[bn], B), ALU.add))
            link(dve, nc.vector.scalar_tensor_tensor(out=RC[:, 0, :, :], in0=RC[:, 1, :, :], scalar=sigma[:, 1:2],
                                                     in1=RC[:, 0, :, :], op0=ALU.mult, op1=ALU.add))
            for b in range(B):
                ins = nc.vector.max(mx[:, b, :], RC[:, 0, b, :])
            link(dve, ins)
            for b in range(B):
                ins = nc.vector.max_index(mi[:, b, :], mx[:, b, :], RC[:, 0, b, :])
            link(dve, ins)
            link(dve, nc.vector.tensor_copy(mif, mi[:, :, 0:2]))
            nc.vector.tensor_tensor(sca[:, :, 0], mx[:, :, 1], mx[:, :, 0], ALU.subtract).then_inc(l1f_d, 1)
            dve.wait_ge(l1f_d, 3)
            dve.wait_ge(l1f_a, 2)
            link(dve, nc.vector.tensor_scalar(sca[:, :, 2], sca[:, :, 1], 1.0, None, ALU.add))
            link(dve, nc.vector.reciprocal(sca[:, :, 2], sca[:, :, 2]))
            link(dve, nc.vector.tensor_tensor(sca[:, :, 3], sca[:, :, 1], sca[:, :, 2], ALU.mult))
            for i in range(2):
                link(dve, nc.vector.tensor_tensor(RQ[:, i, :, :], spread(w["iota8"], B), spread(mif[:, :, i], 8, 2),
                                                  ALU.is_equal))
                link(dve, nc.vector.tensor_tensor(RQ[:, i, :, :], RQ[:, i, :, :], spread(sca[:, :, 2 + i], 8, 2),
                                                  ALU.mult))
            nc.vector.tensor_tensor(wcol[:, :, 0:8], RQ[:, 0, :, :], RQ[:, 1, :, :], ALU.add).then_inc(
                *l1f_w.inc((0,)))
            dve.wait_ge(*l1f_w.at((0,)))
            for n in range(2):
                for c in range(2):
                    bank = ring_score.take(dve, ("wexp", c, n))
                    h = fh[:, c, 4 * n:4 * n + 4, :]
                    nc.vector.tensor_tensor(h, h, bank.rearrange("p (b t) -> p b t", t=S), ALU.mult).then_inc(
                        ring_score.emptied, 1)
                    dve.wait_ge(ring_score.emptied, ring_score.nth(("wexp", c, n)))
                    nc.vector.tensor_copy(rden[:, 0:1], rden[:, 0:1]).then_inc(*l1f_h.inc((c, n)))
                    dve.wait_ge(*l1f_h.at((c, n)))
            for n in range(2):
                bank = ring_dve.take(dve, ("out", "l1f", n))
                xs = x[:, 4 * n:4 * n + 4, :]
                nc.vector.tensor_tensor(xs, bank.rearrange("p (b d) -> p b d", d=D), xs, ALU.add).then_inc(
                    ring_dve.emptied, 1)
                dve.wait_ge(ring_dve.emptied, ring_dve.nth(("out", "l1f", n)))
                finish_dve(dve, "l1f", n)

        l1f_v = sem("l1f_variance")

        def gpsimd_l1f(pool):
            pool.wait_ge(l1f_d, 2)
            nc.gpsimd.tensor_tensor(RC[:, 1, :, :], RQ[:, 1, :, :],
                                    power[:, 1:2].unsqueeze(2).to_broadcast([P, B, 8]), ALU.pow).then_inc(l1f_p, 1)
            pool.wait_ge(l1f_p, 1)
            pool.wait_ge(l1f_v, 1)
            nc.gpsimd.tensor_tensor(rm[:, :, :], rm[:, :, :], power[:, 0:1].unsqueeze(2).to_broadcast([P, 2, B]),
                                    ALU.pow).then_inc(l1f_p, 1)
            pool.wait_ge(l1f_p, 2)
            finish_pool(pool, "l1f")

        aff = ctx[:, 0:2, :].rearrange("p a (b e) -> p (a b) e", e=32)
        rep = ctx[:, 2:4, :].rearrange("p a (b e) -> p (a b) e", e=32)
        whalf = sb("whalf", [P, B, 32], BF16)
        w96 = gate2[:, 0:3, :].rearrange("p m (a e) -> p (m a) e", e=32).rearrange("p (b t) e -> p b (t e)", t=3)
        w96T = OT[0:96, 0, :, :]
        w3T = OT[0:96, 1, :, :].rearrange("p c s -> p (c s)").bitcast(BF16)[:, 0:TOK].rearrange("p (b t) -> p b t", t=S)
        f2_r = sem("f2_router")
        f2_a = sem("f2_router_act")
        f2_w = sem("f2_weights")
        f2_b = sem("f2_half_bias")
        NC2 = 17
        f2_seq = [(n, c) for n in range(2) for c in range(NC2)]
        f2_t = events(sem("f2_tanh"), f2_seq)
        f2_h = events(sem("f2_hidden"), f2_seq)
        hid = [kmask[:, i, :, :, :].rearrange("p a c s -> p (a c s)") for i in range(3)]

        def tensor_l2f(pe):
            pe.wait_ge(loaded["l2f"], 16)
            bank = ring_dve.open(pe, ("router", "l2f"))
            xT = xT_of["l2f"]
            for b in range(B):
                xT_wait(pe, "l2f", b)
                nc.tensor.matmul(bank[:, 32 * b:32 * b + 32], xT[:, b, :], w["f2_wr"], start=True, stop=False)
                last = nc.tensor.matmul(bank[:, 32 * b:32 * b + 32], w["ones"][0:1, :], w["f2_br"], start=False,
                                        stop=True)
            last.then_inc(ring_dve.filled, 1)
            pe.wait_ge(f2_w, 1)
            for n in range(2):
                bank = ring_act.open(pe, ("wT", "l2f", n))
                for i in range(4):
                    last = nc.tensor.transpose(bank[0:96, i * S:(i + 1) * S], w96[:, 4 * n + i, :], w["ident"])
                last.then_inc(ring_act.filled, 1)
            acc = [None, None]

            def down(n, c):
                rows = 64 if c == 16 else P
                rhs = w["f2_wds"] if c == 16 else w["f2_wd"][:, c * D:(c + 1) * D]
                pe.wait_ge(*f2_h.at((n, c)))
                for i in range(4):
                    last = nc.tensor.matmul(acc[n][:, i * D:(i + 1) * D],
                                            hid[(n * NC2 + c) % 3][0:rows, i * S:(i + 1) * S], rhs, start=False,
                                            stop=(c == 16 and i == 3))
                if c == 16:
                    last.then_inc(ring_dve.filled, 1)

            for m, (n, c) in enumerate(f2_seq + [(2, 0), (2, 1)]):
                if n < 2:
                    if c == 0:
                        pe.wait_ge(ring_act.emptied, ring_act.nth(("wT", "l2f", n)))
                    rows = 64 if c == 16 else P
                    wg = w["f2_wgs"] if c == 16 else w["f2_wg"][:, c * P:(c + 1) * P]
                    wu = w["f2_wus"] if c == 16 else w["f2_wu"][:, c * P:(c + 1) * P]
                    bank = ring_act.open(pe, ("up", "l2f", n, c))
                    nc.tensor.matmul(bank[0:rows, :], wu, xT[:, 4 * n:4 * n + 4, :], start=True, stop=True).then_inc(
                        ring_act.filled, 1)
                    bank = ring_score.open(pe, ("gate", "l2f", n, c))
                    nc.tensor.matmul(bank[0:rows, :], wg, xT[:, 4 * n:4 * n + 4, :], start=True, stop=True).then_inc(
                        ring_score.filled, 1)
                    if c < 16:
                        bank = ring_prob.open(pe, ("wexp", "l2f", n, c))
                        nc.tensor.matmul(bank, w["sel32_bf"][:, c * P:(c + 1) * P], w3T[:, 4 * n:4 * n + 4, :],
                                         start=True, stop=True).then_inc(ring_prob.filled, 1)
                if m >= 2:
                    pn, pc = f2_seq[m - 2]
                    if pc == 0:
                        acc[pn] = ring_dve.open(pe, ("out", "l2f", pn))
                        nc.tensor.matmul(acc[pn], w["ones"][0:1, :], spread(w["f2_bds"], 4), start=True, stop=False)
                        for i in range(4):
                            nc.tensor.matmul(acc[pn][:, i * D:(i + 1) * D], w96T[:, 4 * pn + i, :], w["f2_bd3"],
                                             start=False, stop=False)
                    down(pn, pc)
            finish_pe(pe, "l2f")

        def scalar_l2f(act):
            act.wait_ge(loaded["l2f"], 16)
            act.wait_ge(ring_dve.filled, ring_dve.nth(("router", "l2f")))
            nc.scalar.activation(aff[:, :, :].rearrange("p b e -> p (b e)"), ring_dve.bank(("router", "l2f"))[:, 0:256],
                                 ACT.Exp, scale=-1.0).then_inc(f2_a, 1)
            for n in range(2):
                bank = ring_act.take(act, ("wT", "l2f", n))
                src = bank[0:96, :].rearrange("p (b t) -> p b t", t=S)
                nc.scalar.activation(w96T[:, 4 * n:4 * n + 4, :], src, ACT.Copy)
                nc.scalar.activation(w3T[:, 4 * n:4 * n + 4, :], src, ACT.Copy).then_inc(ring_act.emptied, 1)
            act.wait_ge(f2_b, 1)
            for m, (n, c) in enumerate(f2_seq):
                rows = 64 if c == 16 else P
                if m >= 2:
                    act.wait_ge(*f2_h.at(f2_seq[m - 2]))
                bank = ring_act.take(act, ("up", "l2f", n, c))
                ub = w["f2_bus"] if c == 16 else w["f2_bu"][:, c:c + 1]
                hbias2 = hb[0:rows, c:c + 1]
                nc.scalar.activation(prob[0:rows, 2 + m % 2, :, :].rearrange("p c s -> p (c s)"), bank[0:rows, :],
                                     ACT.Identity, bias=ub).then_inc(ring_act.emptied, 1)
                act.wait_ge(ring_score.filled, ring_score.nth(("gate", "l2f", n, c)))
                nc.scalar.activation(prob[0:rows, m % 2, :, :].rearrange("p c s -> p (c s)"),
                                     ring_score.bank(("gate", "l2f", n, c))[0:rows, :], ACT.Tanh, scale=0.5,
                                     bias=hbias2).then_inc(*f2_t.inc((n, c)))
            finish_act(act, "l2f")

        def vector_l2f(dve):
            dve.wait_ge(loaded["l2f"], 16)
            link(dve, nc.vector.tensor_scalar(hb[:, 0:16], w["f2_bg"], 0.5, None, ALU.mult))
            nc.vector.tensor_scalar(hb[0:64, 16:17], w["f2_bgs"], 0.5, None, ALU.mult).then_inc(f2_b, 1)
            dve.wait_ge(f2_b, 1)
            dve.wait_ge(f2_a, 1)
            ring_dve.take(dve, ("router", "l2f"))
            a = aff[:, :, :]
            nc.vector.tensor_scalar(a, a, 1.0, None, ALU.add).then_inc(ring_dve.emptied, 1)
            dve.wait_ge(ring_dve.emptied, ring_dve.nth(("router", "l2f")))
            link(dve, nc.vector.reciprocal(a, a))
            for b in range(B):
                ins = nc.vector.max(mx[:, b, :], aff[:, b, :])
            link(dve, ins)
            for b in range(B):
                link(dve, nc.vector.match_replace(rep[:, b, :], mx[:, b, :], aff[:, b, :], -1.0))
            top = rm[:, 0, :]
            link(dve, nc.vector.tensor_reduce(top, mx, AX.X, ALU.add))
            link(dve, nc.vector.tensor_scalar(top, top, 1e-9, None, ALU.add))
            link(dve, nc.vector.reciprocal(top, top))
            link(dve, nc.vector.scalar_tensor_tensor(out=rep[:, :, :], in0=rep[:, :, :], scalar=0.0, in1=a,
                                                     op0=ALU.is_lt, op1=ALU.mult))
            link(dve, nc.vector.tensor_tensor(rep[:, :, :], rep[:, :, :], spread(top, 32, 2), ALU.mult))
            link(dve, nc.vector.tensor_copy(whalf[:, :, :], rep[:, :, :]))
            link(dve, nc.vector.tensor_copy(w96[:, :, 0:32], whalf[:, :, :]))
            link(dve, nc.vector.tensor_tensor(rep[:, :, :], rep[:, :, :], whalf[:, :, :], ALU.subtract))
            link(dve, nc.vector.tensor_copy(whalf[:, :, :], rep[:, :, :]))
            link(dve, nc.vector.tensor_copy(w96[:, :, 32:64], whalf[:, :, :]))
            nc.vector.tensor_tensor(w96[:, :, 64:96], rep[:, :, :], whalf[:, :, :], ALU.subtract).then_inc(f2_w, 1)
            dve.wait_ge(f2_w, 1)
            for m, (n, c) in enumerate(f2_seq):
                rows = 64 if c == 16 else P
                bank = ring_score.take(dve, ("gate", "l2f", n, c))
                dve.wait_ge(*f2_t.at((n, c)))
                th = prob[0:rows, m % 2, :, :].rearrange("p c s -> p (c s)")
                ub = prob[0:rows, 2 + m % 2, :, :].rearrange("p c s -> p (c s)")
                gb = w["f2_bgs"] if c == 16 else w["f2_bg"][:, c:c + 1]
                nc.vector.scalar_tensor_tensor(out=ub, in0=bank[0:rows, :], scalar=gb, in1=ub, op0=ALU.add,
                                               op1=ALU.mult).then_inc(ring_score.emptied, 1)
                dve.wait_ge(ring_score.emptied, ring_score.nth(("gate", "l2f", n, c)))
                link(dve, nc.vector.scalar_tensor_tensor(out=ub, in0=th, scalar=1.0, in1=ub, op0=ALU.add,
                                                         op1=ALU.mult))
                if m >= 3:
                    late = ring_score.nth(("gate", "l2f") + f2_seq[m - 1]) if False else None
                h = hid[m % 3][0:rows, 0:512]
                if c < 16:
                    wb = ring_prob.take(dve, ("wexp", "l2f", n, c))
                    nc.vector.tensor_tensor(h, ub, wb, ALU.mult).then_inc(ring_prob.emptied, 1)
                    dve.wait_ge(ring_prob.emptied, ring_prob.nth(("wexp", "l2f", n, c)))
                    nc.vector.tensor_copy(rden[:, 0:1], rden[:, 0:1]).then_inc(*f2_h.inc((n, c)))
                    dve.wait_ge(*f2_h.at((n, c)))
                else:
                    nc.vector.tensor_scalar(h, ub, 0.5, None, ALU.mult).then_inc(*f2_h.inc((n, c)))
                    dve.wait_ge(*f2_h.at((n, c)))
                if (n, c) == (1, 1):
                    finish_out(dve, 0)
            finish_out(dve, 1)

        def finish_out(dve, n):
            bank = ring_dve.take(dve, ("out", "l2f", n))
            xs = x[:, 4 * n:4 * n + 4, :]
            nc.vector.tensor_tensor(xs, bank.rearrange("p (b d) -> p b d", d=D), xs, ALU.add).then_inc(
                ring_dve.emptied, 1)
            dve.wait_ge(ring_dve.emptied, ring_dve.nth(("out", "l2f", n)))
            finish_dve(dve, "l2f", n)

        def gpsimd_l2f(pool):
            finish_pool(pool, "l2f")

        sc = O[0:8, 0, :]
        sw = [O[0:8, 1, :], qT[0:8, 0, :, :].rearrange("p c s -> p (c s)")]
        se = qT[0:8, 1, :, :].rearrange("p c s -> p (c s)")
        mx3 = sb("mx3", [8, 16, 8])
        s8 = sb("s8", [8, 4])
        f3_d = sem("f3_dve")
        f3_a = sem("f3_act")
        f3_seq = [(e, n, k) for e in range(8) for n in range(2) for k in range(2)]
        f3_t = events(sem("f3_tanh"), f3_seq)
        f3_h = events(sem("f3_hidden"), f3_seq)

        def tensor_l3f(pe):
            pe.wait_ge(loaded["l3f"], 16)
            xT = xT_of["l3f"]
            for n in range(2):
                for b in halves[n]:
                    xT_wait(pe, "l3f", b)
                bank = ring_dve.open(pe, ("sc", n))
                nc.tensor.matmul(bank[0:8, :], w["f3_wg"], xT[:, 4 * n:4 * n + 4, :], start=True, stop=True).then_inc(
                    ring_dve.filled, 1)

            def y(e, n):
                bank = ring_dve.open(pe, ("y", e, n))
                for k in range(2):
                    pe.wait_ge(*f3_h.at((e, n, k)))
                for i in range(4):
                    for k in range(2):
                        last = nc.tensor.matmul(bank[:, i * D:(i + 1) * D],
                                                hid[(2 * e + n) % 3][:, 512 * k + i * S:512 * k + (i + 1) * S],
                                                w["f3_w2"][:, (2 * e + k) * D:(2 * e + k + 1) * D], start=(k == 0),
                                                stop=(k == 1))
                last.then_inc(ring_dve.filled, 1)

            for e, n, k in f3_seq:
                c = 2 * e + k
                bank = ring_score.open(pe, ("gate", e, n, k))
                nc.tensor.matmul(bank, w["f3_w1"][:, c * P:(c + 1) * P], xT[:, 4 * n:4 * n + 4, :], start=True,
                                 stop=True).then_inc(ring_score.filled, 1)
                bank = ring_prob.open(pe, ("up", e, n, k))
                nc.tensor.matmul(bank, w["f3_w3"][:, c * P:(c + 1) * P], xT[:, 4 * n:4 * n + 4, :], start=True,
                                 stop=True).then_inc(ring_prob.filled, 1)
                if (e, n, k) == (0, 1, 0):
                    pe.wait_ge(f3_d, 2)
                    bank = ring_act.open(pe, ("wcol",))
                    for b in range(B):
                        last = nc.tensor.transpose(bank[:, 8 * b:8 * b + 8], se[:, b * S:(b + 1) * S],
                                                   w["ident"][0:8, 0:8])
                    last.then_inc(ring_act.filled, 1)
                if k == 1 and (e, n) != (0, 0):
                    y(*((e, 0) if n else (e - 1, 1)))
            y(7, 1)

        def scalar_l3f(act):
            act.wait_ge(f3_d, 1)
            nc.scalar.activation(se, sc, ACT.Exp, bias=s8[:, 0:1]).then_inc(f3_a, 1)
            for m, (e, n, k) in enumerate(f3_seq):
                if m >= 4:
                    act.wait_ge(*f3_h.at(f3_seq[m - 4]))
                act.wait_ge(ring_score.filled, ring_score.nth(("gate", e, n, k)))
                nc.scalar.activation(prob[:, m % 4, :, :].rearrange("p c s -> p (c s)"),
                                     ring_score.bank(("gate", e, n, k)), ACT.Tanh, scale=0.5).then_inc(
                    *f3_t.inc((e, n, k)))
                if m == 2:
                    bank = ring_act.take(act, ("wcol",))
                    nc.scalar.activation(wcol[:, :, 0:8], bank[:, 0:64].rearrange("p (b e) -> p b e", e=8), ACT.Copy
                                         ).then_inc(ring_act.emptied, 1)

        def vector_l3f(dve):
            for n in range(2):
                bank = ring_dve.take(dve, ("sc", n))
                nc.vector.tensor_copy(sc[:, 512 * n:512 * n + 512], bank[0:8, :]).then_inc(ring_dve.emptied, 1)
                dve.wait_ge(ring_dve.emptied, ring_dve.taken)
            dve.wait_ge(ring_dve.emptied, ring_dve.nth(("sc", 1)))
            src = sc
            for r in range(16):
                link(dve, nc.vector.max(mx3[:, r, :], src))
                if r == 0:
                    nc.vector.tensor_scalar(s8[:, 0:1], mx3[:, 0, 0:1], -1.0, None, ALU.mult).then_inc(f3_d, 1)
                    dve.wait_ge(f3_d, 1)
                link(dve, nc.vector.match_replace(sw[r % 2], mx3[:, r, :], src, -3.0e38))
                src = sw[r % 2]
            link(dve, nc.vector.tensor_tensor(src, src, sc, ALU.not_equal))
            dve.wait_ge(f3_a, 1)
            link(dve, nc.vector.tensor_tensor(se, se, src, ALU.mult))
            link(dve, nc.vector.tensor_reduce(s8[:, 1:2], se, AX.X, ALU.add))
            link(dve, nc.vector.reciprocal(s8[:, 2:3], s8[:, 1:2]))
            nc.vector.tensor_scalar(se, se, s8[:, 2:3], 0.5, ALU.mult, ALU.mult).then_inc(f3_d, 1)
            dve.wait_ge(f3_d, 2)

            def add(e, n):
                bank = ring_dve.take(dve, ("y", e, n))
                if (e, n) == (0, 0):
                    dve.wait_ge(ring_act.emptied, ring_act.nth(("wcol",)))
                for i in range(4):
                    b = 4 * n + i
                    ins = nc.vector.scalar_tensor_tensor(out=x[:, b, :], in0=bank[:, i * D:(i + 1) * D],
                                                         scalar=wcol[:, b, e:e + 1], in1=x[:, b, :], op0=ALU.mult,
                                                         op1=ALU.add)
                ins.then_inc(ring_dve.emptied, 1)
                dve.wait_ge(ring_dve.emptied, ring_dve.taken)

            for m, (e, n, k) in enumerate(f3_seq):
                dve.wait_ge(*f3_t.at((e, n, k)))
                g = ring_score.take(dve, ("gate", e, n, k))
                th = prob[:, m % 4, :, :].rearrange("p c s -> p (c s)")
                nc.vector.scalar_tensor_tensor(out=th, in0=th, scalar=1.0, in1=g, op0=ALU.add, op1=ALU.mult
                                               ).then_inc(ring_score.emptied, 1)
                dve.wait_ge(ring_score.emptied, ring_score.nth(("gate", e, n, k)))
                u = ring_prob.take(dve, ("up", e, n, k))
                nc.vector.tensor_tensor(hid[(2 * e + n) % 3][:, 512 * k:512 * k + 512], th, u, ALU.mult).then_inc(
                    ring_prob.emptied, 1)
                dve.wait_ge(ring_prob.emptied, ring_prob.nth(("up", e, n, k)))
                nc.vector.tensor_copy(rden[:, 0:1], rden[:, 0:1]).then_inc(*f3_h.inc((e, n, k)))
                dve.wait_ge(*f3_h.at((e, n, k)))
                if k == 1 and (e, n) != (0, 0):
                    add(*((e, 0) if n else (e - 1, 1)))
            add(7, 1)

        def gpsimd_l3f(pool):
            pass

        PE = {"l0a": tensor_l0a, "l0f": tensor_l0f}
        SC = {"l0a": scalar_l0a, "l0f": scalar_l0f}
        VE = {"l0a": vector_l0a, "l0f": vector_l0f}
        PO = {"l0a": gpsimd_l0a, "l0f": gpsimd_l0f}
        PE.update(l1x=tensor_l1x, l1f=tensor_l1f, l2f=tensor_l2f, l3f=tensor_l3f)
        SC.update(l1x=scalar_l1x, l1f=scalar_l1f, l2f=scalar_l2f, l3f=scalar_l3f)
        VE.update(l1x=vector_l1x, l1f=vector_l1f, l2f=vector_l2f, l3f=vector_l3f)
        PO.update(l1x=gpsimd_l1x, l1f=gpsimd_l1f, l2f=gpsimd_l2f, l3f=gpsimd_l3f)
        block = stack.enter_context(nc.Block())

        @block.tensor
        def _(pe):
            for s in subs:
                PE[s](pe) if s in PE else tensor_attention(pe, s)

        @block.scalar
        def _(act):
            act.wait_ge(loaded["const"], 16)
            for s in subs:
                SC[s](act) if s in SC else scalar_attention(act, s)

        @block.vector
        def _(dve):
            dve.wait_ge(loaded["const"], 16)
            for s in subs:
                if s == subs[-1]:
                    pass
                VE[s](dve) if s in VE else vector_attention(dve, s)
            dve.drain().then_inc(x_final, 1)
            dve.wait_ge(x_final, 1)

        @block.gpsimd
        def _(pool):
            for s in subs:
                PO[s](pool) if s in PO else gpsimd_attention(pool, s)

        @block.sync
        def _(sp):
            sp.dma_start(x[:], x_dram.rearrange("b t d -> t b d")).then_inc(x_loaded, 16)
            order = ["l0a", "const", "small", "sel32"]
            order += [s for s in subs if s in groups and s not in order and s not in [later for _, later in PLACES]]
            for g in order:
                sp.dma_start(store[g], groups[g][0]).then_inc(loaded[g], 16)
                if g == "sel32":
                    for name, dst in (("ctxT", ctxT), ("ctx", ctx)):
                        sp.dma_start(dst[:], ctx_dram[name]).then_inc(ctx_loaded, 16)
            sp.dma_start(rowconst, rowconst_dram).then_inc(rowconst_loaded, 16)
            if "l3x" in subs:
                sp.wait_ge(ring_dve.emptied, ring_dve.nth(("out", "l0f", 1)))
                sp.dma_start(mask_i, mask_dram).then_inc(mask_loaded, 16)
            for first, later in PLACES:
                if later in subs:
                    sp.wait_ge(ring_dve.emptied, ring_dve.nth(("out", first, 1 if first == "l0a" else B - 1)))
                    if first == "l0a":
                        sp.wait_ge(*stats_ready.at(("l0x", 0, B - 1)))
                    sp.dma_start(store[later], groups[later][0]).then_inc(loaded[later], 16)
            sp.wait_ge(x_final, 1)
            sp.dma_start(out_dram.rearrange("b t d -> t b d"), x[:]).then_inc(stored, 16)
            sp.wait_ge(stored, 16)
            sp.wait_ge(rowconst_loaded, 16)


def lay_out(inputs):
    def f(name):
        return np.asarray(inputs[name])

    def chunked(a):
        return np.concatenate([a[i:i + P] for i in range(0, a.shape[0], P)], axis=1)

    def col(a):
        return a.reshape(-1, P).T

    def rep(a):
        return np.broadcast_to(a.reshape(1, -1), (P, a.size))

    def row(a):
        return a.reshape(1, -1)

    p = np.arange(P)
    c1024 = np.arange(TOK)
    h8 = np.arange(8)[:, None]
    dim = p % 32
    freq = (1.0 / 10000.0 ** (np.arange(0, 8, 2, dtype=np.float32) / 8)).astype(np.float32)
    angle = np.arange(S, dtype=np.float32)[None, :] * freq[dim % 4][:, None]
    rotated = (dim < 8)[:, None]
    const = {
        "ident": np.eye(P),
        "ones": np.ones((P, P)),
        "mask8": (p[:, None] % 64) // 8 == np.arange(8),
        "mask32": p[:, None] // 32 == np.arange(4),
        "mask16": 0.25 * (p[:, None] // 16 == np.arange(8)),
        "iota8": np.broadcast_to(np.arange(8), (P, 8)),
        "sel8": 0.5 * (np.arange(256)[None, :] // 32 == h8),
        "cos": np.where(rotated, np.cos(angle), 1.0),
        "sin": np.where(rotated, np.sin(angle) * np.where(dim < 4, -1.0, 1.0)[:, None], 0.0),
        "bigparts": np.pad(BIG_PARTS, ((0, P - 3), (0, 0))),
    }
    rowconst = np.zeros((P, 3, TOK), np.float32)
    rowconst[0:8, 0] = c1024[None, :] // S == h8
    rowconst[0:8, 1] = c1024 % S != 0
    rowconst[0:8, 2] = np.where(c1024 % S == 0, NEG, 0.0)
    q, k = p[:, None], p[None, :]
    small = {
        "ident_bf": np.eye(P),
        "ones_bf": np.ones((P, P)),
        "causal_bf": np.where(k <= q, 0.0, NEG),
        "causalT_bf": np.where(q <= k, 0.0, NEG),
    }
    sel32 = {
        "sel32_bf": 0.5 * (np.arange(96)[:, None] % 32 == np.arange(2048)[None, :] // 64),
    }
    perm = np.arange(256).reshape(8, 32).copy()
    perm[:, 0:8] = perm[:, [4, 5, 6, 7, 0, 1, 2, 3]]
    perm = perm.reshape(-1)
    kperm = perm[0:64]
    wq, wk = f("L2_attn_Wq"), f("L2_attn_Wk")

    def rep4(a, kv):
        return np.concatenate([a[:, 32 * kv:32 * kv + 32]] * 4, axis=1)

    gate_cols = {"wi": f("L1_xattn_igate_w"), "wf": f("L1_xattn_fgate_w")}
    groups = {
        "l0a": {
            "l0a_win": f("L0_attn_w_in").T, "l0a_wx": chunked(f("L0_attn_w_x").T), "l0a_wout": chunked(f("L0_attn_w_out").T),
            "l0a_bin": col(f("L0_attn_b_in")[:256]),
            "l0a_wconv": f("L0_attn_w_conv")[:, 0, :].reshape(2, P, 4).transpose(1, 0, 2).reshape(P, 8),
            "l0a_bconv": col(f("L0_attn_b_conv")), "l0a_bx": col(f("L0_attn_b_x")[:256]),
            "l0a_bout": rep(f("L0_attn_b_out")),
        },
        "const": const,
        "l0x": {
            "x0_wq": f("L0_xattn_w_q"), "x0_wk": f("L0_xattn_w_kv")[:, :1024], "x0_wv": f("L0_xattn_w_kv")[:, 1024:],
            "x0_wo": chunked(f("L0_xattn_w_out")), "x0_gamma": col(f("L0_xattn_ln_gamma")),
            "x0_beta": col(f("L0_xattn_ln_beta")), "x0_bout": row(f("L0_xattn_b_out")), "x0_gate": rep(f("L0_xattn_gate")),
        },
        "l0f": {"f0_wr": f("L0_ffn_W_r").T, "f0_wk": f("L0_ffn_W_k").T, "f0_wv": f("L0_ffn_W_v").T,
                "f0_mur": col(f("L0_ffn_mu_r")), "f0_muk": col(f("L0_ffn_mu_k"))},
        "l1a": {
            "a1_wq": f("L1_attn_Q").transpose(1, 2, 0).reshape(D, 1024), "a1_wk": f("L1_attn_K").transpose(1, 2, 0).reshape(D, 1024),
            "a1_wv": f("L1_attn_V").transpose(1, 2, 0).reshape(D, 1024),
            "a1_wo": chunked(f("L1_attn_W").transpose(2, 1, 0).reshape(1024, D)),
        },
        "l1x": {
            "x1_wi": chunked(f("L1_xattn_igate_w").T), "x1_wf": chunked(f("L1_xattn_fgate_w").T),
            "x1_bi": f("L1_xattn_igate_b").reshape(8, 1), "x1_bf": f("L1_xattn_fgate_b").reshape(8, 1),
            "x1_lnscale": rep(f("L1_xattn_ln_scale")),
        },
        "l1f": {
            "f1_wv": f("L1_ffn_Wv").T, "f1_bvc": col(f("L1_ffn_bv")), "f1_bvr": row(f("L1_ffn_bv")),
            "f1_wgp": np.concatenate([f("L1_ffn_Wg").T, f("L1_ffn_Wp").reshape(64, D).T], axis=1),
            "f1_bg": rep(f("L1_ffn_bg")), "f1_gr": rep(f("L1_ffn_g_r")), "f1_br": rep(f("L1_ffn_b_r")),
            "f1_gc": rep(f("L1_ffn_g_c")), "f1_bc": rep(f("L1_ffn_b_c")), "f1_alpha": rep(f("L1_ffn_alpha")),
            "f1_w1": f("L1_ffn_W1").reshape(256, D).T, "f1_b1": col(f("L1_ffn_b1")),
            "f1_w2": chunked(f("L1_ffn_W2").transpose(0, 2, 1).reshape(256, D)), "f1_b2": f("L1_ffn_b2"),
        },
        "l2a": {
            "a2_wq4": np.concatenate([wq[:, 0:256], wq[:, 0:256][:, perm]], axis=1),
            "a2_wk4": np.concatenate([rep4(wk, 0), rep4(wk, 1), rep4(wk[:, kperm], 0), rep4(wk[:, kperm], 1)], axis=1),
            "a2_wvg": np.concatenate([f("L2_attn_Wv"), wq[:, 256:512]], axis=1), "a2_wo": chunked(f("L2_attn_Wo")),
        },
        "l2x": {
            "x2_wq": f("L2_xattn_Wq").T, "x2_wk": f("L2_xattn_Wk").T, "x2_wv": f("L2_xattn_Wv").T,
            "x2_wo": f("L2_xattn_Wo").T, "x2_bq": col(f("L2_xattn_bq")), "x2_bk": col(f("L2_xattn_bk")),
            "x2_bv": row(f("L2_xattn_bv")), "x2_bo": row(f("L2_xattn_bo")),
        },
        "l2f": {
            "f2_wr": f("L2_ffn_Wr"), "f2_br": row(f("L2_ffn_br")),
            "f2_wg": f("L2_ffn_Wg").transpose(1, 0, 2).reshape(D, 2048), "f2_wu": f("L2_ffn_Wu").transpose(1, 0, 2).reshape(D, 2048),
            "f2_wd": chunked(f("L2_ffn_Wd").reshape(2048, D)), "f2_bg": col(f("L2_ffn_bg")), "f2_bu": col(f("L2_ffn_bu")),
            "f2_bd3": np.concatenate([f("L2_ffn_bd")] * 3, axis=0), "f2_wgs": f("L2_ffn_Wg_s"), "f2_wus": f("L2_ffn_Wu_s"),
            "f2_wds": f("L2_ffn_Wd_s"), "f2_bgs": f("L2_ffn_bg_s").reshape(64, 1), "f2_bus": f("L2_ffn_bu_s").reshape(64, 1),
            "f2_bds": row(f("L2_ffn_bd_s")),
        },
        "l3a": {"a3_wq": f("L3_attn_W_attn")[:, 0:128], "a3_wk": f("L3_attn_W_attn")[:, 128:256],
                "a3_wv": f("L3_attn_W_attn")[:, 256:384], "a3_wo": f("L3_attn_W_proj")},
        "l3x": {"x3_wq": f("L3_xattn_w_q").T, "x3_wk": f("L3_xattn_w_k").T, "x3_wv": f("L3_xattn_w_v").T,
                "x3_wo": f("L3_xattn_w_o").T},
        "l3f": {
            "f3_wg": f("L3_ffn_Wg").T, "f3_w1": f("L3_ffn_W1").reshape(2048, D).T, "f3_w3": f("L3_ffn_W3").reshape(2048, D).T,
            "f3_w2": chunked(f("L3_ffn_W2").transpose(0, 2, 1).reshape(2048, D)),
        },
        "small": small, "sel32": sel32,
    }
    packed = {}
    for g, pieces in groups.items():
        width = sum(a.shape[1] for a in pieces.values())
        whole, off, names = np.zeros((P, width), np.float32), 0, {}
        for name, a in pieces.items():
            whole[0:a.shape[0], off:off + a.shape[1]] = a
            names[name] = (off, a.shape[0], a.shape[1])
            off += a.shape[1]
        packed[g] = (whole, names)
    return packed, rowconst


def kernel(**inputs):
    import concourse.bacc as bacc
    from concourse.bass_utils import run_bass_kernel_spmd

    nc = bacc.Bacc("TRN2", target_bir_lowering=False, num_devices=1)
    arrays, groups = {}, {}

    def dram(name, a):
        arrays[name] = np.ascontiguousarray(a)
        return nc.dram_tensor(name, a.shape, mybir.dt.from_np(a.dtype), kind="ExternalInput").ap()

    packed, rowconst = lay_out(inputs)
    for g, (whole, names) in packed.items():
        if g in SUBLAYERS[STOP:]:
            continue
        groups[g] = (dram(f"in_{g}", whole), names)
    x = np.asarray(inputs["x"])
    c = np.asarray(inputs["ctx_1024"])
    ctx = {"ctxT": dram("in_ctxT", c.transpose(2, 0, 1)), "ctx": dram("in_ctx", c.transpose(1, 0, 2))}
    m = np.asarray(inputs["mask_BxS2_if1"])
    mask = dram("in_mask", np.broadcast_to(m[None], (P, B, S)))
    out = nc.dram_tensor("out_x", x.shape, F32, kind="ExternalOutput").ap()
    bass_decoder_kernel(nc, groups, ctx, dram("in_x", x), mask, dram("in_rowconst", rowconst), out)
    r = run_bass_kernel_spmd(nc, [arrays], core_ids=[0])
    return r.results[0]["out_x"]
```

```python
from contextlib import ExitStack

import numpy as np

import concourse.bass as bass
from concourse import mybir

F32 = mybir.dt.float32
BF16 = mybir.dt.bfloat16
I32 = mybir.dt.int32
U32 = mybir.dt.uint32
ALU = mybir.AluOpType
ACT = mybir.ActivationFunctionType
AX = mybir.AxisListType

B, S, D = 8, 128, 128
P = 128
HALF = B // 2
TOK = B * S
NEG = -1.0e30
PLACES = (("l0a", "l2a"), ("l0x", "l3f"), ("l1a", "l2f"))
SUBLAYERS = ("l0a", "l0x", "l0f", "l1a", "l1x", "l1f", "l2a", "l2x", "l2f", "l3a", "l3x", "l3f")
STOP = 12
BIG_PARTS = np.array([[999292928.0], [704512.0], [2560.0]])


def spread(ap, count, at=1):
    u = ap.unsqueeze(at)
    shape = list(u.shape)
    shape[at] = count
    return u.to_broadcast(shape)


class Count:

    def __init__(self, sem, keys):
        self.sem, self.value, self.last = sem, {k: n + 1 for n, k in enumerate(keys)}, 0

    def inc(self, key):
        assert self.value[key] == self.last + 1, (key, self.last)
        self.last += 1
        return self.sem, 1

    def at(self, key):
        return self.sem, self.value[key]


class Ring:

    def __init__(self, banks, filled, emptied):
        self.banks, self.filled, self.emptied, self.use, self.taken = banks, filled, emptied, {}, 0

    def open(self, pe, name):
        assert name not in self.use, name
        n = len(self.use)
        self.use[name] = n + 1
        if n >= len(self.banks):
            pe.wait_ge(self.emptied, n - len(self.banks) + 1)
        return self.bank(name)

    def take(self, eng, name):
        self.taken = self.use[name]
        eng.wait_ge(self.filled, self.taken)
        return self.bank(name)

    def bank(self, name):
        return self.banks[(self.use[name] - 1) % len(self.banks)]

    def nth(self, name):
        return self.use[name]


def bass_decoder_kernel(nc, groups, ctx_dram, x_dram, mask_dram, rowconst_dram, out_dram):
    with ExitStack() as stack:
        def sb(name, shape, dt=F32):
            return stack.enter_context(nc.sbuf_tensor(name, shape, dt))[(slice(None),) * len(shape)]

        def sem(name):
            return stack.enter_context(nc.semaphore(name))

        store, piece = {}, {}
        widths = {g: dram.shape[1] for g, (dram, _) in groups.items()}
        shared = {}
        for first, later in PLACES:
            shared[first] = shared[later] = sb(f"w_{first}_{later}", [P, max(widths.get(first, 1), widths.get(later, 1))])
        for g, (dram, names) in groups.items():
            if g in ("sel32", "small"):
                continue
            store[g] = shared[g][:, 0:widths[g]] if g in shared else sb(f"w_{g}", [P, widths[g]], dram.dtype)
            for name, (off, rows, cols) in names.items():
                piece[name] = store[g][0:rows, off:off + cols]
        w = piece
        const_bf = sb("const_bf", [P, widths["sel32"] + widths["small"]], BF16)
        for name in ("sel32", "small"):
            for part, (off, rows, cols) in groups[name][1].items():
                w[part] = const_bf[0:rows, off:off + cols] if name == "sel32" else \
                    const_bf[0:rows, widths["sel32"] + off:widths["sel32"] + off + cols]

        x = sb("x", [P, B, D])
        ctx = sb("ctx", [P, B, D])
        ctxT = sb("ctxT", [P, B, S])
        xT_pair = [sb("xT_even", [P, B, S]), sb("xT_odd", [P, B, S])]
        xT_of = {s: xT_pair[i % 2] for i, s in enumerate(SUBLAYERS)}
        xpad = sb("xpad", [P, B, S + 1])
        xT_of["l0f"] = xpad[:, :, 1:S + 1]
        stats = sb("stats", [P, B, 6])
        mv = sb("mv", [P, B, 2])
        veps = sb("veps", [P, B, 1])
        rstd = sb("rstd", [P, B, 1])
        xhat = sb("xhat", [P, B, D])
        power = sb("power", [P, 1])

        big = [sb(f"big{i}", [P, 2, 8, 132]) for i in range(2)]
        qT = sb("qT", [P, 2, 8, S])
        kT = sb("kT", [P, 2, 8, S])
        V = sb("V", [P, 2, 16 * 65])
        V9 = sb("V9", [P, 4, 16 * 9 + 23])
        V33 = sb("V33", [P, 4, 2, 33])
        prob = sb("prob", [P, 4, 4, S])
        probT = sb("probT", [P, 2, 4, S])
        V17 = prob.rearrange("p m c s -> p (m c s)")[:, 0:B * 136].rearrange("p (b h e) -> p b h e", b=B, e=17)
        store["sel32"] = prob.rearrange("p m c s -> p (m c s)")[:, 0:widths["sel32"]]
        store["small"] = probT.rearrange("p m c s -> p (m c s)")[:, 0:widths["small"]]
        nmax = sb("nmax", [P, 4, 4])
        rden = sb("rden", [P, 4])
        O = sb("O", [P, 2, 16 * 64])
        OT = sb("OT", [P, 2, 8, S])
        small = sb("small", [P, 32])
        wcol = sb("wcol", [P, B, 32])

        psum = stack.enter_context(nc.psum_tensor("psum", [P, 8, 512], F32))
        ring_act = Ring([psum[:, 0, :], psum[:, 1, :]], sem("act_bank_filled"), sem("act_bank_emptied"))
        ring_dve = Ring([psum[:, 2, :], psum[:, 3, :]], sem("dve_bank_filled"), sem("dve_bank_emptied"))
        ring_score = Ring([psum[:, 4, :], psum[:, 5, :]], sem("scores_filled"), sem("scores_emptied"))
        ring_prob = Ring([psum[:, 6, :], psum[:, 7, :]], sem("probT_filled"), sem("probT_emptied"))

        loaded = {g: sem(f"loaded_{g}") for g in groups}
        rowconst_loaded = sem("rowconst_loaded")
        x_loaded, ctx_loaded, mask_loaded, stored = sem("x_loaded"), sem("ctx_loaded"), sem("mask_loaded"), sem("stored")

        subs = SUBLAYERS[:STOP]
        UNITS = {"l0x": 4, "l1a": 4, "l2a": 2, "l2x": 4, "l3a": 4, "l3x": 4}
        norms = [(s, r, b) for s in subs for h in (0, 1) for r in ((0, 1) if s == "l0x" else (0,))
                 for b in range(HALF * h, HALF * h + HALF)]
        stats_ready = Count(sem("stats_ready"), norms)
        rstd_ready = Count(sem("rstd_ready"), norms)
        xhat_ready = Count(sem("xhat_ready"), norms)
        x_final = sem("x_final")
        units = [(s, b, g) for s in subs if s in UNITS for b in range(B) for g in range(UNITS[s])]
        wide_units = [u for u in units if u[0] in ("l0x", "l1a")]
        sums_ready = Count(sem("probability_sums"), wide_units)
        scaled = Count(sem("probs_scaled"), wide_units)
        exped = Count(sem("probs_exped"), units)
        pool_ready = sem("pool_ready")
        dve_chain, act_chain, pool_chain = sem("dve_chain"), sem("act_chain"), sem("pool_chain")
        k_masked = Count(sem("k_masked"), [(s, b, j) for s in subs if s in ("l2a", "l2x", "l3a", "l3x")
                                           for b in range(B) for j in ((0,) if s == "l2a" else (0, 1))])
        narrow = [(s, b) for s in subs if s in ("l2x", "l3a", "l3x") for b in range(B)]
        avT_filled, avT_copied = Count(sem("avT_filled"), narrow), Count(sem("avT_copied"), narrow)
        av_filled, av_scaled = Count(sem("av_filled"), narrow), Count(sem("av_scaled"), narrow)
        out_filled, out_added = Count(sem("out_filled"), narrow), Count(sem("out_added"), narrow)
        tern = sem("ternary_ready")
        const_cast = sem("const_cast")
        mask_ready = sem("mask_ready")
        gate_tanh = sem("gate_tanh")
        chains = {"dve": 0, "act": 0, "pool": 0}

        def events(sem_, keys):
            return Count(sem_, keys)

        l0a_tap = events(sem("l0a_tap"), [(c, n) for n in range(2) for c in range(2)])
        l0a_conv = events(sem("l0a_conv"), [(c, n) for n in range(2) for c in range(2)])
        l0a_silu = events(sem("l0a_silu"), [(c, n) for n in range(2) for c in range(2)])
        l0a_y = events(sem("l0a_y"), [(c, n) for n in range(2) for c in range(2)])
        scales_ready = sem("scales_ready")
        gate_l0x = sem("gate_l0x")
        l0f_mix = events(sem("l0f_mix"), [(n,) for n in range(2)])
        lstm_wkv = sem("lstm_wkv")
        lstm_abs, lstm_log, lstm_G, lstm_A, lstm_M, lstm_expA = (
            events(sem(f"lstm_{name}"), [(0,), (1,)]) for name in ("abs", "log", "G", "A", "M", "expA"))
        lstm_q = events(sem("lstm_q"), [(b,) for b in range(B)])
        lstm_var = events(sem("lstm_var"), [(b,) for b in range(B)])
        lstm_rstd = events(sem("lstm_rstd"), [(b,) for b in range(B)])
        v_ready = sem("v_ready")

        def ln_stats(dve, s, b, r=0):
            src = x if r == 0 else xhat
            link(dve, nc.vector.bn_stats(stats[:, b, :], src[:, b, :]))
            nc.vector.bn_aggr(mv[:, b, :], stats[:, b, :]).then_inc(*stats_ready.inc((s, r, b)))
            dve.wait_ge(*stats_ready.at((s, r, b)))

        def ln_rstd(pool, s, b, r=0):
            pool.wait_ge(*stats_ready.at((s, r, b)))
            plink(pool, nc.gpsimd.tensor_scalar(veps[:, b, :], mv[:, b, 1:2], 1e-5, None, ALU.add))
            nc.gpsimd.tensor_tensor(rstd[:, b, :], veps[:, b, :], power[:, 0:1], ALU.pow).then_inc(
                *rstd_ready.inc((s, r, b)))
            pool.wait_ge(*rstd_ready.at((s, r, b)))

        def ln_xhat(dve, s, b, r=0):
            src = x if r == 0 else xhat
            dve.wait_ge(*rstd_ready.at((s, r, b)))
            nc.vector.tensor_scalar(xhat[:, b, :], src[:, b, :], mv[:, b, 0:1], rstd[:, b, :], ALU.subtract,
                                    ALU.mult).then_inc(*xhat_ready.inc((s, r, b)))
            dve.wait_ge(*xhat_ready.at((s, r, b)))

        def ln_half_stats(dve, s, n, r=0):
            src = x if r == 0 else xhat
            for b in halves[n]:
                ins = nc.vector.bn_stats(stats[:, b, :], src[:, b, :])
            link(dve, ins)
            for b in halves[n]:
                nc.vector.bn_aggr(mv[:, b, :], stats[:, b, :]).then_inc(*stats_ready.inc((s, r, b)))
            dve.wait_ge(*stats_ready.at((s, r, halves[n][-1])))

        def ln_half_xhat(dve, s, n, r=0):
            src = x if r == 0 else xhat
            dve.wait_ge(*rstd_ready.at((s, r, halves[n][-1])))
            for b in halves[n]:
                nc.vector.tensor_scalar(xhat[:, b, :], src[:, b, :], mv[:, b, 0:1], rstd[:, b, :], ALU.subtract,
                                        ALU.mult).then_inc(*xhat_ready.inc((s, r, b)))
            dve.wait_ge(*xhat_ready.at((s, r, halves[n][-1])))

        def ln_half_rstd(pool, s, n, r=0):
            these = slice(HALF * n, HALF * n + HALF)
            pool.wait_ge(*stats_ready.at((s, r, halves[n][-1])))
            plink(pool, nc.gpsimd.tensor_scalar(veps[:, these, :], mv[:, these, 1:2], 1e-5, None, ALU.add))
            for b in halves[n]:
                rstd_ready.inc((s, r, b))
            nc.gpsimd.tensor_tensor(rstd[:, these, :], veps[:, these, :], spread(power[:, 0:1], HALF), ALU.pow
                                    ).then_inc(rstd_ready.sem, HALF)
            pool.wait_ge(*rstd_ready.at((s, r, halves[n][-1])))

        def ln_transpose(pe, s, bs):
            bank = ring_act.open(pe, ("xT", s, bs))
            for i, b in enumerate(bs):
                pe.wait_ge(*xhat_ready.at((s, 1 if s == "l0x" else 0, b)))
                last = nc.tensor.transpose(bank[:, i * S:(i + 1) * S], xhat[:, b, :], w["ident"])
            last.then_inc(ring_act.filled, 1)

        def ln_copy(act, s, bs):
            bank = ring_act.take(act, ("xT", s, bs))
            src = bank[:, 0:len(bs) * S].rearrange("p (b t) -> p b t", t=S)
            dst = xT_of[s][:, bs[0]:bs[-1] + 1, :]
            if s == "l0x":
                act.wait_ge(loaded["l0x"], 16)
                nc.scalar.activation(dst, src, ACT.Identity, scale=w["x0_gamma"],
                                     bias=w["x0_beta"]).then_inc(ring_act.emptied, 1)
            else:
                nc.scalar.activation(dst, src, ACT.Copy).then_inc(ring_act.emptied, 1)

        def xT_use(s, b):
            return next(n for name, n in ring_act.use.items() if name[0:2] == ("xT", s) and b in name[2])

        def xT_wait(pe, s, b):
            pe.wait_ge(ring_act.emptied, xT_use(s, b))

        def link(dve, ins):
            chains["dve"] += 1
            ins.then_inc(dve_chain, 1)
            dve.wait_ge(dve_chain, chains["dve"])

        def alink(act, ins):
            chains["act"] += 1
            ins.then_inc(act_chain, 1)
            act.wait_ge(act_chain, chains["act"])

        def plink(pool, ins):
            chains["pool"] += 1
            ins.then_inc(pool_chain, 1)
            pool.wait_ge(pool_chain, chains["pool"])

        halves = [tuple(range(HALF * n, HALF * n + HALF)) for n in range(2)]

        def next_of(s):
            i = SUBLAYERS.index(s) + 1
            return SUBLAYERS[i] if i < STOP else None

        xin = big[0][:, :, :, 0:131]
        ycv = big[1][:, :, :, 0:S]
        xc = qT
        y4 = kT
        tin = OT[:, 0, 0:2, :].rearrange("p c s -> p (c s)")
        tx = OT[:, 0, 2:6, :].rearrange("p (c o) s -> p c (o s)", c=2)
        tout = OT[:, 0, 6:8, :]
        tern_w = [("l0a_win", 512 * 128, slice(0, 256)), ("l0a_wx", 400 * 256, None), ("l0a_wout", 128 * 256, None)]
        absum = small[:, 0:3]
        scl = small[:, 4:7]
        thr = small[:, 8:11]
        nthr = small[:, 12:15]
        lowmask = O[:, :, :].rearrange("p a (m c) -> p (a m) c", c=256)
        qscale = small[:, 16:20]
        hbias = small[:, 20:22]

        def tensor_l0a(pe):
            pe.wait_ge(scales_ready, 1)
            bank = ring_dve.open(pe, ("scales",))
            pe.wait_ge(loaded["const"], 16)
            nc.tensor.matmul(bank[:, 0:3], w["ones"], absum, start=True, stop=True).then_inc(ring_dve.filled, 1)
            for n in range(2):
                ln_transpose(pe, "l0a", halves[n])
            pe.wait_ge(tern, 1)
            for n in range(2):
                xT_wait(pe, "l0a", halves[n][0])
                for c in range(2):
                    bank = ring_act.open(pe, ("xin", c, n))
                    nc.tensor.matmul(bank, tin[:, c * P:(c + 1) * P], xT_of["l0a"][:, halves[n][0]:halves[n][0] + 4, :],
                                     start=True, stop=True).then_inc(ring_act.filled, 1)
            for n in range(2):
                for c2 in range(2):
                    bank = ring_act.open(pe, ("delta", c2, n))
                    for c in range(2):
                        pe.wait_ge(*l0a_silu.at((c, n)))
                        last = nc.tensor.matmul(bank, tx[:, c, c2 * P:(c2 + 1) * P], xc[:, c, 4 * n:4 * n + 4, :],
                                                start=(c == 0), stop=(c == 1))
                    last.then_inc(ring_act.filled, 1)
            for n in range(2):
                bank = ring_dve.open(pe, ("out", "l0a", n))
                for c in range(2):
                    pe.wait_ge(*l0a_y.at((c, n)))
                for i in range(HALF):
                    for c in range(2):
                        last = nc.tensor.matmul(bank[:, i * D:(i + 1) * D], y4[:, c, 4 * n + i, :], tout[:, c, :],
                                                start=(c == 0), stop=(c == 1))
                last.then_inc(ring_dve.filled, 1)
            finish_pe(pe, "l0a")

        def finish_pe(pe, s):
            if next_of(s):
                for n in range(1 if next_of(s) in UNITS else 2):
                    ln_transpose(pe, next_of(s), halves[n])

        def finish_act(act, s):
            if next_of(s):
                for n in range(1 if next_of(s) in UNITS else 2):
                    ln_copy(act, next_of(s), halves[n])

        def finish_pool(pool, s):
            if next_of(s):
                for n in range(2):
                    for r in ((0, 1) if next_of(s) == "l0x" else (0,)):
                        ln_half_rstd(pool, next_of(s), n, r)

        def finish_dve(dve, s, n):
            if not next_of(s):
                return
            ln_half_stats(dve, next_of(s), n)
            if n == 1 and next_of(s) in UNITS:
                return
            ln_half_xhat(dve, next_of(s), n)
            if next_of(s) == "l0x":
                ln_half_stats(dve, "l0x", n, 1)
                ln_half_xhat(dve, "l0x", n, 1)

        def scalar_l0a(act):
            for n in range(2):
                ln_copy(act, "l0a", halves[n])
            act.wait_ge(loaded["l0a"], 16)
            act.wait_ge(tern, 1)
            act.wait_ge(pool_ready, 1)
            for n in range(2):
                for c in range(2):
                    bank = ring_act.take(act, ("xin", c, n))
                    nc.scalar.activation(xin[:, c, 4 * n:4 * n + 4, 3:131], bank.rearrange("p (b t) -> p b t", t=S),
                                         ACT.Identity, scale=scl[:, 0:1], bias=w["l0a_bin"][:, c:c + 1]
                                         ).then_inc(ring_act.emptied, 1)
            for n in range(2):
                for c in range(2):
                    act.wait_ge(ring_act.emptied, ring_act.nth(("xin", c, n)))
                    nc.scalar.activation(ycv[:, c, 4 * n:4 * n + 4, :], xin[:, c, 4 * n:4 * n + 4, 3:131], ACT.Identity,
                                         scale=w["l0a_wconv"][:, 4 * c + 3:4 * c + 4], bias=w["l0a_bconv"][:, c:c + 1]
                                         ).then_inc(*l0a_tap.inc((c, n)))
            for n in range(2):
                for c in range(2):
                    act.wait_ge(*l0a_conv.at((c, n)))
                    nc.scalar.activation(xc[:, c, 4 * n:4 * n + 4, :], ycv[:, c, 4 * n:4 * n + 4, :], ACT.Silu
                                         ).then_inc(*l0a_silu.inc((c, n)))
            for n in range(2):
                for c in range(2):
                    bank = ring_act.take(act, ("delta", c, n))
                    nc.scalar.activation(y4[:, c, 4 * n:4 * n + 4, :], bank.rearrange("p (b t) -> p b t", t=S),
                                         ACT.Tanh, scale=qscale[:, 0:1], bias=hbias[:, c:c + 1]
                                         ).then_inc(ring_act.emptied, 1)
            finish_act(act, "l0a")

        def vector_l0a(dve):
            dve.wait_ge(x_loaded, 16)
            for n in range(2):
                ln_half_stats(dve, "l0a", n)
            for n in range(2):
                ln_half_xhat(dve, "l0a", n)
            dve.wait_ge(loaded["const"], 16)
            dve.wait_ge(loaded["l0a"], 16)
            for i, (name, _, _) in enumerate(tern_w):
                last = nc.vector.tensor_reduce(absum[:, i:i + 1], w[name], AX.X, ALU.add, apply_absolute_value=True)
            last.then_inc(scales_ready, 1)
            dve.wait_ge(scales_ready, 1)
            bank = ring_dve.take(dve, ("scales",))
            for i, (_, count, _) in enumerate(tern_w):
                last = nc.vector.tensor_scalar(scl[:, i:i + 1], bank[:, i:i + 1], 1.0 / count, 1e-5, ALU.mult, ALU.max)
            last.then_inc(ring_dve.emptied, 1)
            dve.wait_ge(ring_dve.emptied, ring_dve.nth(("scales",)))
            link(dve, nc.vector.tensor_scalar(thr, scl, 0.5, None, ALU.mult))
            link(dve, nc.vector.tensor_scalar(nthr, scl, -0.5, None, ALU.mult))
            link(dve, nc.vector.tensor_scalar(qscale[:, 0:1], scl[:, 1:2], 0.5, None, ALU.mult))
            link(dve, nc.vector.tensor_scalar(qscale[:, 1:2], scl[:, 2:3], 0.5, None, ALU.mult))
            link(dve, nc.vector.tensor_scalar(hbias, w["l0a_bx"], 0.5, None, ALU.mult))
            parts = [(tin, w["l0a_win"][:, 0:256], 0)]
            parts += [(tx[:, c, :], w["l0a_wx"][:, c * 400:c * 400 + 256], 1) for c in range(2)]
            parts += [(tout[:, c, :], w["l0a_wout"][:, c * P:(c + 1) * P], 2) for c in range(2)]
            for m, (dst, src, i) in enumerate(parts):
                low = lowmask[:, m, 0:src.shape[1]]
                link(dve, nc.vector.tensor_scalar(low, src, nthr[:, i:i + 1], None, ALU.is_lt))
                last = nc.vector.scalar_tensor_tensor(out=dst, in0=src, scalar=thr[:, i:i + 1], in1=low,
                                                      op0=ALU.is_gt, op1=ALU.subtract)
            last.then_inc(tern, 1)
            dve.wait_ge(tern, 1)
            for n in range(2):
                for c in range(2):
                    dve.wait_ge(*l0a_tap.at((c, n)))
                    y = ycv[:, c, 4 * n:4 * n + 4, :]
                    xi = xin[:, c, 4 * n:4 * n + 4, :]
                    wc = w["l0a_wconv"]
                    for j in range(3):
                        ins = nc.vector.scalar_tensor_tensor(out=y, in0=xi[:, :, j:j + S],
                                                             scalar=wc[:, 4 * c + j:4 * c + j + 1], in1=y,
                                                             op0=ALU.mult, op1=ALU.add)
                        if j < 2:
                            link(dve, ins)
                    ins.then_inc(*l0a_conv.inc((c, n)))
                    dve.wait_ge(*l0a_conv.at((c, n)))
            for n in range(2):
                for c in range(2):
                    dve.wait_ge(ring_act.emptied, ring_act.nth(("delta", c, n)))
                    dve.wait_ge(*l0a_silu.at((c, n)))
                    t = y4[:, c, 4 * n:4 * n + 4, :]
                    nc.vector.scalar_tensor_tensor(out=t, in0=t, scalar=1.0, in1=xc[:, c, 4 * n:4 * n + 4, :],
                                                   op0=ALU.add, op1=ALU.mult).then_inc(*l0a_y.inc((c, n)))
                    dve.wait_ge(*l0a_y.at((c, n)))
            for n in range(2):
                bank = ring_dve.take(dve, ("out", "l0a", n))
                xs = x[:, 4 * n:4 * n + 4, :]
                ins = nc.vector.scalar_tensor_tensor(out=xs, in0=bank.rearrange("p (b d) -> p b d", d=D),
                                                     scalar=qscale[:, 1:2], in1=xs, op0=ALU.mult, op1=ALU.add)
                ins.then_inc(ring_dve.emptied, 1)
                dve.wait_ge(ring_dve.emptied, ring_dve.nth(("out", "l0a", n)))
                link(dve, nc.vector.tensor_tensor(xs, xs, spread(w["l0a_bout"], 4), ALU.add))
                finish_dve(dve, "l0a", n)

        def gpsimd_l0a(pool):
            plink(pool, nc.gpsimd.memset(power[:, 0:1], -0.5))
            plink(pool, nc.gpsimd.memset(xin[:, :, :, 0:3], 0.0))
            plink(pool, nc.gpsimd.memset(xpad[:, :, 0:1], 0.0))
            plink(pool, nc.gpsimd.memset(V9[:, :, :], 1.0))
            nc.gpsimd.memset(V33[:, :, :, :], 1.0).then_inc(pool_ready, 1)
            pool.wait_ge(pool_ready, 1)
            for n in range(2):
                ln_half_rstd(pool, "l0a", n)
            pool.wait_ge(loaded["small"], 16)
            pool.wait_ge(loaded["sel32"], 16)
            nc.gpsimd.tensor_copy(const_bf[:, widths["sel32"]:], store["small"]).then_inc(const_cast, 1)
            nc.gpsimd.tensor_copy(const_bf[:, 0:widths["sel32"]], store["sel32"]).then_inc(const_cast, 1)
            pool.wait_ge(const_cast, 2)
            finish_pool(pool, "l0a")

        SPEC = {
            "l0x": dict(kind="wide", dh=64, wq="x0_wq", wk="x0_wk", wv="x0_wv", wo="x0_wo", kv="ctx", causal=False,
                        scale=64 ** -0.5),
            "l1a": dict(kind="wide", dh=64, wq="a1_wq", wk="a1_wk", wv="a1_wv", wo="a1_wo", kv="x", causal=True,
                        scale=0.5 / 64, alpha=0.5 ** 0.5 * 2 ** 0.5 / 16),
            "l2a": dict(kind="rope", dh=32, kv="x", causal=False, scale=32 ** -0.5, alpha=0.5),
            "l2x": dict(kind="narrow", dh=8, wq="x2_wq", wk="x2_wk", wv="x2_wv", wo="x2_wo", kv="ctx", causal=False,
                        scale=8 ** -0.5, alpha=1.0, bias=True),
            "l3a": dict(kind="narrow", dh=8, wq="a3_wq", wk="a3_wk", wv="a3_wv", wo="a3_wo", kv="x", causal=True,
                        scale=8 ** -0.5, alpha=1.0),
            "l3x": dict(kind="narrow", dh=8, wq="x3_wq", wk="x3_wk", wv="x3_wv", wo="x3_wo", kv="ctx", causal=False,
                        scale=1.0, qscale=8 ** -0.5, alpha=1.0, masked=True),
        }

        TAIL = {"wide": ((5, "out"), (6, "xhat"), (7, "norm"))}
        TAIL["rope"] = ((5, "outT"), (6, "out"), (7, "xhat"), (8, "norm"))
        TAIL["narrow"] = ((4, "back"), (5, "outT"), (6, "out"), (8, "xhat"), (10, "norm"))

        def attention_steps(run):
            plan, at_tick, base = {}, {}, 0
            late = ("late_xhat", "late_xhat2", "late_norm") if run[0] == "l0x" else ("late_xhat", "late_norm")
            for t, step in enumerate(late):
                plan[t] = [(run[0], step, 0, 0)]
            for s in run:
                U, kind = UNITS[s], SPEC[s]["kind"]
                if s != run[0] and SPEC[run[0]]["kind"] != kind:
                    base += 3
                ahead, ahead_v = {"wide": (2, -1), "narrow": (4, None), "rope": (4, 1)}[kind]
                for b in range(B):
                    first = base + U * b - 1
                    if b == 0:
                        plan.setdefault(max(first - ahead, -1), []).append((s, "begin", 0, 0))
                    plan.setdefault(max(first - ahead, -1), []).append((s, "project", b, 0))
                    if ahead_v is not None:
                        plan.setdefault(max(first - ahead_v, -1), []).append((s, "project_v", b, 0))
                    for d, step in TAIL[kind]:
                        plan.setdefault(first + U + d, []).append((s, step, b, 0))
                    for g in range(U):
                        at_tick[base + U * b + g] = (s, b, g)
                if s == "l1a" and next_of(s):
                    first = base + U * HALF + TAIL[kind][-1][0]
                    for t, step in zip((1, 2, 4, 5, 7, 7), GATE_PARTS):
                        plan.setdefault(first + t, []).append((s, step, 0, 0))
                    for b in range(2):
                        plan.setdefault(first + 4 + b, []).append((s, "queries", b, 0))
                if s == "l2x" and next_of(s):
                    first = base + U * HALF + TAIL[kind][-1][0]
                    plan.setdefault(first, []).append((s, "router_logits", 0, 0))
                    for part in range(ROUTER_PIECES):
                        plan.setdefault(first + 1 + part, []).append((s, "router", 0, part))
                base += U * B

            def unit(step, tick):
                if tick in at_tick:
                    s, b, g = at_tick[tick]
                    yield s, step, b, g

            yield from plan.pop(-1)
            yield from unit("score", 0)
            for t in range(base + TAIL[kind][-1][0]):
                yield from unit("score", t + 1)
                yield from unit("softmax", t)
                for s, step, b, g in unit("scale", t - 1):
                    if SPEC[s]["kind"] == "wide":
                        yield s, step, b, g
                steps = plan.pop(t, [])
                yield from (step for step in steps if step[1] != "back")
                yield from unit("transpose", t - 2)
                yield from (step for step in steps if step[1] == "back")
                yield from unit("exp", t)
                for s, step, b, g in unit("turn_back", t - 4):
                    if SPEC[s]["kind"] == "rope":
                        yield s, step, b, g
                for s, step, b, g in unit("value", t - 3):
                    if SPEC[s]["kind"] != "wide" or g % 2:
                        yield s, step, b, g
                for s, step, b, g in unit("copy", t - 3):
                    if SPEC[s]["kind"] == "rope" or SPEC[s]["kind"] == "narrow" and g == UNITS[s] - 1:
                        yield s, step, b, g
            assert not plan

        src_of = {"ctx": lambda s: ctxT, "x": lambda s: xT_of[s]}
        mask01 = big[0][:, 0, :, 0:S]
        maskrow = sb("maskrow", [P, B, S], BF16)
        mask_i = xpad[:, :, :].rearrange("p b t -> p (b t)").bitcast(I32)[:, 0:TOK].rearrange("p (b t) -> p b t", t=S)
        kraw = sb("kraw", [P, 3, 2, S])
        kmask = sb("kmask", [P, 3, 2, 4, S])
        rowconst = kmask.rearrange("p m a c s -> p m (a c s)")
        headrows = rowconst[:, 0, :]
        notfirst, negfirst = (rowconst[0:8, i, :] for i in (1, 2))
        rope1 = V[:, 0, 0:1024].rearrange("p (a c s) -> p a c s", a=2, s=S)
        rope2 = V[:, 1, 0:1024].rearrange("p (a c s) -> p a c s", a=2, s=S)
        gate2 = kT[:, 1, :, :].rearrange("p (a c) s -> p a (c s)", a=4)
        tgate = sb("tgate", [P, 1])

        def heads_of(s, g):
            if SPEC[s]["kind"] == "wide":
                return slice(8 * (g // 2) + g % 2, 8 * (g // 2) + g % 2 + 7, 2)
            return slice(4 * g, 4 * g + 4)

        def q3(b):
            return qT[:, b % 4 // 2, b % 4 % 2 * 4:b % 4 % 2 * 4 + 4, :]

        def kmask_of(b):
            return kmask[:, b % 4, :, :, :] if b % 4 < 3 else kT[:, 0, :, :].rearrange("p (a c) s -> p a c s", a=2)

        def keys16(b, j):
            return kmask_of(2 * (b % 2) + j).rearrange("p a c s -> p (a c) s")

        def v_view(s, b):
            return {"wide": V[:, b % 2, :].rearrange("p (h e) -> p h e", e=65), "narrow": V9[:, b % 4, 0:144].rearrange("p (h e) -> p h e", e=9),
                    "rope": V33[:, b % 4, :, :]}[SPEC[s]["kind"]]

        def seq_bank(b):
            return psum[:, 2 + b % 2, :]

        avT = O[:, :, 512:1024]

        def probT_of(s, n):
            if SPEC[s]["kind"] == "wide":
                return O[:, n // 2, n % 2 * 512:n % 2 * 512 + 512].rearrange("p (c t) -> p c t", t=S)
            return probT[:, n % 2, :, :]

        def tensor_attention(pe, run):
            pe.wait_ge(const_cast, 2)
            pe.wait_ge(ctx_loaded, 32)
            for s, step, b, g in attention_steps(run):
                sp = SPEC[s]
                kind, kvT = sp["kind"], src_of[sp["kv"]](s)
                xT = xT_of[s]
                if step in GATE_PARTS:
                    gates_pe(pe, step, 0)
                elif step == "begin":
                    pe.wait_ge(loaded[s], 16)
                elif step == "late_norm":
                    ln_transpose(pe, s, halves[1])
                elif step == "project" and kind == "wide":
                    xT_wait(pe, s, b)
                    for ring, what, wt, src in ((ring_act, "q", sp["wq"], xT), (ring_dve, "k", sp["wk"], kvT)):
                        for i in range(2):
                            bank = ring.open(pe, (what, s, b, i))
                            for c in range(4):
                                last = nc.tensor.matmul(bank[:, c * S:(c + 1) * S],
                                                        w[wt][:, (4 * i + c) * P:(4 * i + c + 1) * P], src[:, b, :],
                                                        start=True, stop=True)
                            last.then_inc(ring.filled, 1)
                elif step == "project_v" and kind == "wide":
                    for i in range(2):
                        bank = ring_act.open(pe, ("v", s, b, i))
                        nc.tensor.matmul(bank, kvT[:, b, :], w[sp["wv"]][:, i * 512:(i + 1) * 512], start=True,
                                         stop=True).then_inc(ring_act.filled, 1)
                elif step == "project" and kind == "narrow":
                    xT_wait(pe, s, b)
                    bank = ring_act.open(pe, ("qkv", s, b))
                    nc.tensor.matmul(bank[:, 0:S], w[sp["wq"]], xT[:, b, :], start=True, stop=True)
                    nc.tensor.matmul(bank[:, S:2 * S], w[sp["wk"]], kvT[:, b, :], start=True, stop=True)
                    last = nc.tensor.matmul(bank[:, 2 * S:3 * S], kvT[:, b, :], w[sp["wv"]], start=True,
                                            stop=not sp.get("bias"))
                    if sp.get("bias"):
                        last = nc.tensor.matmul(bank[:, 2 * S:3 * S], w["ones"][0:1, :], w["x2_bv"], start=False,
                                                stop=True)
                    last.then_inc(ring_act.filled, 1)
                elif step == "project":
                    xT_wait(pe, s, b)
                    for what, wt in (("q", "a2_wq4"), ("k", "a2_wk4")):
                        bank = ring_dve.open(pe, (what, s, b))
                        for c in range(4):
                            last = nc.tensor.matmul(bank[:, c * S:(c + 1) * S], w[wt][:, c * P:(c + 1) * P],
                                                    xT[:, b, :], start=True, stop=True)
                        last.then_inc(ring_dve.filled, 1)
                elif step == "project_v" and kind == "rope":
                    bank = ring_dve.open(pe, ("vg", s, b))
                    nc.tensor.matmul(bank[:, 0:320], xT[:, b, :], w["a2_wvg"], start=True, stop=True).then_inc(
                        ring_dve.filled, 1)
                elif step == "score":
                    if g == 0:
                        if kind == "wide":
                            pe.wait_ge(ring_act.emptied, ring_act.nth(("q", s, b, 1)))
                            pe.wait_ge(ring_dve.emptied, ring_dve.nth(("k", s, b, 1)))
                        else:
                            if kind == "narrow":
                                pe.wait_ge(ring_act.emptied, ring_act.nth(("qkv", s, b)))
                            else:
                                pe.wait_ge(ring_dve.emptied, ring_dve.nth(("k", s, b)))
                            pe.wait_ge(*k_masked.at((s, b, 0)))
                    if kind == "narrow" and g == 2:
                        pe.wait_ge(*k_masked.at((s, b, 1)))
                    bank = ring_score.open(pe, ("S", s, b, g))
                    open_ = True
                    if sp["causal"]:
                        nc.tensor.matmul(bank, w["ident_bf"], spread(w["causal_bf"], 4), start=True, stop=False)
                        open_ = False
                    if sp.get("masked"):
                        if b == 0 and g == 0:
                            pe.wait_ge(mask_ready, 1)
                        nc.tensor.matmul(bank, w["ones_bf"], spread(maskrow[:, b, :], 4), start=True, stop=False)
                        open_ = False
                    if kind == "wide":
                        i, p = g // 2, g % 2
                        for c in range(4):
                            last = nc.tensor.matmul(bank[:, c * S:(c + 1) * S], qT[64 * p:64 * p + 64, b % 2, 4 * i + c, :],
                                                    kT[64 * p:64 * p + 64, b % 2, 4 * i + c, :], start=open_,
                                                    stop=open_ or c == 3)
                    elif kind == "narrow":
                        last = nc.tensor.matmul(bank, q3(b)[:, 0, :], keys16(b, g // 2)[:, g % 2 * 4:g % 2 * 4 + 4, :],
                                                start=open_, stop=True)
                    else:
                        last = nc.tensor.matmul(bank, q3(b)[:, g, :], kmask_of(b)[:, g, :, :], start=True, stop=True)
                    last.then_inc(ring_score.filled, 1)
                elif step == "transpose":
                    bank = ring_prob.open(pe, ("T", s, b, g))
                    pe.wait_ge(*(scaled if kind == "wide" else exped).at((s, b, g)))
                    n = units.index((s, b, g)) % 4
                    for c in range(4):
                        last = nc.tensor.transpose(bank[:, c * S:(c + 1) * S], prob[:, n, c, :], w["ident"])
                    last.then_inc(ring_prob.filled, 1)
                elif step == "value" and kind == "narrow":
                    bank = seq_bank(b)
                    if g == 0 and b >= 2:
                        pe.wait_ge(*out_added.at((s, b - 2)))
                    elif g == 0 and s != run[0] and SPEC[run[0]]["kind"] == "narrow":
                        pe.wait_ge(*out_added.at((run[0], B - 2 + b)))
                    elif g == 0:
                        pe.wait_ge(ring_dve.emptied, len(ring_dve.use))
                    pe.wait_ge(ring_prob.emptied, ring_prob.nth(("T", s, b, g)))
                    n = units.index((s, b, g)) % 2
                    for c in range(4):
                        h = 4 * g + c
                        last = nc.tensor.matmul(bank[32 * c:32 * c + 32, g * S:(g + 1) * S],
                                                V9[:, b % 4, 9 * h:9 * h + 32], probT[:, n, c, :], start=True,
                                                stop=True)
                    if g == 3:
                        last.then_inc(*avT_filled.inc((s, b)))
                elif step == "back":
                    pe.wait_ge(*avT_copied.at((s, b)))
                    for i in range(4):
                        last = nc.tensor.transpose(seq_bank(b)[:, i * S:(i + 1) * S], avT[:, b % 2, i * S:(i + 1) * S],
                                                   w["ident"])
                    last.then_inc(*av_filled.inc((s, b)))
                elif step == "value" and kind == "rope":
                    bank = ring_act.open(pe, ("AVT", s, b, g))
                    pe.wait_ge(ring_prob.emptied, ring_prob.nth(("T", s, b, g)))
                    if g == 0:
                        pe.wait_ge(ring_dve.emptied, ring_dve.nth(("vg", s, b)))
                    nc.tensor.matmul(bank[0:33, :], V33[:, b % 4, g, :], probT[:, units.index((s, b, g)) % 2, :, :],
                                     start=True, stop=True).then_inc(ring_act.filled, 1)
                elif step == "turn_back":
                    bank = ring_dve.open(pe, ("AV", s, b, g))
                    pe.wait_ge(ring_act.emptied, ring_act.nth(("AVT", s, b, g)))
                    for c in range(4):
                        last = nc.tensor.transpose(bank[:, 33 * c:33 * c + 33], avT[0:33, g, c * S:(c + 1) * S],
                                                   w["ident"][0:33, 0:33])
                    last.then_inc(ring_dve.filled, 1)
                elif step == "value":
                    i = g // 2
                    bank = ring_act.open(pe, ("OT", s, b, i))
                    pe.wait_ge(ring_prob.emptied, ring_prob.nth(("T", s, b, g)))
                    if i == 0:
                        pe.wait_ge(ring_act.emptied, ring_act.nth(("v", s, b, 1)))
                    for c in range(4):
                        for p in range(2):
                            n = units.index((s, b, 2 * i + p)) % 4
                            last = nc.tensor.matmul(bank[64 * p:64 * p + 64, c * S:(c + 1) * S],
                                                    v_view(s, b)[:, heads_of(s, 2 * i + p).start + 2 * c, 0:64],
                                                    probT_of(s, n)[:, c, :], start=True, stop=True)
                    last.then_inc(ring_act.filled, 1)
                elif step == "outT":
                    chunks = {"rope": 2, "narrow": 1}[kind]
                    if kind == "narrow":
                        pe.wait_ge(*av_scaled.at((s, b)))
                    else:
                        pe.wait_ge(ring_dve.emptied, ring_dve.nth(("AV", s, b, UNITS[s] - 1)))
                    bank = ring_act.open(pe, ("OT", s, b, 0))
                    for c in range(chunks):
                        last = nc.tensor.transpose(bank[:, c * S:(c + 1) * S], O[:, b % 2, c * P:(c + 1) * P],
                                                   w["ident"])
                    last.then_inc(ring_act.filled, 1)
                elif step == "out":
                    chunks = {"wide": 8, "rope": 2, "narrow": 1}[kind]
                    wo = {"rope": "a2_wo"}.get(kind) or sp["wo"]
                    bank = seq_bank(b) if kind == "narrow" else ring_dve.open(pe, ("out", s, b))
                    bias = {"l0x": "x0_bout", "l2x": "x2_bo"}.get(s)
                    pe.wait_ge(ring_act.emptied, ring_act.nth(("OT", s, b, 1 if kind == "wide" else 0)))
                    for c in range(chunks):
                        last = nc.tensor.matmul(bank[:, 0:D], OT[:, b % 2, c, :], w[wo][:, c * D:(c + 1) * D],
                                                start=(c == 0), stop=(c == chunks - 1) and not bias)
                    if bias:
                        last = nc.tensor.matmul(bank[:, 0:D], w["ones"][0:1, :], w[bias], start=False, stop=True)
                    if kind == "narrow":
                        last.then_inc(*out_filled.inc((s, b)))
                    else:
                        last.then_inc(ring_dve.filled, 1)
                elif step == "norm" and next_of(s):
                    ln_transpose(pe, next_of(s), (b,))
                elif step == "router_logits":
                    router_pe(pe, 0)
            if SPEC[run[-1]]["kind"] == "narrow":
                for b in (B - 2, B - 1):
                    pe.wait_ge(*out_added.at((run[-1], b)))

        def scalar_attention(act, run):
            for s, step, b, g in attention_steps(run):
                sp = SPEC[s]
                kind = sp["kind"]
                if step in GATE_PARTS:
                    gates_act(act, step, 0)
                elif step == "begin":
                    act.wait_ge(loaded[s], 16)
                    if s == "l0x":
                        nc.scalar.activation(tgate[:, :], w["x0_gate"], ACT.Tanh).then_inc(gate_l0x, 1)
                elif step == "late_norm":
                    ln_copy(act, s, halves[1])
                elif step == "project" and kind == "wide":
                    for i in range(2):
                        bank = ring_act.take(act, ("q", s, b, i))
                        nc.scalar.activation(qT[:, b % 2, 4 * i:4 * i + 4, :], bank.rearrange("p (c t) -> p c t", t=S),
                                             ACT.Copy).then_inc(ring_act.emptied, 1)
                elif step == "project_v" and kind == "wide":
                    for i in range(2):
                        bank = ring_act.take(act, ("v", s, b, i))
                        nc.scalar.activation(v_view(s, b)[:, 8 * i:8 * i + 8, 0:64],
                                             bank.rearrange("p (h e) -> p h e", e=64), ACT.Copy
                                             ).then_inc(ring_act.emptied, 1)
                elif step == "project" and kind == "narrow":
                    bank = ring_act.take(act, ("qkv", s, b))
                    if sp.get("bias"):
                        nc.scalar.activation(kraw[:, b % 3, 0, :], bank[:, S:2 * S], ACT.Identity, bias=w["x2_bk"])
                        nc.scalar.activation(q3(b)[:, 0, :], bank[:, 0:S], ACT.Identity, bias=w["x2_bq"])
                    else:
                        nc.scalar.activation(kraw[:, b % 3, 0, :], bank[:, S:2 * S], ACT.Copy)
                        nc.scalar.activation(q3(b)[:, 0, :], bank[:, 0:S], ACT.Copy, scale=sp.get("qscale", 1.0))
                    nc.scalar.activation(v_view(s, b)[:, :, 0:8], bank[:, 2 * S:3 * S].rearrange("p (h e) -> p h e", e=8),
                                         ACT.Copy).then_inc(ring_act.emptied, 1)
                elif step == "project_v":
                    act.wait_ge(ring_dve.filled, ring_dve.nth(("vg", s, b)))
                    bank = ring_dve.bank(("vg", s, b))
                    nc.scalar.activation(v_view(s, b)[:, :, 0:32], bank[:, 0:64].rearrange("p (h e) -> p h e", e=32),
                                         ACT.Copy)
                    nc.scalar.activation(gate2[:, b % 4, :], bank[:, 64:320], ACT.Tanh, scale=0.5).then_inc(gate_tanh, 1)
                elif step == "exp":
                    n = units.index((s, b, g)) % 4
                    act.wait_ge(ring_score.emptied, ring_score.nth(("S", s, b, g)))
                    nc.scalar.activation(prob[:, n, :, :], prob[:, n, :, :], ACT.Exp, scale=sp["scale"]
                                         ).then_inc(*exped.inc((s, b, g)))
                elif step == "transpose":
                    bank = ring_prob.take(act, ("T", s, b, g))
                    n = units.index((s, b, g)) % 4
                    nc.scalar.activation(probT_of(s, n), bank.rearrange("p (c t) -> p c t", t=S), ACT.Copy
                                         ).then_inc(ring_prob.emptied, 1)
                elif step == "copy" and kind == "rope":
                    bank = ring_act.take(act, ("AVT", s, b, g))
                    nc.scalar.activation(avT[0:33, g, :], bank[0:33, :], ACT.Copy).then_inc(ring_act.emptied, 1)
                elif step == "copy":
                    act.wait_ge(*avT_filled.at((s, b)))
                    nc.scalar.activation(avT[:, b % 2, :], seq_bank(b), ACT.Copy).then_inc(*avT_copied.inc((s, b)))
                elif step == "value" and kind == "wide":
                    bank = ring_act.take(act, ("OT", s, b, g // 2))
                    nc.scalar.activation(OT[:, b % 2, 4 * (g // 2):4 * (g // 2) + 4, :],
                                         bank.rearrange("p (c t) -> p c t", t=S), ACT.Copy
                                         ).then_inc(ring_act.emptied, 1)
                elif step == "outT":
                    chunks = {"rope": 2, "narrow": 1}[kind]
                    bank = ring_act.take(act, ("OT", s, b, 0))
                    nc.scalar.activation(OT[:, b % 2, 0:chunks, :],
                                         bank[:, 0:chunks * S].rearrange("p (c t) -> p c t", t=S), ACT.Copy
                                         ).then_inc(ring_act.emptied, 1)
                elif step == "norm" and next_of(s):
                    ln_copy(act, next_of(s), (b,))
                elif step == "router_logits":
                    router_act(act, 0)

        def vector_attention(dve, run):
            dve.wait_ge(const_cast, 2)
            dve.wait_ge(pool_ready, 1)
            for s, step, b, g in attention_steps(run):
                sp = SPEC[s]
                kind = sp["kind"]
                if step in GATE_PARTS:
                    gates_dve(dve, step, 0)
                elif step == "begin" and s == "l0x":
                    dve.wait_ge(gate_l0x, 1)
                elif step == "late_xhat":
                    ln_half_xhat(dve, s, 1)
                    if s == "l0x":
                        ln_half_stats(dve, s, 1, 1)
                elif step == "late_xhat2":
                    ln_half_xhat(dve, s, 1, 1)
                elif step == "begin" and sp.get("masked"):
                    dve.wait_ge(mask_loaded, 16)
                    link(dve, nc.vector.tensor_scalar(mask01, mask_i[:, :, :], 0, None, ALU.not_equal))
                    nc.vector.tensor_scalar(maskrow[:, :, :], mask01, 1.0, w["bigparts"], ALU.subtract,
                                            ALU.mult).then_inc(mask_ready, 1)
                    dve.wait_ge(mask_ready, 1)
                elif step == "project" and kind == "wide":
                    for i in range(2):
                        bank = ring_dve.take(dve, ("k", s, b, i))
                        nc.vector.tensor_copy(kT[:, b % 2, 4 * i:4 * i + 4, :], bank.rearrange("p (c t) -> p c t", t=S)
                                              ).then_inc(ring_dve.emptied, 1)
                        dve.wait_ge(ring_dve.emptied, ring_dve.taken)
                elif step == "project" and kind == "rope":
                    for j, what in enumerate(("q", "k")):
                        bank = ring_dve.take(dve, (what, s, b)).rearrange("p (c t) -> p c t", t=S)
                        if j == 0 and b >= 2:
                            dve.wait_ge(*k_masked.at((s, b - 2, 0)))
                        link(dve, nc.vector.tensor_tensor(rope1[:, b % 2, 2 * j:2 * j + 2, :], bank[:, 0:2, :],
                                                spread(w["cos"], 2), ALU.mult))
                        nc.vector.tensor_tensor(rope2[:, b % 2, 2 * j:2 * j + 2, :], bank[:, 2:4, :],
                                                spread(w["sin"], 2), ALU.mult).then_inc(ring_dve.emptied, 1)
                        dve.wait_ge(ring_dve.emptied, ring_dve.taken)
                elif step == "project_v" and kind == "rope":
                    bank = ring_dve.take(dve, ("vg", s, b))
                    dve.wait_ge(gate_tanh, b + 1)
                    nc.vector.scalar_tensor_tensor(out=gate2[:, b % 4, :], in0=gate2[:, b % 4, :], scalar=1.0,
                                                   in1=bank[:, 64:320], op0=ALU.add, op1=ALU.mult
                                                   ).then_inc(ring_dve.emptied, 1)
                    dve.wait_ge(ring_dve.emptied, ring_dve.taken)
                elif step == "softmax":
                    bank = ring_score.take(dve, ("S", s, b, g)).rearrange("p (c t) -> p c t", t=S)
                    n = units.index((s, b, g)) % 4
                    u = units.index((s, b, g))
                    if u >= 4:
                        dve.wait_ge(ring_prob.filled, ring_prob.nth(("T",) + units[u - 4]))
                    link(dve, nc.vector.tensor_reduce(nmax[:, n, :], bank, AX.X, ALU.max))
                    nc.vector.tensor_tensor(prob[:, n, :, :], bank, spread(nmax[:, n, :], S, 2), ALU.subtract
                                            ).then_inc(ring_score.emptied, 1)
                    dve.wait_ge(ring_score.emptied, ring_score.taken)
                elif step == "back":
                    dve.wait_ge(*av_filled.at((s, b)))
                    av = seq_bank(b).rearrange("p (h e) -> p h e", e=32)
                    den = small[:, 0:16]
                    link(dve, nc.vector.reciprocal(den, av[:, :, 8:9].rearrange("p h e -> p (h e)")))
                    nc.vector.tensor_tensor(O[:, b % 2, 0:128].rearrange("p (h e) -> p h e", e=8), av[:, :, 0:8],
                                            spread(den, 8, 2), ALU.mult).then_inc(*av_scaled.inc((s, b)))
                    dve.wait_ge(*av_scaled.at((s, b)))
                elif step == "scale":
                    n = units.index((s, b, g)) % 4
                    dve.wait_ge(*exped.at((s, b, g)))
                    link(dve, nc.vector.tensor_reduce(nmax[:, n, :], prob[:, n, :, :], AX.X, ALU.add))
                    nc.vector.reciprocal(nmax[:, n, :], nmax[:, n, :]).then_inc(*sums_ready.inc((s, b, g)))
                    dve.wait_ge(*sums_ready.at((s, b, g)))
                elif step == "turn_back":
                    e = sp["dh"] + 1
                    bank = ring_dve.take(dve, ("AV", s, b, g))[:, 0:4 * e].rearrange("p (c e) -> p c e", e=e)
                    link(dve, nc.vector.reciprocal(rden, bank[:, :, e - 1:e].rearrange("p c e -> p (c e)")))
                    o = O[:, b % 2, 0:256].rearrange("p (h e) -> p h e", e=32)[:, heads_of(s, g), :]
                    link(dve, nc.vector.tensor_tensor(o, bank[:, :, 0:e - 1], spread(rden, e - 1, 2), ALU.mult))
                    if g == 0:
                        dve.wait_ge(ring_dve.emptied, ring_dve.nth(("vg", s, b)))
                    gate = gate2[:, b % 4, :].rearrange("p (h e) -> p h e", e=32)[:, heads_of(s, g), :]
                    nc.vector.tensor_tensor(o, o, gate, ALU.mult).then_inc(ring_dve.emptied, 1)
                    dve.wait_ge(ring_dve.emptied, ring_dve.taken)
                elif step == "out":
                    if kind == "narrow":
                        dve.wait_ge(*out_filled.at((s, b)))
                        bank = seq_bank(b)
                    else:
                        bank = ring_dve.take(dve, ("out", s, b))
                    scalar = tgate[:, :] if s == "l0x" else float(sp["alpha"])
                    ins = nc.vector.scalar_tensor_tensor(out=x[:, b, :], in0=bank[:, 0:D], scalar=scalar,
                                                         in1=x[:, b, :], op0=ALU.mult, op1=ALU.add)
                    if kind == "narrow":
                        ins.then_inc(*out_added.inc((s, b)))
                        dve.wait_ge(*out_added.at((s, b)))
                    else:
                        ins.then_inc(ring_dve.emptied, 1)
                        dve.wait_ge(ring_dve.emptied, ring_dve.nth(("out", s, b)))
                    if next_of(s):
                        ln_stats(dve, next_of(s), b)
                elif step == "xhat" and next_of(s):
                    ln_xhat(dve, next_of(s), b)
                elif step == "router":
                    router_dve(dve, 0, g)

        def gpsimd_attention(pool, run):
            for s, step, b, g in attention_steps(run):
                sp = SPEC[s]
                kind = sp["kind"]
                if step == "queries":
                    queries(pool, b)
                elif step == "scale":
                    n = units.index((s, b, g)) % 4
                    pool.wait_ge(*sums_ready.at((s, b, g)))
                    nc.gpsimd.tensor_tensor(prob[:, n, :, :], prob[:, n, :, :], spread(nmax[:, n, :], S, 2), ALU.mult
                                            ).then_inc(*scaled.inc((s, b, g)))
                    pool.wait_ge(*scaled.at((s, b, g)))
                elif step == "project" and kind == "narrow":
                    pool.wait_ge(ring_act.emptied, ring_act.nth(("qkv", s, b)))
                    k = kraw[:, b % 3, 0, :]
                    if sp.get("masked"):
                        if b == 0:
                            pool.wait_ge(mask_ready, 1)
                        plink(pool, nc.gpsimd.tensor_tensor(k, k, mask01[:, b, :], ALU.mult))
                    for j in range(2):
                        nc.gpsimd.tensor_tensor(keys16(b, j), spread(k, 8), spread(w["mask8"][:, 8 * j:8 * j + 8], S, 2),
                                                ALU.mult).then_inc(*k_masked.inc((s, b, j)))
                        pool.wait_ge(*k_masked.at((s, b, j)))
                elif step == "project" and kind == "rope":
                    pool.wait_ge(ring_dve.emptied, ring_dve.nth(("k", s, b)))
                    plink(pool, nc.gpsimd.tensor_tensor(q3(b)[:, 0:2, :], rope1[:, b % 2, 0:2, :], rope2[:, b % 2, 0:2, :], ALU.add))
                    plink(pool, nc.gpsimd.tensor_tensor(kraw[:, b % 3, :, :], rope1[:, b % 2, 2:4, :],
                                                        rope2[:, b % 2, 2:4, :], ALU.add))
                    plink(pool, nc.gpsimd.tensor_tensor(kmask_of(b)[:, 0, :, :], spread(kraw[:, b % 3, 0, :], 4),
                                            spread(w["mask32"], S, 2), ALU.mult))
                    nc.gpsimd.tensor_tensor(kmask_of(b)[:, 1, :, :], spread(kraw[:, b % 3, 1, :], 4),
                                            spread(w["mask32"], S, 2), ALU.mult).then_inc(*k_masked.inc((s, b, 0)))
                    pool.wait_ge(*k_masked.at((s, b, 0)))
                elif step == "out" and next_of(s):
                    ln_rstd(pool, next_of(s), b)

        xr = big[0][:, 0, :, 0:S]
        xk = big[0][:, 1, :, 0:S]
        xd = big[1][:, 0, :, 0:S]
        kact = big[1][:, 1, :, 0:S]
        rgate = O[:, 0, :].rearrange("p (b d) -> p b d", d=D)

        def tensor_l0f(pe):
            pe.wait_ge(loaded["l0f"], 16)
            for n in range(2):
                pe.wait_ge(*l0f_mix.at((n,)))
                bank = ring_dve.open(pe, ("k", "l0f", n))
                nc.tensor.matmul(bank, w["f0_wk"], xk[:, 4 * n:4 * n + 4, :], start=True, stop=True).then_inc(
                    ring_dve.filled, 1)
                bank = ring_act.open(pe, ("r", n))
                for i in range(4):
                    last = nc.tensor.matmul(bank[:, i * D:(i + 1) * D], xr[:, 4 * n + i, :], w["f0_wr"], start=True,
                                            stop=True)
                last.then_inc(ring_act.filled, 1)
            for n in range(2):
                bank = ring_dve.open(pe, ("out", "l0f", n))
                pe.wait_ge(ring_dve.emptied, ring_dve.nth(("k", "l0f", n)))
                for i in range(4):
                    last = nc.tensor.matmul(bank[:, i * D:(i + 1) * D], kact[:, 4 * n + i, :], w["f0_wv"], start=True,
                                            stop=True)
                last.then_inc(ring_dve.filled, 1)
            finish_pe(pe, "l0f")

        def scalar_l0f(act):
            for n in range(2):
                bank = ring_act.take(act, ("r", n))
                nc.scalar.activation(rgate[:, 4 * n:4 * n + 4, :], bank.rearrange("p (b t) -> p b t", t=S), ACT.Tanh,
                                     scale=0.5).then_inc(ring_act.emptied, 1)
            finish_act(act, "l0f")

        def vector_l0f(dve):
            dve.wait_ge(loaded["l0f"], 16)
            for n in range(2):
                dve.wait_ge(ring_act.emptied, xT_use("l0f", 4 * n + 3))
                now, prev = xpad[:, 4 * n:4 * n + 4, 1:S + 1], xpad[:, 4 * n:4 * n + 4, 0:S]
                d = xd[:, 4 * n:4 * n + 4, :]
                link(dve, nc.vector.tensor_tensor(d, now, prev, ALU.subtract))
                link(dve, nc.vector.scalar_tensor_tensor(out=xk[:, 4 * n:4 * n + 4, :], in0=d, scalar=w["f0_muk"], in1=prev,
                                               op0=ALU.mult, op1=ALU.add))
                nc.vector.scalar_tensor_tensor(out=xr[:, 4 * n:4 * n + 4, :], in0=d, scalar=w["f0_mur"], in1=prev,
                                               op0=ALU.mult, op1=ALU.add).then_inc(*l0f_mix.inc((n,)))
                dve.wait_ge(*l0f_mix.at((n,)))
            for n in range(2):
                bank = ring_dve.take(dve, ("k", "l0f", n))
                kk = kact[:, 4 * n:4 * n + 4, :]
                link(dve, nc.vector.tensor_scalar(kk, bank.rearrange("p (b t) -> p b t", t=S), 0.0, None, ALU.max))
                nc.vector.tensor_tensor(kk, kk, kk, ALU.mult).then_inc(ring_dve.emptied, 1)
                dve.wait_ge(ring_dve.emptied, ring_dve.taken)
            for n in range(2):
                bank = ring_dve.take(dve, ("out", "l0f", n))
                dve.wait_ge(ring_act.emptied, ring_act.nth(("r", n)))
                r = rgate[:, 4 * n:4 * n + 4, :]
                xs = x[:, 4 * n:4 * n + 4, :]
                link(dve, nc.vector.scalar_tensor_tensor(out=r, in0=r, scalar=1.0,
                                                         in1=bank.rearrange("p (b t) -> p b t", t=S), op0=ALU.add,
                                                         op1=ALU.mult))
                nc.vector.scalar_tensor_tensor(out=xs, in0=r, scalar=0.5, in1=xs, op0=ALU.mult, op1=ALU.add
                                               ).then_inc(ring_dve.emptied, 1)
                dve.wait_ge(ring_dve.emptied, ring_dve.nth(("out", "l0f", n)))
                finish_dve(dve, "l0f", n)

        def gpsimd_l0f(pool):
            finish_pool(pool, "l0f")

        first_rows = big[1].rearrange("p a h s -> p (a h s)")[0:8, :]
        second_rows = O.rearrange("p a c -> p (a c)")[0:8, :]
        rF, rI, rA, rCS = ([t[:, 512 * k:512 * k + 512] for t in (first_rows, second_rows)] for k in range(4))
        rG = [kraw.rearrange("p m c s -> p (m c s)")[0:8, 0:512], kT[0:8, 0, 0:4, :].rearrange("p c s -> p (c s)")]
        rM_all = [rowconst[:, 1 + n, 512:1024] for n in range(2)]
        rM = [m[0:8, :] for m in rM_all]
        qm = [big[0][:, i, :, 0:S] for i in range(2)]
        DC = [big[1][:, i, :, 0:S] for i in range(2)]
        hbuf = OT[:, 0, 0:2, :]
        wkv = small[:, 8:24].rearrange("p (g h) -> p g h", g=2)
        gcol, floor = wcol[:, :, 0:8], wcol[:, :, 8:16]

        GATE_PARTS = ("gates", "logs", "scan", "scan2", "turn", "turned")

        def lstm_steps():
            for t in range(B + 4):
                if t < B:
                    yield "weights", t
                if t == 0:
                    yield "gates", 1
                    yield "logs", 1
                if t == 3:
                    yield "turn", 1
                if 0 <= t - 1 < B:
                    yield "value", t - 1
                if 0 <= t - 2 < B:
                    yield "normalise", t - 2
                if t == 3:
                    yield "turned", 1
                if 0 <= t - 3 < B:
                    yield "add", t - 3
                if 0 <= t - 4 < B:
                    yield "norm", t - 4
                if t < B:
                    yield "apply", t
                if t in (0, 1):
                    yield ("scan", "scan2")[t], 1

        def gates_pe(pe, step, n):
            if step == "gates":
                pe.wait_ge(loaded["l1x"], 16)
                pe.wait_ge(rowconst_loaded, 16)
                pe.wait_ge(lstm_wkv, 1)
                xT_wait(pe, "l1x", halves[n][-1])
                for ring, gate in ((ring_dve, "f"), (ring_act, "i")):
                    bank = ring.open(pe, (gate, "l1x", n))
                    nc.tensor.matmul(bank[0:8, :], w[f"x1_w{gate}"][:, 0:8], xT_of["l1x"][:, 4 * n:4 * n + 4, :],
                                     start=True, stop=False)
                    nc.tensor.matmul(bank[0:8, :], wkv[:, "fi".index(gate), :], ctxT[:, 4 * n:4 * n + 4, :],
                                     start=False, stop=True).then_inc(ring.filled, 1)
            elif step == "turn":
                bank = ring_dve.open(pe, ("turn", n))
                pe.wait_ge(*lstm_G.at((n,)))
                pe.wait_ge(*lstm_expA.at((n,)))
                for i in range(4):
                    for j, row in enumerate((rG[n], rA[n])):
                        last = nc.tensor.transpose(bank[:, 16 * i + 8 * j:16 * i + 8 * j + 8],
                                                   row[:, i * S:(i + 1) * S], w["ident"][0:8, 0:8])
                last.then_inc(ring_dve.filled, 1)

        def gates_act(act, step, n):
            if step == "gates":
                act.wait_ge(loaded["l1x"], 16)
                bank = ring_act.take(act, ("i", "l1x", n))
                nc.scalar.activation(rI[n], bank[0:8, :], ACT.Identity, bias=w["x1_bi"]).then_inc(ring_act.emptied, 1)
            elif step == "logs":
                act.wait_ge(*lstm_abs.at((n,)))
                alink(act, nc.scalar.activation(rA[n], rA[n], ACT.Exp, scale=-1.0))
                nc.scalar.activation(rA[n], rA[n], ACT.Ln, bias=1.0).then_inc(*lstm_log.inc((n,)))
            elif step == "scan2":
                act.wait_ge(*lstm_A.at((n,)))
                nc.scalar.activation(rA[n], rA[n], ACT.Exp, scale=-1.0).then_inc(*lstm_expA.inc((n,)))

        def gates_dve(dve, step, n):
            f, a, cs, m = rF[n], rA[n], rCS[n], rM[n]
            if step == "gates":
                if n == 0:
                    dve.wait_ge(loaded["l1x"], 16)
                    dve.wait_ge(rowconst_loaded, 16)
                    for i, gate in enumerate("fi"):
                        ins = nc.vector.tensor_tensor(wkv[:, i, :], w[f"x1_w{gate}"][:, 8:16],
                                                      w[f"x1_w{gate}"][:, 16:24], ALU.add)
                    ins.then_inc(lstm_wkv, 1)
                    dve.wait_ge(lstm_wkv, 1)
                bank = ring_dve.take(dve, ("f", "l1x", n))
                nc.vector.tensor_scalar(f, bank[0:8, :], w["x1_bf"], None, ALU.add).then_inc(ring_dve.emptied, 1)
                dve.wait_ge(ring_dve.emptied, ring_dve.taken)
                nc.vector.scalar_tensor_tensor(out=a, in0=f, scalar=-1.0, in1=f, op0=ALU.mult, op1=ALU.max
                                               ).then_inc(*lstm_abs.inc((n,)))
                dve.wait_ge(*lstm_abs.at((n,)))
                link(dve, nc.vector.tensor_scalar(f, f, 0.0, None, ALU.min))
            elif step == "scan":
                dve.wait_ge(*lstm_log.at((n,)))
                link(dve, nc.vector.tensor_tensor(f, f, a, ALU.subtract))
                link(dve, nc.vector.tensor_tensor_scan(cs, notfirst[:, 0:512], f, 0.0, ALU.mult, ALU.add))
                dve.wait_ge(ring_act.emptied, ring_act.nth(("i", "l1x", n)))
                nc.vector.tensor_tensor(rG[n], rI[n], cs, ALU.subtract).then_inc(*lstm_G.inc((n,)))
                dve.wait_ge(*lstm_G.at((n,)))
            elif step == "scan2":
                link(dve, nc.vector.tensor_tensor_scan(m, negfirst[:, 0:512], rG[n], NEG, ALU.add, ALU.max))
                nc.vector.tensor_tensor(a, cs, m, ALU.add).then_inc(*lstm_A.inc((n,)))
                dve.wait_ge(*lstm_A.at((n,)))
                nc.vector.tensor_scalar(m, m, -1.0, None, ALU.mult).then_inc(*lstm_M.inc((n,)))
                dve.wait_ge(*lstm_M.at((n,)))
            elif step == "turned":
                bank = ring_dve.take(dve, ("turn", n))[:, 0:64].rearrange("p (b e) -> p b e", e=16)
                link(dve, nc.vector.tensor_scalar(floor[:, 4 * n:4 * n + 4, :], bank[:, :, 8:16], 1e-6, None,
                                                  ALU.add))
                nc.vector.tensor_copy(gcol[:, 4 * n:4 * n + 4, :], bank[:, :, 0:8]).then_inc(ring_dve.emptied, 1)
                dve.wait_ge(ring_dve.emptied, ring_dve.taken)

        def tensor_l1x(pe):
            for step, b in lstm_steps():
                if step in GATE_PARTS:
                    gates_pe(pe, step, b)
                elif step == "weights":
                    if b % HALF == 0:
                        pe.wait_ge(*lstm_M.at((b // HALF,)))
                    for i in range(2):
                        bank = ring_act.open(pe, ("arg", b, i))
                        nc.tensor.matmul(bank, w["ident_bf"], spread(w["causalT_bf"], 4), start=True, stop=False)
                        for c in range(4):
                            h = 4 * i + c
                            last = nc.tensor.matmul(bank[:, c * S:(c + 1) * S], headrows[:, h * S:(h + 1) * S],
                                                    rM_all[b // HALF][:, b % HALF * S:(b % HALF + 1) * S],
                                                    start=False, stop=(c == 3))
                        last.then_inc(ring_act.filled, 1)
                    pe.wait_ge(*lstm_q.at((b,)))
                    for i in range(2):
                        bank = ring_score.open(pe, ("qk", b, i))
                        nc.tensor.matmul(bank, ctxT[:, b, :], qm[b % 2][:, 4 * i:4 * i + 4, :], start=True, stop=True
                                         ).then_inc(ring_score.filled, 1)
                elif step == "value":
                    bank = ring_dve.open(pe, ("h", b))
                    pe.wait_ge(ring_score.emptied, ring_score.nth(("qk", b, 1)))
                    if b == 0:
                        pe.wait_ge(v_ready, 2)
                    for h in range(8):
                        last = nc.tensor.matmul(bank[:, 17 * h:17 * h + 17], DC[b % 2][:, h, :], V17[:, b, h, :],
                                                start=True, stop=True)
                    last.then_inc(ring_dve.filled, 1)
                elif step == "norm" and next_of("l1x"):
                    ln_transpose(pe, next_of("l1x"), (b,))

        def scalar_l1x(act):
            act.wait_ge(v_ready, 1)
            for i in range(2):
                these = slice(4 * i, 4 * i + 4)
                ins = nc.scalar.activation(V17[:, these, :, 0:16].rearrange("p b h e -> p (b h) e"),
                                           ctx[:, these, :].rearrange("p b (h e) -> p (b h) e", e=16), ACT.Copy)
            ins.then_inc(v_ready, 1)
            for step, b in lstm_steps():
                if step in GATE_PARTS:
                    gates_act(act, step, b)
                elif step == "weights":
                    if b % HALF == 0:
                        act.wait_ge(ring_dve.emptied, ring_dve.nth(("turn", b // HALF)))
                    for i in range(2):
                        bank = ring_act.take(act, ("arg", b, i))
                        if b >= 2 and i == 0:
                            act.wait_ge(ring_dve.filled, ring_dve.nth(("h", b - 2)))
                        for c in range(4):
                            h = 4 * i + c
                            last = nc.scalar.activation(DC[b % 2][:, h, :], bank[:, c * S:(c + 1) * S], ACT.Exp,
                                                        bias=gcol[:, b, h:h + 1])
                        last.then_inc(ring_act.emptied, 1)
                elif step == "norm" and next_of("l1x"):
                    ln_copy(act, next_of("l1x"), (b,))

        def vector_l1x(dve):
            for step, b in lstm_steps():
                if step in GATE_PARTS:
                    gates_dve(dve, step, b)
                elif step == "apply":
                    for i in range(2):
                        bank = ring_score.take(dve, ("qk", b, i))
                        dve.wait_ge(ring_act.emptied, ring_act.nth(("arg", b, i)))
                        d = DC[b % 2][:, 4 * i:4 * i + 4, :]
                        nc.vector.tensor_tensor(d, bank.rearrange("p (c t) -> p c t", t=S), d, ALU.mult).then_inc(
                            ring_score.emptied, 1)
                        dve.wait_ge(ring_score.emptied, ring_score.taken)
                elif step == "normalise":
                    bank = ring_dve.take(dve, ("h", b))
                    hv = bank[:, 0:136].rearrange("p (h e) -> p h e", e=17)
                    den = small[:, 0:8]
                    link(dve, nc.vector.tensor_copy(den, hv[:, :, 16:17].rearrange("p h e -> p (h e)")))
                    link(dve, nc.vector.scalar_tensor_tensor(out=den, in0=den, scalar=-1.0, in1=den, op0=ALU.mult,
                                                             op1=ALU.max))
                    link(dve, nc.vector.scalar_tensor_tensor(out=den, in0=den, scalar=1e-6, in1=floor[:, b, :],
                                                             op0=ALU.add, op1=ALU.max))
                    link(dve, nc.vector.reciprocal(den, den))
                    nc.vector.tensor_tensor(hbuf[:, b % 2, :].rearrange("p (h e) -> p h e", e=16), hv[:, :, 0:16],
                                            spread(den, 16, 2), ALU.mult).then_inc(ring_dve.emptied, 1)
                    dve.wait_ge(ring_dve.emptied, ring_dve.nth(("h", b)))
                    link(dve, nc.vector.bn_stats(stats[:, b, :], hbuf[:, b % 2, :]))
                    nc.vector.bn_aggr(mv[:, b, :], stats[:, b, :]).then_inc(*lstm_var.inc((b,)))
                    dve.wait_ge(*lstm_var.at((b,)))
                elif step == "add":
                    dve.wait_ge(*lstm_rstd.at((b,)))
                    h = hbuf[:, b % 2, :]
                    link(dve, nc.vector.scalar_tensor_tensor(out=h, in0=h, scalar=mv[:, b, 0:1], in1=w["x1_lnscale"],
                                                             op0=ALU.subtract, op1=ALU.mult))
                    link(dve, nc.vector.scalar_tensor_tensor(out=x[:, b, :], in0=h, scalar=rstd[:, b, :],
                                                             in1=x[:, b, :], op0=ALU.mult, op1=ALU.add))
                    if next_of("l1x"):
                        ln_stats(dve, next_of("l1x"), b)
                elif step == "norm" and next_of("l1x"):
                    ln_xhat(dve, next_of("l1x"), b)

        def gpsimd_l1x(pool):
            pool.wait_ge(ctx_loaded, 32)
            pool.wait_ge(ring_dve.emptied, ring_dve.nth(("out", "l1a", B - 1)))
            nc.gpsimd.memset(V17, 1.0).then_inc(v_ready, 1)
            pool.wait_ge(v_ready, 1)
            for step, b in lstm_steps():
                if step == "gates":
                    continue
                elif step == "normalise":
                    pool.wait_ge(*lstm_var.at((b,)))
                    plink(pool, nc.gpsimd.tensor_scalar(veps[:, b, :], mv[:, b, 1:2], 1e-5, None, ALU.add))
                    nc.gpsimd.tensor_tensor(rstd[:, b, :], veps[:, b, :], power[:, 0:1], ALU.pow).then_inc(
                        *lstm_rstd.inc((b,)))
                    pool.wait_ge(*lstm_rstd.at((b,)))
                elif step == "add" and next_of("l1x"):
                    ln_rstd(pool, next_of("l1x"), b)
                elif step == "apply" and 1 <= b < B - 1:
                    queries(pool, b + 1)

        def queries(pool, b):
            pool.wait_ge(ring_act.emptied, xT_use("l1x", b))
            if b >= 2:
                pool.wait_ge(ring_score.filled, ring_score.nth(("qk", b - 2, 1)))
            nc.gpsimd.tensor_tensor(qm[b % 2], spread(xT_of["l1x"][:, b, :], 8), spread(w["mask16"], S, 2),
                                    ALU.mult).then_inc(*lstm_q.inc((b,)))
            pool.wait_ge(*lstm_q.at((b,)))

        VT = qT[:, 0, :, :]
        fh = big[0][:, :, :, 0:S]
        wT8 = O[0:8, 0, :]
        RC = sb("RC", [P, 2, B, 8])
        RQ = sb("RQ", [P, 2, B, 8])
        pvs = sb("pvs", [P, 4, 64])
        rm = sb("rm", [P, 2, B])
        mx = sb("mx", [P, B, 8])
        mi = sb("mi", [P, B, 8], U32)
        mif = sb("mif", [P, B, 2])
        sca = sb("sca", [P, B, 4])
        sigma = sb("sigma", [P, 2])

        def tensor_l1f(pe):
            pe.wait_ge(loaded["l1f"], 16)
            for n in range(2):
                for b in halves[n]:
                    xT_wait(pe, "l1f", b)
                bank = ring_act.open(pe, ("VT", n))
                nc.tensor.matmul(bank, w["f1_wv"], xT_of["l1f"][:, 4 * n:4 * n + 4, :], start=True, stop=True
                                 ).then_inc(ring_act.filled, 1)
            for n in range(2):
                bank = ring_dve.open(pe, ("router", "l1f", n))
                pe.wait_ge(ring_act.emptied, ring_act.nth(("VT", n)))
                for i in range(4):
                    last = nc.tensor.matmul(bank[:, 72 * i:72 * i + 72], VT[:, 4 * n + i, :], w["f1_wgp"], start=True,
                                            stop=True)
                last.then_inc(ring_dve.filled, 1)
            for n in range(2):
                for c in range(2):
                    bank = ring_act.open(pe, ("h1", c, n))
                    nc.tensor.matmul(bank, w["f1_w1"][:, c * P:(c + 1) * P], VT[:, 4 * n:4 * n + 4, :], start=True,
                                     stop=True).then_inc(ring_act.filled, 1)
            pe.wait_ge(*l1f_w.at((0,)))
            for n in range(2):
                bank = ring_act.open(pe, ("wT", "l1f", n))
                for i in range(4):
                    last = nc.tensor.transpose(bank[0:8, i * S:(i + 1) * S], wcol[:, 4 * n + i, 0:8], w["ident"])
                last.then_inc(ring_act.filled, 1)
            for n in range(2):
                pe.wait_ge(ring_act.emptied, ring_act.nth(("wT", "l1f", n)))
                for c in range(2):
                    bank = ring_score.open(pe, ("wexp", c, n))
                    nc.tensor.matmul(bank, w["sel8"][:, c * P:(c + 1) * P], wT8[:, 512 * n:512 * n + 512], start=True,
                                     stop=True).then_inc(ring_score.filled, 1)
            for n in range(2):
                bank = ring_dve.open(pe, ("out", "l1f", n))
                nc.tensor.matmul(bank, w["ones"][0:1, :], spread(w["f1_bvr"], 4), start=True, stop=False)
                pe.wait_ge(ring_score.emptied, ring_score.nth(("wexp", 1, n)))
                for i in range(4):
                    b = 4 * n + i
                    o = bank[:, i * D:(i + 1) * D]
                    nc.tensor.matmul(o, xT_of["l1f"][:, b, :], w["f1_wv"], start=False, stop=False)
                    nc.tensor.matmul(o, wT8[:, b * S:(b + 1) * S], w["f1_b2"], start=False, stop=False)
                    for c in range(2):
                        last = nc.tensor.matmul(o, fh[:, c, b, :], w["f1_w2"][:, c * D:(c + 1) * D], start=False,
                                                stop=(i == 3 and c == 1))
                last.then_inc(ring_dve.filled, 1)
            finish_pe(pe, "l1f")

        l1f_w = events(sem("l1f_weights"), [(0,)])
        l1f_d = sem("l1f_dve")
        l1f_root = sem("l1f_roots")
        l1f_a = sem("l1f_act")

        def scalar_l1f(act):
            act.wait_ge(loaded["l1f"], 16)
            for n in range(2):
                bank = ring_act.take(act, ("VT", n))
                nc.scalar.activation(VT[:, 4 * n:4 * n + 4, :], bank.rearrange("p (b t) -> p b t", t=S), ACT.Identity,
                                     bias=w["f1_bvc"]).then_inc(ring_act.emptied, 1)
            nc.scalar.activation(sigma[:, 0:1], w["f1_alpha"], ACT.Exp, scale=-1.0).then_inc(l1f_a, 1)
            for n in range(2):
                for c in range(2):
                    bank = ring_act.take(act, ("h1", c, n))
                    nc.scalar.activation(fh[:, c, 4 * n:4 * n + 4, :], bank.rearrange("p (b t) -> p b t", t=S), ACT.Silu,
                                         bias=w["f1_b1"][:, c:c + 1]).then_inc(ring_act.emptied, 1)
            act.wait_ge(l1f_d, 1)
            nc.scalar.activation(RC[:, 1, :, :], RQ[:, 1, :, :], ACT.Sqrt).then_inc(l1f_root, 1)
            act.wait_ge(l1f_v, 1)
            nc.scalar.activation(rm[:, :, :], rm[:, :, :], ACT.Sqrt).then_inc(l1f_root, 1)
            act.wait_ge(l1f_d, 2)
            nc.scalar.activation(sca[:, :, 1], sca[:, :, 0], ACT.Exp).then_inc(l1f_a, 1)
            for n in range(2):
                bank = ring_act.take(act, ("wT", "l1f", n))
                nc.scalar.activation(wT8[:, 512 * n:512 * n + 512], bank[0:8, :], ACT.Copy).then_inc(
                    ring_act.emptied, 1)
            finish_act(act, "l1f")

        def vector_l1f(dve):
            dve.wait_ge(loaded["l1f"], 16)
            dve.wait_ge(l1f_a, 1)
            link(dve, nc.vector.tensor_scalar(sigma[:, 0:1], sigma[:, 0:1], 1.0, None, ALU.add))
            link(dve, nc.vector.reciprocal(sigma[:, 1:2], sigma[:, 0:1]))
            for n in range(2):
                bank = ring_dve.take(dve, ("router", "l1f", n))[:, 0:288].rearrange("p (b e) -> p b e", e=72)
                link(dve, nc.vector.tensor_tensor(RC[:, 0, 4 * n:4 * n + 4, :], bank[:, :, 0:8], spread(w["f1_bg"], 4), ALU.add))
                nc.vector.tensor_copy(pvs, bank[:, :, 8:72]).then_inc(ring_dve.emptied, 1)
                dve.wait_ge(ring_dve.emptied, ring_dve.nth(("router", "l1f", n)))
                link(dve, nc.vector.tensor_tensor(pvs, pvs, pvs, ALU.mult))
                link(dve, nc.vector.tensor_reduce(RQ[:, 1, 4 * n:4 * n + 4, :],
                                                  pvs.rearrange("p b (e k) -> p b e k", k=8), AX.X, ALU.add))
            nc.vector.tensor_scalar(RQ[:, 1, :, :], RQ[:, 1, :, :], 0.125, None, ALU.mult).then_inc(l1f_d, 1)
            dve.wait_ge(l1f_d, 1)
            dve.wait_ge(l1f_root, 1)
            rc = RC[:, :, :, :].rearrange("p a b e -> p (a b) e")
            rq = RQ[:, :, :, :].rearrange("p a b e -> p (a b) e")
            rms = rm[:, :, :].rearrange("p a b -> p (a b)")
            link(dve, nc.vector.tensor_reduce(rms, rc, AX.X, ALU.add))
            link(dve, nc.vector.tensor_scalar(rms, rms, 0.125, None, ALU.mult))
            link(dve, nc.vector.tensor_tensor(rc, rc, spread(rms, 8, 2), ALU.subtract))
            link(dve, nc.vector.tensor_tensor(rq, rc, rc, ALU.mult))
            link(dve, nc.vector.tensor_reduce(rms, rq, AX.X, ALU.add))
            nc.vector.tensor_scalar(rms, rms, 0.125, 1e-5, ALU.mult, ALU.add).then_inc(l1f_v, 1)
            dve.wait_ge(l1f_v, 1)
            dve.wait_ge(l1f_root, 2)
            link(dve, nc.vector.reciprocal(rms, rms))
            link(dve, nc.vector.tensor_tensor(rc, rc, spread(rms, 8, 2), ALU.mult))
            for i, (gn, bn) in enumerate((("f1_gr", "f1_br"), ("f1_gc", "f1_bc"))):
                link(dve, nc.vector.tensor_tensor(RC[:, i, :, :], RC[:, i, :, :], spread(w[gn], B), ALU.mult))
                link(dve, nc.vector.tensor_tensor(RC[:, i, :, :], RC[:, i, :, :], spread(w[bn], B), ALU.add))
            link(dve, nc.vector.scalar_tensor_tensor(out=RC[:, 0, :, :], in0=RC[:, 1, :, :], scalar=sigma[:, 1:2],
                                                     in1=RC[:, 0, :, :], op0=ALU.mult, op1=ALU.add))
            for b in range(B):
                ins = nc.vector.max(mx[:, b, :], RC[:, 0, b, :])
            link(dve, ins)
            for b in range(B):
                ins = nc.vector.max_index(mi[:, b, :], mx[:, b, :], RC[:, 0, b, :])
            link(dve, ins)
            link(dve, nc.vector.tensor_copy(mif, mi[:, :, 0:2]))
            nc.vector.tensor_tensor(sca[:, :, 0], mx[:, :, 1], mx[:, :, 0], ALU.subtract).then_inc(l1f_d, 1)
            dve.wait_ge(l1f_d, 2)
            dve.wait_ge(l1f_a, 2)
            link(dve, nc.vector.tensor_scalar(sca[:, :, 2], sca[:, :, 1], 1.0, None, ALU.add))
            link(dve, nc.vector.reciprocal(sca[:, :, 2], sca[:, :, 2]))
            link(dve, nc.vector.tensor_tensor(sca[:, :, 3], sca[:, :, 1], sca[:, :, 2], ALU.mult))
            for i in range(2):
                link(dve, nc.vector.tensor_tensor(RQ[:, i, :, :], spread(w["iota8"], B), spread(mif[:, :, i], 8, 2),
                                                  ALU.is_equal))
                link(dve, nc.vector.tensor_tensor(RQ[:, i, :, :], RQ[:, i, :, :], spread(sca[:, :, 2 + i], 8, 2),
                                                  ALU.mult))
            nc.vector.tensor_tensor(wcol[:, :, 0:8], RQ[:, 0, :, :], RQ[:, 1, :, :], ALU.add).then_inc(
                *l1f_w.inc((0,)))
            dve.wait_ge(*l1f_w.at((0,)))
            for n in range(2):
                for c in range(2):
                    bank = ring_score.take(dve, ("wexp", c, n))
                    dve.wait_ge(ring_act.emptied, ring_act.nth(("h1", c, n)))
                    h = fh[:, c, 4 * n:4 * n + 4, :]
                    nc.vector.tensor_tensor(h, h, bank.rearrange("p (b t) -> p b t", t=S), ALU.mult).then_inc(
                        ring_score.emptied, 1)
                    dve.wait_ge(ring_score.emptied, ring_score.taken)
            for n in range(2):
                bank = ring_dve.take(dve, ("out", "l1f", n))
                xs = x[:, 4 * n:4 * n + 4, :]
                nc.vector.tensor_tensor(xs, bank.rearrange("p (b d) -> p b d", d=D), xs, ALU.add).then_inc(
                    ring_dve.emptied, 1)
                dve.wait_ge(ring_dve.emptied, ring_dve.nth(("out", "l1f", n)))
                finish_dve(dve, "l1f", n)

        l1f_v = sem("l1f_variance")

        def gpsimd_l1f(pool):
            finish_pool(pool, "l1f")

        aff = ctx[:, 0:2, :].rearrange("p a (b e) -> p (a b) e", e=32)
        rep = ctx[:, 2:4, :].rearrange("p a (b e) -> p (a b) e", e=32)
        whalf = sb("whalf", [P, B, 32], BF16)
        w96 = gate2[:, 0:3, :].rearrange("p m (a e) -> p (m a) e", e=32).rearrange("p (b t) e -> p b (t e)", t=3)
        w96T = OT[0:96, 0, :, :]
        w3T = OT[0:96, 1, :, :].rearrange("p c s -> p (c s)").bitcast(BF16)[:, 0:TOK].rearrange("p (b t) -> p b t", t=S)
        NC2 = 17
        f2_seq = [(n, c) for n in range(2) for c in range(NC2)]
        f2_weights = events(sem("f2_weights"), [(0,), (1,)])
        hid = [kmask[:, i, :, :, :].rearrange("p a c s -> p (a c s)") for i in range(3)]

        ROUTER_PIECES = 5

        def router_pe(pe, n):
            pe.wait_ge(loaded["l2f"], 16)
            bank = ring_act.open(pe, ("router", "l2f", n))
            for i, b in enumerate(halves[n]):
                xT_wait(pe, "l2f", b)
                nc.tensor.matmul(bank[:, 32 * i:32 * i + 32], xT_of["l2f"][:, b, :], w["f2_wr"], start=True, stop=False)
                last = nc.tensor.matmul(bank[:, 32 * i:32 * i + 32], w["ones"][0:1, :], w["f2_br"], start=False,
                                        stop=True)
            last.then_inc(ring_act.filled, 1)

        def router_act(act, n):
            bank = ring_act.take(act, ("router", "l2f", n))
            nc.scalar.activation(aff[:, 4 * n:4 * n + 4, :], bank[:, 0:128].rearrange("p (b e) -> p b e", e=32),
                                 ACT.Exp, scale=-1.0).then_inc(ring_act.emptied, 1)

        def router_dve(dve, n, part):
            these = slice(4 * n, 4 * n + 4)
            a, r, top = aff[:, these, :], rep[:, these, :], rm[:, 0, these]
            if part == 0:
                dve.wait_ge(ring_act.emptied, ring_act.nth(("router", "l2f", n)))
                link(dve, nc.vector.tensor_scalar(a, a, 1.0, None, ALU.add))
                link(dve, nc.vector.reciprocal(a, a))
                for b in halves[n]:
                    ins = nc.vector.max(mx[:, b, :], aff[:, b, :])
                link(dve, ins)
            elif part == 1:
                for b in halves[n]:
                    ins = nc.vector.match_replace(rep[:, b, :], mx[:, b, :], aff[:, b, :], -1.0)
                link(dve, ins)
                link(dve, nc.vector.tensor_reduce(top, mx[:, these, :], AX.X, ALU.add))
            elif part == 2:
                link(dve, nc.vector.tensor_scalar(top, top, 1e-9, None, ALU.add))
                link(dve, nc.vector.reciprocal(top, top))
                link(dve, nc.vector.scalar_tensor_tensor(out=r, in0=r, scalar=0.0, in1=a, op0=ALU.is_lt,
                                                         op1=ALU.mult))
                link(dve, nc.vector.tensor_tensor(r, r, spread(top, 32, 2), ALU.mult))
            elif part == 3:
                link(dve, nc.vector.tensor_copy(whalf[:, these, :], r))
                link(dve, nc.vector.tensor_copy(w96[:, these, 0:32], whalf[:, these, :]))
                link(dve, nc.vector.tensor_tensor(r, r, whalf[:, these, :], ALU.subtract))
            else:
                link(dve, nc.vector.tensor_copy(whalf[:, these, :], r))
                link(dve, nc.vector.tensor_copy(w96[:, these, 32:64], whalf[:, these, :]))
                nc.vector.tensor_tensor(w96[:, these, 64:96], r, whalf[:, these, :], ALU.subtract).then_inc(
                    *f2_weights.inc((n,)))
                dve.wait_ge(*f2_weights.at((n,)))

        def turn_weights(pe, n):
            pe.wait_ge(*f2_weights.at((n,)))
            bank = ring_act.open(pe, ("wT", "l2f", n))
            for i in range(4):
                last = nc.tensor.transpose(bank[0:96, i * S:(i + 1) * S], w96[:, 4 * n + i, :], w["ident"])
            last.then_inc(ring_act.filled, 1)

        def turned_weights(act, n):
            bank = ring_act.take(act, ("wT", "l2f", n))
            src = bank[0:96, :].rearrange("p (b t) -> p b t", t=S)
            nc.scalar.activation(w96T[:, 4 * n:4 * n + 4, :], src, ACT.Copy)
            nc.scalar.activation(w3T[:, 4 * n:4 * n + 4, :], src, ACT.Copy).then_inc(ring_act.emptied, 1)

        TURN = 12

        def tensor_l2f(pe):
            pe.wait_ge(loaded["l2f"], 16)
            xT = xT_of["l2f"]
            turn_weights(pe, 0)
            router_pe(pe, 1)
            acc = [None, None]

            def down(n, c):
                rows = 64 if c == 16 else P
                rhs = w["f2_wds"] if c == 16 else w["f2_wd"][:, c * D:(c + 1) * D]
                if c < 16:
                    pe.wait_ge(ring_prob.emptied, ring_prob.nth(("wexp", "l2f", n, c)))
                else:
                    pe.wait_ge(ring_score.emptied, ring_score.nth(("up", "l2f", n, c)))
                for i in range(4):
                    last = nc.tensor.matmul(acc[n][:, i * D:(i + 1) * D],
                                            hid[(n * NC2 + c) % 3][0:rows, i * S:(i + 1) * S], rhs, start=False,
                                            stop=(c == 16 and i == 3))
                if c == 16:
                    last.then_inc(ring_dve.filled, 1)

            for m, (n, c) in enumerate(f2_seq + [(2, 0), (2, 1)]):
                if n < 2:
                    if c == 0:
                        pe.wait_ge(ring_act.emptied, ring_act.nth(("wT", "l2f", n)))
                    rows = 64 if c == 16 else P
                    wg = w["f2_wgs"] if c == 16 else w["f2_wg"][:, c * P:(c + 1) * P]
                    wu = w["f2_wus"] if c == 16 else w["f2_wu"][:, c * P:(c + 1) * P]
                    bank = ring_act.open(pe, ("gate", "l2f", n, c))
                    nc.tensor.matmul(bank[0:rows, :], wg, xT[:, 4 * n:4 * n + 4, :], start=True, stop=True).then_inc(
                        ring_act.filled, 1)
                    bank = ring_score.open(pe, ("up", "l2f", n, c))
                    nc.tensor.matmul(bank[0:rows, :], wu, xT[:, 4 * n:4 * n + 4, :], start=True, stop=True).then_inc(
                        ring_score.filled, 1)
                    if c < 16:
                        bank = ring_prob.open(pe, ("wexp", "l2f", n, c))
                        nc.tensor.matmul(bank, w["sel32_bf"][:, c * P:(c + 1) * P], w3T[:, 4 * n:4 * n + 4, :],
                                         start=True, stop=True).then_inc(ring_prob.filled, 1)
                if m >= 2:
                    pn, pc = f2_seq[m - 2]
                    if pc == 0:
                        acc[pn] = ring_dve.open(pe, ("out", "l2f", pn))
                        nc.tensor.matmul(acc[pn], w["ones"][0:1, :], spread(w["f2_bds"], 4), start=True, stop=False)
                        for i in range(4):
                            nc.tensor.matmul(acc[pn][:, i * D:(i + 1) * D], w96T[:, 4 * pn + i, :], w["f2_bd3"],
                                             start=False, stop=False)
                    down(pn, pc)
                if (n, c) == (0, TURN):
                    turn_weights(pe, 1)
            finish_pe(pe, "l2f")

        def silu2_of(m):
            return prob[:, m % 4, :, :].rearrange("p c s -> p (c s)")

        def scalar_l2f(act):
            act.wait_ge(loaded["l2f"], 16)
            turned_weights(act, 0)
            router_act(act, 1)
            for m, (n, c) in enumerate(f2_seq):
                rows = 64 if c == 16 else P
                if m >= 4:
                    before = f2_seq[m - 4]
                    if before[1] < 16:
                        act.wait_ge(ring_prob.emptied, ring_prob.nth(("wexp", "l2f") + before))
                    else:
                        act.wait_ge(ring_score.emptied, ring_score.nth(("up", "l2f") + before))
                bank = ring_act.take(act, ("gate", "l2f", n, c))
                gb = w["f2_bgs"] if c == 16 else w["f2_bg"][:, c:c + 1]
                nc.scalar.activation(silu2_of(m)[0:rows, :], bank[0:rows, :], ACT.Silu, bias=gb).then_inc(
                    ring_act.emptied, 1)
                if (n, c) == (0, TURN):
                    turned_weights(act, 1)
            finish_act(act, "l2f")

        def vector_l2f(dve):
            dve.wait_ge(loaded["l2f"], 16)
            for m, (n, c) in enumerate(f2_seq):
                rows = 64 if c == 16 else P
                silu = silu2_of(m)[0:rows, :]
                h = hid[m % 3][0:rows, 0:512]
                ub = w["f2_bus"] if c == 16 else w["f2_bu"][:, c:c + 1]
                bank = ring_score.take(dve, ("up", "l2f", n, c))
                dve.wait_ge(ring_act.emptied, ring_act.nth(("gate", "l2f", n, c)))
                if c < 16:
                    nc.vector.scalar_tensor_tensor(out=silu, in0=bank[0:rows, :], scalar=ub, in1=silu, op0=ALU.add,
                                                   op1=ALU.mult).then_inc(ring_score.emptied, 1)
                    dve.wait_ge(ring_score.emptied, ring_score.taken)
                    wb = ring_prob.take(dve, ("wexp", "l2f", n, c))
                    nc.vector.tensor_tensor(h, silu, wb, ALU.mult).then_inc(ring_prob.emptied, 1)
                    dve.wait_ge(ring_prob.emptied, ring_prob.taken)
                else:
                    nc.vector.scalar_tensor_tensor(out=h, in0=bank[0:rows, :], scalar=ub, in1=silu, op0=ALU.add,
                                                   op1=ALU.mult).then_inc(ring_score.emptied, 1)
                    dve.wait_ge(ring_score.emptied, ring_score.taken)
                if n == 0 and 1 <= c <= ROUTER_PIECES:
                    router_dve(dve, 1, c - 1)
                if (n, c) == (1, 1):
                    finish_out(dve, 0)
            finish_out(dve, 1)

        def finish_out(dve, n):
            bank = ring_dve.take(dve, ("out", "l2f", n))
            xs = x[:, 4 * n:4 * n + 4, :]
            nc.vector.tensor_tensor(xs, bank.rearrange("p (b d) -> p b d", d=D), xs, ALU.add).then_inc(
                ring_dve.emptied, 1)
            dve.wait_ge(ring_dve.emptied, ring_dve.nth(("out", "l2f", n)))
            finish_dve(dve, "l2f", n)

        def gpsimd_l2f(pool):
            finish_pool(pool, "l2f")

        sc = O[0:8, 0, :]
        sw = [O[0:8, 1, :], qT[0:8, 0, :, :].rearrange("p c s -> p (c s)")]
        se = qT[0:8, 1, :, :].rearrange("p c s -> p (c s)")
        mx3 = sb("mx3", [8, 16, 8])
        s8 = sb("s8", [8, 4])
        f3_d = sem("f3_dve")
        f3_a = sem("f3_act")
        f3_seq = [(e, n, k) for e in range(8) for n in range(2) for k in range(2)]
        f3_hid = [kmask[:, i, :, :, :].rearrange("p a c s -> p (a c) s") for i in range(3)]
        f3_hid += [t[:, i, :, 0:S] for t in (kT, OT, big[0], big[1]) for i in range(2)]
        f3_hid += [V[:, i, 0:8 * S].rearrange("p (c s) -> p c s", s=S) for i in range(2)]
        f3_hid += [ctx, ctxT, xhat]

        def hidden(e, n):
            return f3_hid[2 * e + n]

        def silu_of(m):
            return prob[:, m % 4, :, :]

        def up_of(m):
            return probT[:, m // 2 % 2, :, :]

        f3_pool = events(sem("f3_hidden_pool"), [(e, n) for e in range(8) for n in range(2)])

        def tensor_l3f(pe):
            pe.wait_ge(loaded["l3f"], 16)
            xT = xT_of["l3f"]
            for n in range(2):
                for b in halves[n]:
                    xT_wait(pe, "l3f", b)
                bank = ring_dve.open(pe, ("sc", n))
                nc.tensor.matmul(bank[0:8, :], w["f3_wg"], xT[:, 4 * n:4 * n + 4, :], start=True, stop=True).then_inc(
                    ring_dve.filled, 1)

            for e, n, k in f3_seq:
                c = 2 * e + k
                bank = ring_score.open(pe, ("gate", e, n, k))
                nc.tensor.matmul(bank, w["f3_w1"][:, c * P:(c + 1) * P], xT[:, 4 * n:4 * n + 4, :], start=True,
                                 stop=True).then_inc(ring_score.filled, 1)
                ring = (ring_prob, ring_act)[k]
                bank = ring.open(pe, ("up", e, n, k))
                nc.tensor.matmul(bank, w["f3_w3"][:, c * P:(c + 1) * P], xT[:, 4 * n:4 * n + 4, :], start=True,
                                 stop=True).then_inc(ring.filled, 1)
            bank = ring_act.open(pe, ("wcol",))
            pe.wait_ge(f3_d, 2)
            for b in range(B):
                last = nc.tensor.transpose(bank[:, 8 * b:8 * b + 8], se[:, b * S:(b + 1) * S], w["ident"][0:8, 0:8])
            last.then_inc(ring_act.filled, 1)
            for n in range(2):
                for e in range(8):
                    bank = ring_dve.open(pe, ("y", e, n))
                    pe.wait_ge(ring_prob.emptied, ring_prob.nth(("up", e, n, 0)))
                    pe.wait_ge(*f3_pool.at((e, n)))
                    for i in range(4):
                        for k in range(2):
                            last = nc.tensor.matmul(bank[:, i * D:(i + 1) * D], hidden(e, n)[:, 4 * k + i, :],
                                                    w["f3_w2"][:, (2 * e + k) * D:(2 * e + k + 1) * D],
                                                    start=(k == 0), stop=(k == 1))
                    last.then_inc(ring_dve.filled, 1)

        def scalar_l3f(act):
            for m, (e, n, k) in enumerate(f3_seq):
                if m == 2:
                    act.wait_ge(f3_d, 1)
                    nc.scalar.activation(se, sc, ACT.Exp, bias=s8[:, 0:1]).then_inc(f3_a, 1)
                bank = ring_score.take(act, ("gate", e, n, k)).rearrange("p (c s) -> p c s", s=S)
                if m >= 4:
                    if k:
                        act.wait_ge(*f3_pool.at(f3_seq[m - 4][0:2]))
                    else:
                        act.wait_ge(ring_prob.emptied, ring_prob.nth(("up",) + f3_seq[m - 4]))
                nc.scalar.activation(silu_of(m), bank, ACT.Silu).then_inc(ring_score.emptied, 1)
                if k:
                    bank = ring_act.take(act, ("up", e, n, k))
                    nc.scalar.activation(up_of(m), bank.rearrange("p (c s) -> p c s", s=S), ACT.Copy).then_inc(
                        ring_act.emptied, 1)
            bank = ring_act.take(act, ("wcol",))
            nc.scalar.activation(wcol[:, :, 0:8], bank[:, 0:64].rearrange("p (b e) -> p b e", e=8), ACT.Copy
                                 ).then_inc(ring_act.emptied, 1)

        def vector_l3f(dve):
            def hid(m):
                e, n, k = f3_seq[m]
                bank = ring_prob.take(dve, ("up", e, n, k)).rearrange("p (c s) -> p c s", s=S)
                dve.wait_ge(ring_score.emptied, ring_score.nth(("gate", e, n, k)))
                nc.vector.tensor_tensor(hidden(e, n)[:, 4 * k:4 * k + 4, :], silu_of(m), bank, ALU.mult).then_inc(
                    ring_prob.emptied, 1)
                dve.wait_ge(ring_prob.emptied, ring_prob.taken)

            for n in range(2):
                bank = ring_dve.take(dve, ("sc", n))
                nc.vector.tensor_copy(sc[:, 512 * n:512 * n + 512], bank[0:8, :]).then_inc(ring_dve.emptied, 1)
                dve.wait_ge(ring_dve.emptied, ring_dve.taken)
            src = sc
            for r in range(16):
                link(dve, nc.vector.max(mx3[:, r, :], src))
                if r == 0:
                    nc.vector.tensor_scalar(s8[:, 0:1], mx3[:, 0, 0:1], -1.0, None, ALU.mult).then_inc(f3_d, 1)
                    dve.wait_ge(f3_d, 1)
                link(dve, nc.vector.match_replace(sw[r % 2], mx3[:, r, :], src, -3.0e38))
                src = sw[r % 2]
                if r >= 1:
                    hid(2 * r - 2)
            link(dve, nc.vector.tensor_tensor(src, src, sc, ALU.not_equal))
            dve.wait_ge(f3_a, 1)
            link(dve, nc.vector.tensor_tensor(se, se, src, ALU.mult))
            link(dve, nc.vector.tensor_reduce(s8[:, 1:2], se, AX.X, ALU.add))
            link(dve, nc.vector.reciprocal(s8[:, 2:3], s8[:, 1:2]))
            nc.vector.tensor_scalar(se, se, s8[:, 2:3], None, ALU.mult).then_inc(f3_d, 1)
            dve.wait_ge(f3_d, 2)
            hid(30)
            dve.wait_ge(ring_act.emptied, ring_act.nth(("wcol",)))
            for n in range(2):
                for e in range(8):
                    bank = ring_dve.take(dve, ("y", e, n))
                    for i in range(4):
                        b = 4 * n + i
                        ins = nc.vector.scalar_tensor_tensor(out=x[:, b, :], in0=bank[:, i * D:(i + 1) * D],
                                                             scalar=wcol[:, b, e:e + 1], in1=x[:, b, :],
                                                             op0=ALU.mult, op1=ALU.add)
                    ins.then_inc(ring_dve.emptied, 1)
                    dve.wait_ge(ring_dve.emptied, ring_dve.taken)

        def gpsimd_l3f(pool):
            for m, (e, n, k) in enumerate(f3_seq):
                if k:
                    pool.wait_ge(ring_act.emptied, ring_act.nth(("up", e, n, k)))
                    nc.gpsimd.tensor_tensor(hidden(e, n)[:, 4:8, :], silu_of(m), up_of(m), ALU.mult).then_inc(
                        *f3_pool.inc((e, n)))
                    pool.wait_ge(*f3_pool.at((e, n)))

        PE = dict(l0a=tensor_l0a, l0f=tensor_l0f, l1x=tensor_l1x, l1f=tensor_l1f, l2f=tensor_l2f, l3f=tensor_l3f)
        SC = dict(l0a=scalar_l0a, l0f=scalar_l0f, l1x=scalar_l1x, l1f=scalar_l1f, l2f=scalar_l2f, l3f=scalar_l3f)
        VE = dict(l0a=vector_l0a, l0f=vector_l0f, l1x=vector_l1x, l1f=vector_l1f, l2f=vector_l2f, l3f=vector_l3f)
        PO = dict(l0a=gpsimd_l0a, l0f=gpsimd_l0f, l1x=gpsimd_l1x, l1f=gpsimd_l1f, l2f=gpsimd_l2f, l3f=gpsimd_l3f)
        RUNS = [tuple(s for s in run if s in subs) for run in
                (("l0a",), ("l0x",), ("l0f",), ("l1a",), ("l1x",), ("l1f",), ("l2a", "l2x"), ("l2f",), ("l3a", "l3x"),
                 ("l3f",)) if run[0] in subs]
        block = stack.enter_context(nc.Block())

        @block.tensor
        def _(pe):
            for run in RUNS:
                PE[run[0]](pe) if run[0] in PE else tensor_attention(pe, run)

        @block.scalar
        def _(act):
            act.wait_ge(loaded["const"], 16)
            for run in RUNS:
                SC[run[0]](act) if run[0] in SC else scalar_attention(act, run)

        @block.vector
        def _(dve):
            for run in RUNS:
                VE[run[0]](dve) if run[0] in VE else vector_attention(dve, run)
            dve.drain().then_inc(x_final, 1)
            dve.wait_ge(x_final, 1)

        @block.gpsimd
        def _(pool):
            for run in RUNS:
                PO[run[0]](pool) if run[0] in PO else gpsimd_attention(pool, run)

        @block.sync
        def _(sp):
            sp.dma_start(x[:], x_dram.rearrange("b t d -> t b d")).then_inc(x_loaded, 16)
            order = ["l0a", "const", "small", "sel32"]
            order += [s for s in subs if s in groups and s not in order and s not in [later for _, later in PLACES]]
            for g in order:
                sp.dma_start(store[g], groups[g][0]).then_inc(loaded[g], 16)
                if g == "sel32":
                    for name, dst in (("ctxT", ctxT), ("ctx", ctx)):
                        sp.dma_start(dst[:], ctx_dram[name]).then_inc(ctx_loaded, 16)
            sp.dma_start(rowconst, rowconst_dram).then_inc(rowconst_loaded, 16)
            if "l3x" in subs:
                sp.wait_ge(ring_dve.emptied, ring_dve.nth(("out", "l0f", 1)))
                sp.dma_start(mask_i, mask_dram).then_inc(mask_loaded, 16)
            for first, later in PLACES:
                if later in subs:
                    sp.wait_ge(ring_dve.emptied, ring_dve.nth(("out", first, 1 if first == "l0a" else B - 1)))
                    if first == "l0a":
                        sp.wait_ge(*stats_ready.at(("l0x", 0, B - 1)))
                    sp.dma_start(store[later], groups[later][0]).then_inc(loaded[later], 16)
            out_view = out_dram.rearrange("b t d -> t b d")
            if STOP == 12:
                sp.wait_ge(ring_dve.emptied, ring_dve.nth(("y", 7, 0)))
                sp.dma_start(out_view[:, 0:HALF, :], x[:, 0:HALF, :]).then_inc(stored, 16)
            sp.wait_ge(x_final, 1)
            rest = slice(HALF if STOP == 12 else 0, B)
            sp.dma_start(out_view[:, rest, :], x[:, rest, :]).then_inc(stored, 16)
            sp.wait_ge(stored, 32 if STOP == 12 else 16)
            sp.wait_ge(rowconst_loaded, 16)


def lay_out(inputs):
    def f(name):
        return np.asarray(inputs[name])

    def chunked(a):
        return np.concatenate([a[i:i + P] for i in range(0, a.shape[0], P)], axis=1)

    def col(a):
        return a.reshape(-1, P).T

    def rep(a):
        return np.broadcast_to(a.reshape(1, -1), (P, a.size))

    def row(a):
        return a.reshape(1, -1)

    p = np.arange(P)
    c1024 = np.arange(TOK)
    h8 = np.arange(8)[:, None]
    dim = p % 32
    freq = (1.0 / 10000.0 ** (np.arange(0, 8, 2, dtype=np.float32) / 8)).astype(np.float32)
    angle = np.arange(S, dtype=np.float32)[None, :] * freq[dim % 4][:, None]
    rotated = (dim < 8)[:, None]
    const = {
        "ident": np.eye(P),
        "ones": np.ones((P, P)),
        "mask8": p[:, None] // 8 == np.arange(16),
        "mask32": p[:, None] // 32 == np.arange(4),
        "mask16": 0.25 * (p[:, None] // 16 == np.arange(8)),
        "iota8": np.broadcast_to(np.arange(8), (P, 8)),
        "sel8": 1.0 * (np.arange(256)[None, :] // 32 == h8),
        "cos": np.where(rotated, np.cos(angle), 1.0),
        "sin": np.where(rotated, np.sin(angle) * np.where(dim < 4, -1.0, 1.0)[:, None], 0.0),
        "bigparts": np.pad(BIG_PARTS, ((0, P - 3), (0, 0))),
    }
    rowconst = np.zeros((P, 3, TOK), np.float32)
    rowconst[0:8, 0] = c1024[None, :] // S == h8
    rowconst[0:8, 1] = c1024 % S != 0
    rowconst[0:8, 2] = np.where(c1024 % S == 0, NEG, 0.0)
    q, k = p[:, None], p[None, :]
    small = {
        "ident_bf": np.eye(P),
        "ones_bf": np.ones((P, P)),
        "causal_bf": np.where(k <= q, 0.0, NEG),
        "causalT_bf": np.where(q <= k, 0.0, NEG),
    }
    sel32 = {
        "sel32_bf": 1.0 * (np.arange(96)[:, None] % 32 == np.arange(2048)[None, :] // 64),
    }
    perm = np.arange(256).reshape(8, 32).copy()
    perm[:, 0:8] = perm[:, [4, 5, 6, 7, 0, 1, 2, 3]]
    perm = perm.reshape(-1)
    kperm = perm[0:64]
    wq, wk = f("L2_attn_Wq"), f("L2_attn_Wk")

    def rep4(a, kv):
        return np.concatenate([a[:, 32 * kv:32 * kv + 32]] * 4, axis=1)

    groups = {
        "l0a": {
            "l0a_win": f("L0_attn_w_in").T, "l0a_wx": chunked(f("L0_attn_w_x").T), "l0a_wout": chunked(f("L0_attn_w_out").T),
            "l0a_bin": col(f("L0_attn_b_in")[:256]),
            "l0a_wconv": f("L0_attn_w_conv")[:, 0, :].reshape(2, P, 4).transpose(1, 0, 2).reshape(P, 8),
            "l0a_bconv": col(f("L0_attn_b_conv")), "l0a_bx": col(f("L0_attn_b_x")[:256]),
            "l0a_bout": rep(f("L0_attn_b_out")),
        },
        "const": const,
        "l0x": {
            "x0_wq": f("L0_xattn_w_q"), "x0_wk": f("L0_xattn_w_kv")[:, :1024], "x0_wv": f("L0_xattn_w_kv")[:, 1024:],
            "x0_wo": chunked(f("L0_xattn_w_out")), "x0_gamma": col(f("L0_xattn_ln_gamma")),
            "x0_beta": col(f("L0_xattn_ln_beta")), "x0_bout": row(f("L0_xattn_b_out")), "x0_gate": rep(f("L0_xattn_gate")),
        },
        "l0f": {"f0_wr": f("L0_ffn_W_r").T, "f0_wk": f("L0_ffn_W_k").T, "f0_wv": f("L0_ffn_W_v").T,
                "f0_mur": col(f("L0_ffn_mu_r")), "f0_muk": col(f("L0_ffn_mu_k"))},
        "l1a": {
            "a1_wq": f("L1_attn_Q").transpose(1, 2, 0).reshape(D, 1024), "a1_wk": f("L1_attn_K").transpose(1, 2, 0).reshape(D, 1024),
            "a1_wv": f("L1_attn_V").transpose(1, 2, 0).reshape(D, 1024),
            "a1_wo": chunked(f("L1_attn_W").transpose(2, 1, 0).reshape(1024, D)),
        },
        "l1x": {
            "x1_wi": chunked(f("L1_xattn_igate_w").T), "x1_wf": chunked(f("L1_xattn_fgate_w").T),
            "x1_bi": f("L1_xattn_igate_b").reshape(8, 1), "x1_bf": f("L1_xattn_fgate_b").reshape(8, 1),
            "x1_lnscale": rep(f("L1_xattn_ln_scale")),
        },
        "l1f": {
            "f1_wv": f("L1_ffn_Wv").T, "f1_bvc": col(f("L1_ffn_bv")), "f1_bvr": row(f("L1_ffn_bv")),
            "f1_wgp": np.concatenate([f("L1_ffn_Wg").T, f("L1_ffn_Wp").reshape(64, D).T], axis=1),
            "f1_bg": rep(f("L1_ffn_bg")), "f1_gr": rep(f("L1_ffn_g_r")), "f1_br": rep(f("L1_ffn_b_r")),
            "f1_gc": rep(f("L1_ffn_g_c")), "f1_bc": rep(f("L1_ffn_b_c")), "f1_alpha": rep(f("L1_ffn_alpha")),
            "f1_w1": f("L1_ffn_W1").reshape(256, D).T, "f1_b1": col(f("L1_ffn_b1")),
            "f1_w2": chunked(f("L1_ffn_W2").transpose(0, 2, 1).reshape(256, D)), "f1_b2": f("L1_ffn_b2"),
        },
        "l2a": {
            "a2_wq4": np.concatenate([wq[:, 0:256], wq[:, 0:256][:, perm]], axis=1),
            "a2_wk4": np.concatenate([rep4(wk, 0), rep4(wk, 1), rep4(wk[:, kperm], 0), rep4(wk[:, kperm], 1)], axis=1),
            "a2_wvg": np.concatenate([f("L2_attn_Wv"), wq[:, 256:512]], axis=1), "a2_wo": chunked(f("L2_attn_Wo")),
        },
        "l2x": {
            "x2_wq": f("L2_xattn_Wq").T, "x2_wk": f("L2_xattn_Wk").T, "x2_wv": f("L2_xattn_Wv").T,
            "x2_wo": f("L2_xattn_Wo").T, "x2_bq": col(f("L2_xattn_bq")), "x2_bk": col(f("L2_xattn_bk")),
            "x2_bv": row(f("L2_xattn_bv")), "x2_bo": row(f("L2_xattn_bo")),
        },
        "l2f": {
            "f2_wr": f("L2_ffn_Wr"), "f2_br": row(f("L2_ffn_br")),
            "f2_wg": f("L2_ffn_Wg").transpose(1, 0, 2).reshape(D, 2048), "f2_wu": f("L2_ffn_Wu").transpose(1, 0, 2).reshape(D, 2048),
            "f2_wd": chunked(f("L2_ffn_Wd").reshape(2048, D)), "f2_bg": col(f("L2_ffn_bg")), "f2_bu": col(f("L2_ffn_bu")),
            "f2_bd3": np.concatenate([f("L2_ffn_bd")] * 3, axis=0), "f2_wgs": f("L2_ffn_Wg_s"), "f2_wus": f("L2_ffn_Wu_s"),
            "f2_wds": f("L2_ffn_Wd_s"), "f2_bgs": f("L2_ffn_bg_s").reshape(64, 1), "f2_bus": f("L2_ffn_bu_s").reshape(64, 1),
            "f2_bds": row(f("L2_ffn_bd_s")),
        },
        "l3a": {"a3_wq": f("L3_attn_W_attn")[:, 0:128], "a3_wk": f("L3_attn_W_attn")[:, 128:256],
                "a3_wv": f("L3_attn_W_attn")[:, 256:384], "a3_wo": f("L3_attn_W_proj")},
        "l3x": {"x3_wq": f("L3_xattn_w_q").T, "x3_wk": f("L3_xattn_w_k").T, "x3_wv": f("L3_xattn_w_v").T,
                "x3_wo": f("L3_xattn_w_o").T},
        "l3f": {
            "f3_wg": f("L3_ffn_Wg").T, "f3_w1": f("L3_ffn_W1").reshape(2048, D).T, "f3_w3": f("L3_ffn_W3").reshape(2048, D).T,
            "f3_w2": chunked(f("L3_ffn_W2").transpose(0, 2, 1).reshape(2048, D)),
        },
        "small": small, "sel32": sel32,
    }
    packed = {}
    for g, pieces in groups.items():
        width = sum(a.shape[1] for a in pieces.values())
        whole, off, names = np.zeros((P, width), np.float32), 0, {}
        for name, a in pieces.items():
            whole[0:a.shape[0], off:off + a.shape[1]] = a
            names[name] = (off, a.shape[0], a.shape[1])
            off += a.shape[1]
        packed[g] = (whole, names)
    return packed, rowconst


def kernel(**inputs):
    import concourse.bacc as bacc
    from concourse.bass_utils import run_bass_kernel_spmd

    nc = bacc.Bacc("TRN2", target_bir_lowering=False, num_devices=1)
    arrays, groups = {}, {}

    def dram(name, a):
        arrays[name] = np.ascontiguousarray(a)
        return nc.dram_tensor(name, a.shape, mybir.dt.from_np(a.dtype), kind="ExternalInput").ap()

    packed, rowconst = lay_out(inputs)
    for g, (whole, names) in packed.items():
        if g in SUBLAYERS[STOP:]:
            continue
        groups[g] = (dram(f"in_{g}", whole), names)
    x = np.asarray(inputs["x"])
    c = np.asarray(inputs["ctx_1024"])
    ctx = {"ctxT": dram("in_ctxT", c.transpose(2, 0, 1)), "ctx": dram("in_ctx", c.transpose(1, 0, 2))}
    m = np.asarray(inputs["mask_BxS2_if1"])
    mask = dram("in_mask", np.broadcast_to(m[None], (P, B, S)))
    out = nc.dram_tensor("out_x", x.shape, F32, kind="ExternalOutput").ap()
    bass_decoder_kernel(nc, groups, ctx, dram("in_x", x), mask, dram("in_rowconst", rowconst), out)
    r = run_bass_kernel_spmd(nc, [arrays], core_ids=[0])
    return r.results[0]["out_x"]
```
